# Optimizing a Trainium2 kernel written in Bass

```python
import numpy as np
import jax
import jax.numpy as jnp

def _softmax(x, axis=-1):
    return jax.nn.softmax(x, axis=axis)

def _gelu(x):
    return jax.nn.gelu(x, approximate=True)

def _silu(x):
    return jax.nn.silu(x)

def _sigmoid(x):
    return jax.nn.sigmoid(x)

def _layernorm(x, axis=-1, eps=1e-05):
    m = jnp.mean(x, axis=axis, keepdims=True)
    v = jnp.var(x, axis=axis, keepdims=True)
    return (x - m) / jnp.sqrt(v + eps)

def _scatter_add(tgt, idx, src, axis=0):
    return tgt.at[idx].add(src)

def _segment_sum(src, seg, n):
    return jax.ops.segment_sum(src, seg, n)
kernel_name = 'mk_decoder_postln_d2_seqx_r8_aace52'

def setup_inputs(seed: int=0):
    np.random.seed(seed)
    _w = jnp.asarray

    def _rec_inputs():
        import jax
        import jax.numpy as jnp
        _rk = jax.random.key(seed)
        x = 7.22e-05 + 1 * jax.random.normal(jax.random.fold_in(_rk, 1), (128, 64, 128), jnp.float32)
        _lenS = 64 - jax.random.randint(jax.random.fold_in(_rk, 7), (128,), 0, max(1, 64 // 4) + 1, jnp.int32)
        _lenS2 = 64 - jax.random.randint(jax.random.fold_in(_rk, 8), (128,), 0, max(1, 64 // 4) + 1, jnp.int32)
        _ctx_1024P = jax.random.normal(jax.random.fold_in(_rk, 11), (128, 16, 128), jnp.float32)
        _ctx_1024c = jax.random.dirichlet(jax.random.fold_in(_rk, 511), 0.3 * jnp.ones((16,), jnp.float32), (128, 64))
        _ctx_1024t = jnp.einsum('bsk,bkd->bsd', _ctx_1024c, _ctx_1024P)
        _ctx_1024t = _ctx_1024t * jax.lax.rsqrt(jnp.mean(jnp.square(_ctx_1024t)) + 1e-12) * 0.953939
        ctx_1024 = 4.13588e-05 + 0.999923 * (_ctx_1024t + 0.3 * jax.random.normal(jax.random.fold_in(_rk, 611), (128, 64, 128), jnp.float32))
        _validS = jnp.arange(64)[None, :] < _lenS[:, None]
        _validS2 = jnp.arange(64)[None, :] < _lenS2[:, None]
        _causal = jnp.tril(jnp.ones((64, 64), dtype=bool))
        mask_Bx1x1xS2_if1 = jnp.where(jnp.ones((128, 1, 1, 64), dtype=bool), 1, 0).astype(jnp.int32)
        return (x, ctx_1024, mask_Bx1x1xS2_if1)
    x, ctx_1024, mask_Bx1x1xS2_if1 = _rec_inputs()

    def _L0_attn_setup():
        import jax, jax.numpy as jnp
        import numpy as np
        from math import sqrt
        NUM_HEADS = 16
        key = jax.random.key(seed)
        ks = jax.random.split(key, 5)
        B, S, H = (2, 256, 128)
        scale = 0.02
        return {'x': jax.random.normal(ks[0], (B, S, H), dtype=jnp.float32), 'W_qkv': jax.random.normal(ks[1], (3 * H, H), dtype=jnp.float32) * scale, 'b_qkv': jax.random.normal(ks[2], (3 * H,), dtype=jnp.float32) * scale, 'W_o': jax.random.normal(ks[3], (H, H), dtype=jnp.float32) * scale, 'b_o': jax.random.normal(ks[4], (H,), dtype=jnp.float32) * scale}
    _L0_attn_all = _L0_attn_setup()
    _L0_attn_in = {k: v for k, v in _L0_attn_all.items() if k in ('W_qkv', 'b_qkv', 'W_o', 'b_o')}
    del _L0_attn_all

    def _L0_xattn_setup():
        import jax, jax.numpy as jnp
        import numpy as np
        D_MODEL = 128
        NUM_HEADS = 16
        D_K = D_MODEL // NUM_HEADS
        B, S = (4, 256)
        key = jax.random.key(seed)
        ks = jax.random.split(key, 12)
        scale = 1.0 / np.sqrt(D_MODEL)
        inp = {'q': jax.random.normal(ks[0], (B, S, D_MODEL), dtype=jnp.float32), 'k': jax.random.normal(ks[1], (B, S, D_MODEL), dtype=jnp.float32), 'v': jax.random.normal(ks[2], (B, S, D_MODEL), dtype=jnp.float32), 'mask': jnp.ones((B, 1, 1, S), dtype=jnp.int32), 'Wq': jax.random.normal(ks[3], (D_MODEL, D_MODEL), dtype=jnp.float32) * scale, 'bq': jnp.zeros((D_MODEL,), dtype=jnp.float32), 'Wk': jax.random.normal(ks[4], (D_MODEL, D_MODEL), dtype=jnp.float32) * scale, 'bk': jnp.zeros((D_MODEL,), dtype=jnp.float32), 'Wv': jax.random.normal(ks[5], (D_MODEL, D_MODEL), dtype=jnp.float32) * scale, 'bv': jnp.zeros((D_MODEL,), dtype=jnp.float32), 'Wo': jax.random.normal(ks[6], (D_MODEL, D_MODEL), dtype=jnp.float32) * scale, 'bo': jnp.zeros((D_MODEL,), dtype=jnp.float32)}
        return inp
    _L0_xattn_all = _L0_xattn_setup()
    _L0_xattn_in = {k: v for k, v in _L0_xattn_all.items() if k in ('Wq', 'bq', 'Wk', 'bk', 'Wv', 'bv', 'Wo', 'bo')}
    del _L0_xattn_all

    def _L0_ffn_setup():
        import jax, jax.numpy as jnp
        import numpy as np
        B, S, D, F, E, K = (2, 256, 128, 256, 8, 2)
        key = jax.random.key(seed)
        ks = jax.random.split(key, 5)
        scale = 0.02
        return {'x': jax.random.normal(ks[0], (B, S, D), dtype=jnp.float32), 'Wg': jax.random.normal(ks[1], (E, D), dtype=jnp.float32) * scale, 'W1': jax.random.normal(ks[2], (E, F, D), dtype=jnp.float32) * scale, 'W2': jax.random.normal(ks[3], (E, F, D), dtype=jnp.float32) * scale, 'W3': jax.random.normal(ks[4], (E, D, F), dtype=jnp.float32) * scale}
    _L0_ffn_all = _L0_ffn_setup()
    _L0_ffn_in = {k: v for k, v in _L0_ffn_all.items() if k in ('Wg', 'W1', 'W2', 'W3')}
    del _L0_ffn_all

    def _L1_attn_setup():
        import jax, jax.numpy as jnp
        import numpy as np
        EPS_RMS = 1e-06
        EPS_LN = 1e-05
        ETA_MIN = 1e-06
        B, T, D, F = (8, 64, 128, 64)

        def _rmsnorm(x, w):
            return x * jax.lax.rsqrt(jnp.mean(x * x, axis=-1, keepdims=True) + EPS_RMS) * w

        def _phi(x):
            return jax.nn.elu(x) + 1.0

        def _ln2(M):
            mu = jnp.mean(M, axis=(-2, -1), keepdims=True)
            var = jnp.mean((M - mu) ** 2, axis=(-2, -1), keepdims=True)
            return (M - mu) * jax.lax.rsqrt(var + EPS_LN)

        def _reference_tuple_inner(x, norm_weight, Wk, Wv, Wq, eta, Wout):
            b, t, d = x.shape
            f = Wk.shape[0]
            x_norm = _rmsnorm(x, norm_weight)
            k = _phi(jnp.einsum('btd,fd->btf', x_norm, Wk))
            v = jnp.einsum('btd,ed->bte', x_norm, Wv)
            eta_c = jnp.maximum(jnp.abs(eta), ETA_MIN)

            def step(M, kv):
                k_t, v_t = kv
                v_pred = jnp.einsum('bf,bfd->bd', k_t, M)
                surprise = jnp.linalg.norm(v_t - v_pred, axis=-1, keepdims=True)
                delta = k_t[:, :, None] * v_t[:, None, :]
                M = M + eta_c[None, :, None] * surprise[:, :, None] * delta
                return (_ln2(M), None)
            M0 = jnp.zeros((b, f, d), dtype=x.dtype)
            kT = jnp.transpose(k, (1, 0, 2))
            vT = jnp.transpose(v, (1, 0, 2))
            M, _ = jax.lax.scan(step, M0, (kT, vT))
            q = _phi(jnp.einsum('btd,fd->btf', x_norm, Wq))
            mem_out = jnp.einsum('btf,bfd->btd', q, M)
            out = jnp.einsum('btd,ed->bte', mem_out, Wout)
            output = x + out
            return (output, M)
        key = jax.random.key(seed)
        ks = jax.random.split(key, 5)
        x = jax.random.normal(ks[0], (B, T, D), dtype=jnp.float32)
        norm_weight = jnp.ones((D,), dtype=jnp.float32)
        Wk = jax.random.normal(ks[1], (F, D), dtype=jnp.float32) * 0.02
        Wv = jax.random.normal(ks[2], (D, D), dtype=jnp.float32) * 0.02
        Wq = jax.random.normal(ks[3], (F, D), dtype=jnp.float32) * 0.02
        Wout = jax.random.normal(ks[4], (D, D), dtype=jnp.float32) * 0.02
        eta = jnp.ones((F,), dtype=jnp.float32) * 0.01
        return {'x': x, 'norm_weight': norm_weight, 'Wk': Wk, 'Wv': Wv, 'Wq': Wq, 'eta': eta, 'Wout': Wout}
    _L1_attn_all = _L1_attn_setup()
    _L1_attn_in = {k: v for k, v in _L1_attn_all.items() if k in ('norm_weight', 'Wk', 'Wv', 'Wq', 'eta', 'Wout')}
    del _L1_attn_all

    def _L1_xattn_setup():
        import jax, jax.numpy as jnp
        import numpy as np
        E, T, H, F = (8, 128, 128, 512)
        key = jax.random.key(seed)
        k1, k2, k3 = jax.random.split(key, 3)
        x = jax.random.normal(k1, (E, T, H), dtype=jnp.float32)
        w1 = jax.random.normal(k2, (E, F, H), dtype=jnp.float32) * (1.0 / np.sqrt(H))
        w2 = jax.random.normal(k3, (E, F, H), dtype=jnp.float32) * (1.0 / np.sqrt(F))
        return {'x': x, 'w1': w1, 'w2': w2}
    _L1_xattn_all = _L1_xattn_setup()
    _L1_xattn_in = {k: v for k, v in _L1_xattn_all.items() if k in ()}
    del _L1_xattn_all

    def _L1_ffn_setup():
        import jax, jax.numpy as jnp
        import numpy as np
        H, E, DFF = (128, 8, 512)
        key = jax.random.key(seed)
        ks = jax.random.split(key, 7)
        s = lambda *shape: 1.0 / np.sqrt(shape[-2] if len(shape) > 1 else shape[-1])
        x = jax.random.normal(ks[0], (2, 256, H), dtype=jnp.float32)
        Wr = jax.random.normal(ks[1], (H, E), dtype=jnp.float32) * (1.0 / np.sqrt(H))
        br = jnp.zeros((E,), dtype=jnp.float32)
        W1 = jax.random.normal(ks[2], (E, H, DFF), dtype=jnp.float32) * (1.0 / np.sqrt(H))
        b1 = jnp.zeros((E, DFF), dtype=jnp.float32)
        W2 = jax.random.normal(ks[3], (E, DFF, H), dtype=jnp.float32) * (1.0 / np.sqrt(DFF))
        b2 = jnp.zeros((E, H), dtype=jnp.float32)
        return {'x': x, 'Wr': Wr, 'br': br, 'W1': W1, 'b1': b1, 'W2': W2, 'b2': b2}
    _L1_ffn_all = _L1_ffn_setup()
    _L1_ffn_in = {k: v for k, v in _L1_ffn_all.items() if k in ('Wr', 'br', 'W1', 'b1', 'W2', 'b2')}
    del _L1_ffn_all
    return {'x': x, 'ctx_1024': ctx_1024, 'mask_Bx1x1xS2_if1': mask_Bx1x1xS2_if1, 'L0_attn_W_qkv': _L0_attn_in['W_qkv'], 'L0_attn_b_qkv': _L0_attn_in['b_qkv'], 'L0_attn_W_o': _L0_attn_in['W_o'], 'L0_attn_b_o': _L0_attn_in['b_o'], 'L0_xattn_Wq': _L0_xattn_in['Wq'], 'L0_xattn_bq': _L0_xattn_in['bq'], 'L0_xattn_Wk': _L0_xattn_in['Wk'], 'L0_xattn_bk': _L0_xattn_in['bk'], 'L0_xattn_Wv': _L0_xattn_in['Wv'], 'L0_xattn_bv': _L0_xattn_in['bv'], 'L0_xattn_Wo': _L0_xattn_in['Wo'], 'L0_xattn_bo': _L0_xattn_in['bo'], 'L0_ffn_Wg': _L0_ffn_in['Wg'], 'L0_ffn_W1': _L0_ffn_in['W1'], 'L0_ffn_W2': _L0_ffn_in['W2'], 'L0_ffn_W3': _L0_ffn_in['W3'], 'L1_attn_norm_weight': _L1_attn_in['norm_weight'], 'L1_attn_Wk': _L1_attn_in['Wk'], 'L1_attn_Wv': _L1_attn_in['Wv'], 'L1_attn_Wq': _L1_attn_in['Wq'], 'L1_attn_eta': _L1_attn_in['eta'], 'L1_attn_Wout': _L1_attn_in['Wout'], 'L1_ffn_Wr': _L1_ffn_in['Wr'], 'L1_ffn_br': _L1_ffn_in['br'], 'L1_ffn_W1': _L1_ffn_in['W1'], 'L1_ffn_b1': _L1_ffn_in['b1'], 'L1_ffn_W2': _L1_ffn_in['W2'], 'L1_ffn_b2': _L1_ffn_in['b2']}

def reference(x, ctx_1024, mask_Bx1x1xS2_if1, L0_attn_W_qkv, L0_attn_b_qkv, L0_attn_W_o, L0_attn_b_o, L0_xattn_Wq, L0_xattn_bq, L0_xattn_Wk, L0_xattn_bk, L0_xattn_Wv, L0_xattn_bv, L0_xattn_Wo, L0_xattn_bo, L0_ffn_Wg, L0_ffn_W1, L0_ffn_W2, L0_ffn_W3, L1_attn_norm_weight, L1_attn_Wk, L1_attn_Wv, L1_attn_Wq, L1_attn_eta, L1_attn_Wout, L1_ffn_Wr, L1_ffn_br, L1_ffn_W1, L1_ffn_b1, L1_ffn_W2, L1_ffn_b2):
    import jax
    import jax.numpy as jnp

    def _L0_attn_ref(x, W_qkv, b_qkv, W_o, b_o):
        import jax, jax.numpy as jnp
        import numpy as np
        from math import sqrt
        NUM_HEADS = 16
        B, S, H = x.shape
        nh = NUM_HEADS
        hd = H // nh
        qkv = x @ W_qkv.T + b_qkv
        Q, K, V = (qkv[..., :H], qkv[..., H:2 * H], qkv[..., 2 * H:])
        Q = Q.reshape(B, S, nh, hd)
        K = K.reshape(B, S, nh, hd)
        V = V.reshape(B, S, nh, hd)
        scores = jnp.einsum('bqhd,bkhd->bhqk', Q, K)
        causal = jnp.tril(jnp.ones((S, S), dtype=bool))
        scores = jnp.where(causal, scores, -jnp.inf)
        probs = jax.nn.softmax(scores / sqrt(hd), axis=-1)
        out = jnp.einsum('bkhd,bhqk->bqhd', V, probs)
        out = out.reshape(B, S, H)
        return out @ W_o.T + b_o

    def _L0_xattn_ref(q, k, v, mask, Wq, bq, Wk, bk, Wv, bv, Wo, bo):
        import jax, jax.numpy as jnp
        import numpy as np
        D_MODEL = 128
        NUM_HEADS = 16
        D_K = D_MODEL // NUM_HEADS
        B, S = (4, 256)
        b, s, d = q.shape
        query = (q @ Wq + bq).reshape(b, s, NUM_HEADS, D_K).transpose(0, 2, 1, 3)
        key_ = (k @ Wk + bk).reshape(b, s, NUM_HEADS, D_K).transpose(0, 2, 1, 3)
        value = (v @ Wv + bv).reshape(b, s, NUM_HEADS, D_K).transpose(0, 2, 1, 3)
        scores = jnp.einsum('bhqd,bhkd->bhqk', query, key_) / jnp.sqrt(jnp.float32(D_K))
        scores = jnp.where(mask == 0, jnp.float32(-jnp.inf), scores)
        attn = jax.nn.softmax(scores, axis=-1)
        out = jnp.einsum('bhqk,bhkd->bhqd', attn, value)
        out = out.transpose(0, 2, 1, 3).reshape(b, s, NUM_HEADS * D_K)
        return out @ Wo + bo

    def _L0_ffn_ref(x, Wg, W1, W2, W3):
        import jax, jax.numpy as jnp
        import numpy as np
        B, S, D, F, E, K = (2, 256, 128, 256, 8, 2)
        k = K
        scores = jnp.einsum('bsd,ed->bse', x, Wg)
        topk_scores, topk_idx = jax.lax.top_k(scores, k)
        topk_probs = jax.nn.softmax(topk_scores, axis=-1)
        h1 = jnp.einsum('bsd,efd->bsef', x, W1)
        h2 = jnp.einsum('bsd,efd->bsef', x, W2)
        hidden = jax.nn.silu(h1) * h2
        expert_out = jnp.einsum('bsef,edf->bsed', hidden, W3)
        onehot = jax.nn.one_hot(topk_idx, scores.shape[-1], dtype=x.dtype)
        gating = jnp.einsum('bsk,bske->bse', topk_probs, onehot)
        return jnp.einsum('bse,bsed->bsd', gating, expert_out)

    def _L1_attn_ref(x, norm_weight, Wk, Wv, Wq, eta, Wout):
        import jax, jax.numpy as jnp
        import numpy as np
        EPS_RMS = 1e-06
        EPS_LN = 1e-05
        ETA_MIN = 1e-06
        B, T, D, F = (8, 64, 128, 64)

        def _rmsnorm(x, w):
            return x * jax.lax.rsqrt(jnp.mean(x * x, axis=-1, keepdims=True) + EPS_RMS) * w

        def _phi(x):
            return jax.nn.elu(x) + 1.0

        def _ln2(M):
            mu = jnp.mean(M, axis=(-2, -1), keepdims=True)
            var = jnp.mean((M - mu) ** 2, axis=(-2, -1), keepdims=True)
            return (M - mu) * jax.lax.rsqrt(var + EPS_LN)

        def _reference_tuple_inner(x, norm_weight, Wk, Wv, Wq, eta, Wout):
            b, t, d = x.shape
            f = Wk.shape[0]
            x_norm = _rmsnorm(x, norm_weight)
            k = _phi(jnp.einsum('btd,fd->btf', x_norm, Wk))
            v = jnp.einsum('btd,ed->bte', x_norm, Wv)
            eta_c = jnp.maximum(jnp.abs(eta), ETA_MIN)

            def step(M, kv):
                k_t, v_t = kv
                v_pred = jnp.einsum('bf,bfd->bd', k_t, M)
                surprise = jnp.linalg.norm(v_t - v_pred, axis=-1, keepdims=True)
                delta = k_t[:, :, None] * v_t[:, None, :]
                M = M + eta_c[None, :, None] * surprise[:, :, None] * delta
                return (_ln2(M), None)
            M0 = jnp.zeros((b, f, d), dtype=x.dtype)
            kT = jnp.transpose(k, (1, 0, 2))
            vT = jnp.transpose(v, (1, 0, 2))
            M, _ = jax.lax.scan(step, M0, (kT, vT))
            q = _phi(jnp.einsum('btd,fd->btf', x_norm, Wq))
            mem_out = jnp.einsum('btf,bfd->btd', q, M)
            out = jnp.einsum('btd,ed->bte', mem_out, Wout)
            output = x + out
            return (output, M)
        return _reference_tuple_inner(x, norm_weight, Wk, Wv, Wq, eta, Wout)[0]

    def _L1_xattn_ref(x, w1, w2):
        import jax, jax.numpy as jnp
        import numpy as np
        E, T, H, F = (8, 128, 128, 512)
        h = jnp.einsum('eth,efh->etf', x, w1)
        g = jax.nn.gelu(h, approximate=True)
        out = jnp.einsum('etf,efh->eth', g, w2)
        return out

    def _L1_ffn_ref(x, Wr, br, W1, b1, W2, b2):
        import jax, jax.numpy as jnp
        import numpy as np
        H, E, DFF = (128, 8, 512)
        B, S, Hd = x.shape
        n_exp = W1.shape[0]
        xt = x.reshape(-1, Hd)
        logits = xt @ Wr + br
        probs = jax.nn.softmax(logits, axis=-1)
        gate = jnp.max(probs, axis=-1)
        idx = jnp.argmax(probs, axis=-1)
        h1 = jnp.maximum(jnp.einsum('th,ehf->etf', xt, W1) + b1[:, None, :], 0.0)
        ye = jnp.einsum('etf,efh->eth', h1, W2) + b2[:, None, :]
        onehot = jax.nn.one_hot(idx, n_exp, dtype=xt.dtype)
        y = jnp.einsum('te,eth->th', onehot, ye) * gate[:, None]
        return y.reshape(B, S, Hd)
    x = _layernorm(x + _L0_attn_ref(x, L0_attn_W_qkv, L0_attn_b_qkv, L0_attn_W_o, L0_attn_b_o), axis=-1)
    x = _layernorm(x + _L0_xattn_ref(x, ctx_1024, ctx_1024, mask_Bx1x1xS2_if1, L0_xattn_Wq, L0_xattn_bq, L0_xattn_Wk, L0_xattn_bk, L0_xattn_Wv, L0_xattn_bv, L0_xattn_Wo, L0_xattn_bo), axis=-1)
    x = _layernorm(x + _L0_ffn_ref(x, L0_ffn_Wg, L0_ffn_W1, L0_ffn_W2, L0_ffn_W3), axis=-1)
    x = _layernorm(x + _L1_attn_ref(x, L1_attn_norm_weight, L1_attn_Wk, L1_attn_Wv, L1_attn_Wq, L1_attn_eta, L1_attn_Wout), axis=-1)
    x = _layernorm(x + _L1_xattn_ref(x, ctx_1024, ctx_1024), axis=-1)
    x = _layernorm(x + _L1_ffn_ref(x, L1_ffn_Wr, L1_ffn_br, L1_ffn_W1, L1_ffn_b1, L1_ffn_W2, L1_ffn_b2), axis=-1)
    return x

_drawn_inputs = setup_inputs


def setup_inputs(seed=0):
    import zlib

    import numpy as np

    out = dict(_drawn_inputs(seed))
    spreads = {'L0_xattn_bq': (0.0, 0.1),
     'L0_xattn_bk': (0.0, 0.8),
     'L0_xattn_bv': (0.0, 0.1),
     'L0_xattn_bo': (0.0, 0.1),
     'L1_attn_norm_weight': (1.0, 0.2),
     'L1_attn_eta': (0.009999999776482582, 0.6),
     'L1_ffn_br': (0.0, 0.1),
     'L1_ffn_b1': (0.0, 0.308),
     'L1_ffn_b2': (0.0, 0.1)}
    factors = {'L0_attn_W_qkv': 3.597,
     'L0_attn_b_qkv': 4.979,
     'L0_attn_W_o': 3.26,
     'L0_ffn_Wg': 5.628,
     'L0_ffn_W1': 4.841,
     'L0_ffn_W2': 4.628,
     'L0_ffn_W3': 5.499,
     'L1_attn_Wq': 5.23}
    for name, (base, spread) in spreads.items():
        noise = np.random.default_rng([zlib.crc32(name.encode()), seed]).standard_normal(out[name].shape)
        drawn = base * np.exp(spread * noise) if base else spread * noise
        out[name] = jnp.asarray(drawn.astype(out[name].dtype))
    for name, factor in factors.items():
        out[name] = (out[name] * factor).astype(out[name].dtype)
    return out
```

```python
from contextlib import ExitStack

import concourse.bass as bass
from concourse import mybir

F32 = mybir.dt.float32
BF16 = mybir.dt.bfloat16
I32 = mybir.dt.int32
ALU = mybir.AluOpType
ACT = mybir.ActivationFunctionType
AX = mybir.AxisListType.X

P = 128
B, S, D = 128, 64, 128
NT = B * S // P
NH, HD = 16, 8
UNROLL = 4
NEG = -1.0e30
LN_EPS = 1e-5


class Tile:
    BODY, ALL = UNROLL, NT

    def __init__(self, j, c):
        self.j, self.c = j, c

    def __add__(self, k):
        return type(self)(self.j, self.c + k)

    def count(self, per=1, less=0):
        k = (self.c + 1 - less) * per
        return k if self.static else self.j * (self.BODY * per) + k

    @property
    def static(self):
        return isinstance(self.j, int)

    @property
    def n(self):
        return self.c if self.static else self.j * self.BODY + self.c

    def slot(self, n):
        return self.c % n

    def uses(self, n):
        k = self.c // n + 1
        return k if self.static else self.j * (self.BODY // n) + k

    def exists(self):
        return not self.static or 0 <= self.c < self.ALL

    def after(self, k):
        return not self.static or self.c >= k


class Group(Tile):
    BODY, ALL = 2, NT // 4


def skewed(eng, step, before, after, kind=Tile):
    first = 4 // kind.BODY
    for c in range(-before, first * kind.BODY):
        step(kind(0, c))
    last = kind.ALL // kind.BODY - -(-before // kind.BODY)
    with eng.Fori(first, last) as j:
        for c in range(kind.BODY):
            step(kind(j, c))
    for c in range(last * kind.BODY, kind.ALL + after):
        step(kind(0, c))


class Maker:

    def __init__(self, nc, ctx, stage):
        self.nc, self.ctx, self.stage = nc, ctx, stage
        self.sems = []

    def sb(self, name, shape, dt=F32):
        return self.ctx.enter_context(self.nc.sbuf_tensor(f"{self.stage}_{name}", shape, dt))

    def ps(self, name, shape, dt=F32):
        return self.ctx.enter_context(self.nc.psum_tensor(f"{self.stage}_{name}_ps", shape, dt))

    def sem(self, name):
        self.sems.append(self.ctx.enter_context(self.nc.semaphore(f"{self.stage}_{name}")))
        return self.sems[-1]

    def block(self):
        self.ctx.callback(self.zero)
        return self.ctx.enter_context(self.nc.Block())

    def zero(self):
        with self.nc.Block() as block:

            @block.sync
            def _(sp):
                for s in self.sems:
                    sp.sem_clear(s)


def settle(eng, passed):
    eng.sem_inc(passed, 1)


def constants(nc, mk):
    k = {
        "ident": mk.sb("ident", [P, P]),
        "ident_bf": mk.sb("ident_bf", [P, P], BF16),
        "head_mask": mk.sb("head_mask", [P, 8]),
        "head_mask2": mk.sb("head_mask2", [P, 2, 8]),
        "causal": mk.sb("causal", [P, 8, S], BF16),
        "pick": mk.sb("pick", [2, 2, S], BF16),
        "ones": mk.sb("ones", [1, P]),
        "half": mk.sb("half", [P, 4]),
    }
    cleared, stamped, drawn = mk.sem("cleared"), mk.sem("stamped"), mk.sem("drawn")
    with nc.Block() as block:

        @block.gpsimd
        def _(pool):
            for n, v in (("ident", 0.0), ("ident_bf", 0.0), ("pick", 0.0), ("causal", 0.0),
                         ("head_mask2", 1.0), ("ones", 1.0), ("half", -0.5)):
                pool.memset(k[n][tuple(slice(None) for _ in k[n].shape)], v).then_inc(cleared, 1)
            pool.wait_ge(cleared, 7)
            for m in (k["ident"], k["ident_bf"]):
                pool.affine_select(out=m[:, :], in_=m[:, :], compare_op=ALU.not_equal, fill=1.0,
                                   base=0, pattern=[[-1, P]], channel_multiplier=1).then_inc(stamped, 1)
            pool.affine_select(out=k["pick"][:, :, :], in_=k["pick"][:, :, :], compare_op=ALU.not_equal,
                               fill=1.0, base=0, pattern=[[-1, 2], [0, S]], channel_multiplier=1)\
                .then_inc(stamped, 1)
            for b in range(2):
                rows = k["causal"][b * S:(b + 1) * S, :, :]
                pool.wait_ge(stamped, 3 + b)
                pool.affine_select(out=rows, in_=rows, compare_op=ALU.is_ge, fill=NEG, base=0,
                                   pattern=[[0, 8], [-1, S]], channel_multiplier=1).then_inc(stamped, 1)
            m = k["head_mask2"][:, :, :]
            pool.wait_ge(stamped, 5)
            pool.affine_select(out=m, in_=m, compare_op=ALU.is_ge, fill=0.0, base=0,
                               pattern=[[-S, 2], [-HD, 8]], channel_multiplier=1).then_inc(stamped, 1)
            pool.wait_ge(stamped, 6)
            pool.affine_select(out=m, in_=m, compare_op=ALU.is_ge, fill=0.0, base=HD - 1,
                               pattern=[[S, 2], [HD, 8]], channel_multiplier=-1).then_inc(stamped, 1)
            pool.wait_ge(stamped, 7)
            pool.tensor_tensor(k["head_mask"][:, :], k["head_mask2"][:, 0, :], k["head_mask2"][:, 1, :],
                               ALU.add).then_inc(drawn, 1)
    return k


def attention(nc, stage, k, x_in, ctx_in, mask_in, w, x_out):
    cross = ctx_in is not None
    scale = float(HD) ** -0.5
    with ExitStack() as ctx:
        mk = Maker(nc, ctx, stage)
        sb, ps, sem = mk.sb, mk.ps, mk.sem
        w_raw = sb("w_raw", [P, 4, P])
        w_t = sb("w_t", [P, 4, P])
        b_rows = sb("b_rows", [1, 3, P])
        bv_col = sb("bv_col", [P, 1])
        bo_all = sb("bo_all", [P, P])
        x = sb("x", [P, 2, P])
        c = sb("c", [P, 2, P])
        xr = sb("xr", [P, 2, P])
        xt = sb("xt", [P, 2, P])
        ct = sb("ct", [P, 2, P])
        q_bd = sb("q_bd", [P, 2, 2, 2, S])
        kt = sb("kt", [P, 2, 2, S])
        k_ex = sb("k_ex", [P, 2, 2, 8, S])
        v_bd = sb("v_bd", [P, 4, 8, 2, 18])
        prob = sb("prob", [P, 2, NH, S])
        prob_t = sb("prob_t", [P, 8, P])
        top = sb("top", [P, 2, NH])
        rden = sb("rden", [P, 8, 2])
        o = sb("o", [P, 8, 2, HD])
        ot = sb("ot", [P, P])
        r = sb("r", [P, 2, P])
        stats = sb("stats", [P, 6])
        mv = sb("mv", [P, 2, 2])
        ve = sb("ve", [P, 2, 1])
        rstd = sb("rstd", [P, 2, 1])
        y = sb("y", [P, 2, P])
        mask_i = sb("mask_i", [2, NT, S], I32)
        mask_n = sb("mask_n", [2, NT, S], BF16)

        s_ps = [ps(f"s_ps{i}", [P, NH, S]) for i in range(2)]
        pt_ps = [ps(f"pt_ps{i}", [P, 4, P]) for i in range(2)]
        front = ps("front", [P, 512])
        back = ps("back", [P, 512])
        fq = front[:, 0:128]
        fk = front[:, 128:256]
        fv = front[:, 256:384].rearrange("p (b n) -> p b n", b=2)
        pv = back[:, 0:288].rearrange("p (a b n) -> p a b n", a=8, b=2)
        b_xt, b_ct, b_ot, b_y = (back[:, n * P:(n + 1) * P] for n in (0, 1, 2, 3))

        weights_in, w_psum, w_ready, bo_psum = sem("weights_in"), sem("w_psum"), sem("w_ready"), sem("bo_psum")
        zeroed, ones_set, mask_ready = sem("zeroed"), sem("ones_set"), sem("mask_ready")
        x_in_sem = [sem(f"x_loaded{i}") for i in range(2)]
        c_in_sem = [sem(f"ctx_loaded{i}") for i in range(2)]
        xr_in_sem = [sem(f"residual_loaded{i}") for i in range(2)]
        stored = [sem(f"stored{i}") for i in range(2)]
        xt_ready, xt_copied = sem("xt_ready"), sem("xt_copied")
        qkv_ready, q_copied, k_copied, v_copied = sem("qkv_ready"), sem("q_copied"), sem("k_copied"), sem("v_copied")
        keys_expanded, s_ready, top_ready, shifted = sem("keys_expanded"), sem("s_ready"), sem("top_ready"), sem("shifted")
        probs_ready, pt_ready, pt_copied, pv_ready = sem("probs_ready"), sem("pt_ready"), sem("pt_copied"), sem("pv_ready")
        inverse_ready, o_ready, ot_ready, ot_copied = sem("inverse_ready"), sem("o_ready"), sem("ot_ready"), sem("ot_copied")
        y_ready, residual_biased, summed, stats_ready = sem("y_ready"), sem("residual_biased"), sem("summed"), sem("stats_ready")
        mean_ready, var_ready, rstd_ready, y_normed = sem("mean_ready"), sem("var_ready"), sem("rstd_ready"), sem("y_normed")

        passed_dve = sem("passed_dve")

        names = ("q", "k", "v", "o")
        x_v = x_in.rearrange("(n p) d -> n p d", p=P)
        c_v = ctx_in.rearrange("(n p) d -> n p d", p=P) if cross else None
        out_v = x_out.rearrange("(n p) d -> n p d", p=P)
        n_weight_dmas = 8

        block = mk.block()

        @block.sync
        def _(sp):
            for n, name in enumerate(names):
                dst = w_t if cross else w_raw
                sp.dma_start(dst[:, n, :], w["w" + name]).then_inc(weights_in, 16)
            for n, name in enumerate(("q", "k", "o")):
                sp.dma_start(b_rows[:, n, :], w["b" + name].rearrange("(a n) -> a n", a=1)).then_inc(weights_in, 16)
            sp.dma_start(bv_col[:, :], w["bv"].rearrange("(n a) -> n a", a=1)).then_inc(weights_in, 16)
            if cross:
                sp.dma_start(mask_i[:, :, :], mask_in.rearrange("(i b) s -> b i s", b=2)).then_inc(mask_ready, 16)

            def step(i):
                t = i + 1
                if t.exists():
                    if t.after(2):
                        sp.wait_ge(summed, t.count(less=2))
                    sp.dma_start(xr[:, t.slot(2), :], x_v[t.n]).then_inc(xr_in_sem[t.slot(2)], 16)
                t = i + -2
                if t.exists():
                    sp.wait_ge(y_normed, t.count())
                    sp.dma_start(out_v[t.n], y[:, t.slot(2), :]).then_inc(stored[t.slot(2)], 16)
                t = i + 6
                if t.exists():
                    if t.after(2):
                        sp.wait_ge(xt_ready, t.count(less=2))
                    sp.dma_start(x[:, t.slot(2), :], x_v[t.n]).then_inc(x_in_sem[t.slot(2)], 16)
                    if cross:
                        sp.dma_start(c[:, t.slot(2), :], c_v[t.n]).then_inc(c_in_sem[t.slot(2)], 16)
            skewed(sp, step, 6, 2)
            for n in range(2):
                sp.wait_ge(stored[n], 16 * NT // 2)

        @block.gpsimd
        def _(pool):
            def step(i):
                t = i + 3
                if t.exists():
                    pool.wait_ge(k_copied, t.count())
                    if t.after(2):
                        pool.wait_ge(s_ready, t.count(less=2))
                    for h in range(2):
                        ex = pool.tensor_tensor(
                            k_ex[:, t.slot(2), h, :, :],
                            kt[:, t.slot(2), h:h + 1, :].to_broadcast([P, 8, S]),
                            k["head_mask"][:, :].unsqueeze(2).to_broadcast([P, 8, S]), ALU.mult)
                    ex.then_inc(keys_expanded, 1)
                t = i
                if t.exists():
                    pool.wait_ge(xr_in_sem[t.slot(2)], t.uses(2) * 16)
                    pool.tensor_tensor(xr[:, t.slot(2), :], xr[:, t.slot(2), :], bo_all[:, :], ALU.add)\
                        .then_inc(residual_biased, 1)
                t = i + -1
                if t.exists():
                    pool.wait_ge(var_ready, t.count())
                    if t.after(2):
                        pool.wait_ge(y_normed, t.count(less=2))
                    pool.tensor_tensor(rstd[:, t.slot(2), :], ve[:, t.slot(2), :], k["half"][:, 0:1], ALU.pow)\
                        .then_inc(rstd_ready, 1)
            pool.wait_ge(w_ready, 2)
            skewed(pool, step, 4, 2)

        @block.tensor
        def _(pe):
            pe.wait_ge(weights_in, 16 * n_weight_dmas)
            if not cross:
                for n in range(4):
                    wt = nc.tensor.transpose(front[:, n * P:(n + 1) * P], w_raw[:, n, :], k["ident"][:, :])
                wt.then_inc(w_psum, 1)
            nc.tensor.matmul(back[:, 0:P], k["ones"][:, :], b_rows[:, 2, :], start=True, stop=True).then_inc(bo_psum, 1)
            pe.wait_ge(w_ready, 2)

            def step(i):
                t = i
                if t.exists():
                    pe.wait_ge(probs_ready, t.count())
                    for h in range(2):
                        if t.after(1):
                            pe.wait_ge(pt_copied, t.count(2, less=1))
                        for n in range(4):
                            a = 2 * (4 * h + n)
                            tr = nc.tensor.transpose(pt_ps[h][:, n, :], prob[:, t.slot(2), a:a + 2, :], k["ident"][:, :])
                        tr.then_inc(pt_ready, 1)
                t = i + -1
                if t.exists():
                    pe.wait_ge(ot_copied, t.count())
                    pe.wait_ge(xt_copied, t.count() + 4 if t.static and t.c + 4 < NT or not t.static else NT)
                    nc.tensor.matmul(b_y, ot[:, :], w_t[:, 3, :], start=True, stop=True).then_inc(y_ready, 1)
                t = i + 2
                if t.exists():
                    pe.wait_ge(keys_expanded, t.count())
                    pe.wait_ge(q_copied, t.count())
                    if t.after(2):
                        pe.wait_ge(shifted, t.count(less=2))
                    if cross:
                        pe.wait_ge(mask_ready, 17)
                    for h in range(2):
                        dst = s_ps[t.slot(2)][:, 8 * h:8 * h + 8, :]
                        nc.tensor.matmul(dst, q_bd[:, t.slot(2), h, :, :], k_ex[:, t.slot(2), h, :, :], start=True, stop=False)
                        if cross:
                            mm = nc.tensor.matmul(dst, k["pick"][:, :, :], mask_n[:, bass.ds(t.n, 1), :].to_broadcast([2, 8, S]),
                                                  start=False, stop=True)
                        else:
                            mm = nc.tensor.matmul(dst, k["ident_bf"][:, :], k["causal"][:, :, :], start=False, stop=True)
                    mm.then_inc(s_ready, 1)
                t = i
                if t.exists():
                    pe.wait_ge(pt_copied, t.count(2))
                    if t.after(1):
                        pe.wait_ge(summed, t.count(less=1))
                    for n in range(8):
                        mm = nc.tensor.matmul(pv[:, n, :, :], prob_t[:, n, :], v_bd[:, t.slot(4), n, :, :], start=True, stop=True)
                    mm.then_inc(pv_ready, 1)
                t = i + 3
                if t.exists():
                    pe.wait_ge(xt_copied, t.count())
                    if t.after(1):
                        pe.wait_ge(q_copied, t.count(less=1))
                        pe.wait_ge(v_copied, t.count(less=1))
                    xq = xt[:, t.slot(2), :]
                    xk = ct[:, t.slot(2), :] if cross else xq
                    for n, (src, dst) in enumerate(((xq, fq), (xk, fk))):
                        for h in range(2):
                            for b in range(2):
                                part = dst[b * S:(b + 1) * S, h * S:(h + 1) * S]
                                nc.tensor.matmul(part, w_t[:, n, h * S:(h + 1) * S], src[:, b * S:(b + 1) * S], start=True, stop=False)
                                nc.tensor.matmul(part, b_rows[:, n, h * S:(h + 1) * S], k["ones"][:, 0:S], start=False, stop=True)
                    wv = w_t[:, 2, :].rearrange("p (a h d) -> p a h d", h=2, d=HD)
                    for b in range(2):
                        for h in range(2):
                            mm = nc.tensor.matmul(fv[h * S:(h + 1) * S, b, :], xk[:, b * S:(b + 1) * S], wv[:, :, h, :], start=True, stop=True)
                    mm.then_inc(qkv_ready, 1)
                t = i
                if t.exists():
                    pe.wait_ge(o_ready, t.count())
                    nc.tensor.transpose(b_ot, o[:, :, :, :], k["ident"][:, :]).then_inc(ot_ready, 1)
                t = i + 4
                if t.exists():
                    pe.wait_ge(x_in_sem[t.slot(2)], t.uses(2) * 16)
                    if t.after(1) and not i.exists():
                        pe.wait_ge(xt_copied, t.count(less=1))
                    tr = nc.tensor.transpose(b_xt, x[:, t.slot(2), :], k["ident"][:, :])
                    if cross:
                        pe.wait_ge(c_in_sem[t.slot(2)], t.uses(2) * 16)
                        tr = nc.tensor.transpose(b_ct, c[:, t.slot(2), :], k["ident"][:, :])
                    tr.then_inc(xt_ready, 1)
            skewed(pe, step, 4, 1)

        @block.scalar
        def _(act):
            act.wait_ge(bo_psum, 1)
            if not cross:
                act.wait_ge(w_psum, 1)
                act.copy(w_t[:, :, :], front[:, :].rearrange("p (a n) -> p a n", a=4)).then_inc(w_ready, 1)
            else:
                act.copy(bo_all[:, 0:1], back[:, 0:1]).then_inc(w_ready, 1)
            act.wait_ge(w_ready, 1)
            act.copy(bo_all[:, :], back[:, 0:P]).then_inc(w_ready, 1)
            act.wait_ge(zeroed, 3)
            act.wait_ge(w_ready, 2)

            def step(i):
                t = i
                if t.exists():
                    for h in range(2):
                        act.wait_ge(pt_ready, t.count(2) - 1 + h)
                        if t.after(1):
                            act.wait_ge(pv_ready, t.count(less=1))
                        act.copy(prob_t[:, 4 * h:4 * h + 4, :], pt_ps[h][:, :, :]).then_inc(pt_copied, 1)
                t = i + 1
                if t.exists():
                    act.wait_ge(shifted, t.count())
                    act.activation(prob[:, t.slot(2), :, :], prob[:, t.slot(2), :, :], ACT.Exp, scale=scale)\
                        .then_inc(probs_ready, 1)
                t = i + 3
                if t.exists():
                    act.wait_ge(qkv_ready, t.count())
                    if t.after(2):
                        act.wait_ge(keys_expanded, t.count(less=2))
                    act.copy(kt[:, t.slot(2), :, :], fk.rearrange("p (h n) -> p h n", h=2)).then_inc(k_copied, 1)
                    if t.after(2):
                        act.wait_ge(s_ready, t.count(less=2))
                    for b in range(2):
                        rows = slice(b * S, (b + 1) * S)
                        cp = act.copy(q_bd[rows, t.slot(2), :, b, :], fq[rows, :].rearrange("p (h n) -> p h n", h=2))
                    cp.then_inc(q_copied, 1)
                    if t.after(4):
                        act.wait_ge(pv_ready, t.count(less=4))
                    for h in range(2):
                        rows = slice(h * S, (h + 1) * S)
                        cp = act.copy(v_bd[rows, t.slot(4), :, :, HD * h:HD * h + HD].rearrange("p a b d -> p b a d"),
                                      fv[rows, :, :].rearrange("p b (a d) -> p b a d", d=HD))
                    cp.then_inc(v_copied, 1)
                t = i
                if t.exists():
                    act.wait_ge(ot_ready, t.count())
                    if (i + 4).exists():
                        act.wait_ge(xt_ready, (i + 4).count())
                    if t.after(1):
                        act.wait_ge(y_ready, t.count(less=1))
                    act.activation(ot[:, :], b_ot, ACT.Identity, bias=bv_col[:, 0:1]).then_inc(ot_copied, 1)
                t = i + 4
                if t.exists():
                    act.wait_ge(xt_ready, t.count())
                    if t.after(2):
                        act.wait_ge(qkv_ready, t.count(less=2))
                    cp = act.copy(xt[:, t.slot(2), :], b_xt)
                    if cross:
                        cp = act.copy(ct[:, t.slot(2), :], b_ct)
                    cp.then_inc(xt_copied, 1)
            skewed(act, step, 4, 1)

        @block.vector
        def _(dve):
            dve.memset(q_bd[:, :, :, :, :], 0.0).then_inc(zeroed, 1)
            dve.memset(v_bd[:, :, :, :, :], 0.0).then_inc(zeroed, 1)
            dve.wait_ge(zeroed, 2)
            for h in range(2):
                one = dve.memset(v_bd[h * S:(h + 1) * S, :, :, :, 16 + h:17 + h], 1.0)
            one.then_inc(zeroed, 1)
            if cross:
                dve.wait_ge(mask_ready, 16)
                dve.tensor_scalar(mask_n[:, :, :], mask_i[:, :, :], 0.0, NEG, ALU.is_equal, ALU.mult).then_inc(mask_ready, 1)

            def step(i):
                t = i + -1
                if t.exists():
                    dve.wait_ge(y_ready, t.count())
                    dve.wait_ge(residual_biased, t.count())
                    if t.after(2):
                        dve.wait_ge(y_normed, t.count(less=2))
                    dve.tensor_tensor(r[:, t.slot(2), :], b_y, xr[:, t.slot(2), :], ALU.add).then_inc(summed, 1)
                    dve.wait_ge(summed, t.count())
                    dve.bn_stats(stats[:, :], r[:, t.slot(2), :]).then_inc(stats_ready, 1)
                    dve.wait_ge(stats_ready, t.count())
                    settle(dve, passed_dve)
                    dve.bn_aggr(mv[:, t.slot(2), :], stats[:, :]).then_inc(mean_ready, 1)
                    dve.wait_ge(mean_ready, t.count())
                    if t.after(2):
                        dve.wait_ge(rstd_ready, t.count(less=2))
                    dve.tensor_scalar(ve[:, t.slot(2), :], mv[:, t.slot(2), 1:2], LN_EPS, None, ALU.add).then_inc(var_ready, 1)
                t = i + 2
                if t.exists():
                    dve.wait_ge(s_ready, t.count())
                    if t.after(2):
                        dve.wait_ge(shifted, t.count(less=2))
                    dve.tensor_reduce(top[:, t.slot(2), :], s_ps[t.slot(2)][:, :, :], AX, ALU.max).then_inc(top_ready, 1)
                    dve.wait_ge(top_ready, t.count())
                    if t.after(2):
                        dve.wait_ge(pt_ready, t.count(2, less=2))
                    dve.tensor_tensor(prob[:, t.slot(2), :, :], s_ps[t.slot(2)][:, :, :],
                                      top[:, t.slot(2), :].unsqueeze(2).to_broadcast([P, NH, S]), ALU.subtract)\
                        .then_inc(shifted, 1)
                t = i
                if t.exists():
                    dve.wait_ge(pv_ready, t.count())
                    if t.after(1):
                        dve.wait_ge(o_ready, t.count(less=1))
                    for b in range(2):
                        rows = slice(b * S, (b + 1) * S)
                        rc = dve.reciprocal(rden[rows, :, :], pv[rows, :, b, 16:18])
                    rc.then_inc(inverse_ready, 1)
                    dve.wait_ge(inverse_ready, t.count())
                    if t.after(1):
                        dve.wait_ge(ot_ready, t.count(less=1))
                    for b in range(2):
                        rows = slice(b * S, (b + 1) * S)
                        mu = dve.tensor_tensor(o[rows, :, :, :], pv[rows, :, b, 0:16].rearrange("p a (h d) -> p a h d", h=2),
                                               rden[rows, :, :].unsqueeze(3).to_broadcast([S, 8, 2, HD]), ALU.mult)
                    mu.then_inc(o_ready, 1)
                t = i + -2
                if t.exists():
                    dve.wait_ge(rstd_ready, t.count())
                    if t.after(2):
                        dve.wait_ge(stored[t.slot(2)], (t.uses(2) - 1) * 16)
                    dve.tensor_scalar(y[:, t.slot(2), :], r[:, t.slot(2), :], mv[:, t.slot(2), 0:1], rstd[:, t.slot(2), :],
                                      ALU.subtract, ALU.mult).then_inc(y_normed, 1)
            skewed(dve, step, 4, 2)


def turn_blocks(nc, stage, k, blocks):
    with ExitStack() as ctx:
        mk = Maker(nc, ctx, stage + "_turn")
        banks = [mk.ps(f"bank{i}", [P, 4, P]) for i in range(4)]
        turned, copied = mk.sem("turned"), mk.sem("copied")
        block = mk.block()

        @block.tensor
        def _(pe):
            for n, (src, dst) in enumerate(blocks):
                if n >= 4:
                    pe.wait_ge(copied, n - 3)
                rows, cols = src.shape
                nc.tensor.transpose(banks[n % 4][0:cols, 0, 0:rows], src, k["ident"][0:rows, 0:rows]).then_inc(turned, 1)

        @block.scalar
        def _(act):
            for n, (src, dst) in enumerate(blocks):
                rows, cols = src.shape
                act.wait_ge(turned, n + 1)
                act.copy(dst, banks[n % 4][0:cols, 0, 0:rows]).then_inc(copied, 1)


def load_all(nc, stage, pairs):
    with ExitStack() as ctx:
        mk = Maker(nc, ctx, stage + "_load")
        loaded = mk.sem("loaded")
        block = mk.block()

        @block.sync
        def _(sp):
            for dst, src in pairs:
                sp.dma_start(dst, src).then_inc(loaded, 16)
            sp.wait_ge(loaded, 16 * len(pairs))


def experts(nc, stage, k, x_in, a, x_out, top2):
    E = 8
    FC = 2 if top2 else 4
    with ExitStack() as ctx:
        mk = Maker(nc, ctx, stage)
        sb, ps, sem = mk.sb, mk.ps, mk.sem
        w_up = sb("w_up", [P, E, FC, P])
        w_up2 = sb("w_up2", [P, E, FC, P]) if top2 else None
        w_down = sb("w_down", [P, E, FC, P])
        w_gate = sb("w_gate", [P, E])
        if top2:
            with ExitStack() as tmp:
                mt = Maker(nc, tmp, stage + "_raw")
                r1, r2, r3 = mt.sb("r1", [P, E, FC, P]), mt.sb("r2", [P, E, FC, P]), mt.sb("r3", [P, E, FC, P])
                rg = mt.sb("rg", [E, P])
                load_all(nc, stage, [
                    (r1[:, :, :, :], a["W1"].rearrange("e (c f) d -> f e c d", f=P)),
                    (r2[:, :, :, :], a["W2"].rearrange("e (c f) d -> f e c d", f=P)),
                    (r3[:, :, :, :], a["W3"].rearrange("e d (c f) -> d e c f", f=P)), (rg[:, :], a["Wg"])])
                turn_blocks(nc, stage, k, [(r[:, e, c, :], w[:, e, c, :]) for r, w in ((r1, w_up), (r2, w_up2), (r3, w_down))
                                           for e in range(E) for c in range(FC)] + [(rg[:, :], w_gate[:, :])])
        else:
            b_up = sb("b_up", [P, E * FC])
            b_down = sb("b_down", [E, P])
            b_gate = sb("b_gate", [1, E])
            with ExitStack() as tmp:
                rb = Maker(nc, tmp, stage + "_raw").sb("rb", [E * FC, P])
                load_all(nc, stage, [
                    (w_up[:, :, :, :], a["W1"].rearrange("e h (c f) -> h e c f", f=P)),
                    (w_down[:, :, :, :], a["W2"].rearrange("e (c f) h -> f e c h", f=P)),
                    (w_gate[:, :], a["Wr"]), (b_gate[:, :], a["br"].rearrange("(a e) -> a e", a=1)),
                    (b_down[:, :], a["b2"]), (rb[:, :], a["b1"].rearrange("e (c f) -> (e c) f", f=P))])
                turn_blocks(nc, stage, k, [(rb[:, :], b_up[:, :])])

        x = sb("x", [P, 2, 4, P])
        xt = sb("xt", [P, 2, 4, P])
        hid = sb("hid", [P, 2, 4, P])
        act1 = sb("act1", [P, 2, 4, P]) if top2 else None
        acc = sb("acc", [P, 2, 4, P])
        prod = sb("prod", [P, 4, P])
        earlier = sb("earlier", [P, E, E])
        logit = sb("logit", [P, 4, E])
        mx = sb("mx", [P, 4])
        sh = sb("sh", [P, 4, E])
        ex = sb("ex", [P, 4, E])
        beats = sb("beats", [P, 4, E, E])
        ties = sb("ties", [P, 4, E, E])
        rank = sb("rank", [P, 4, E])
        sel = sb("sel", [P, 4, E])
        z = sb("z", [P, 4])
        rz = sb("rz", [P, 4])
        gate = sb("gate", [P, 2, 4, E])
        gate_t = sb("gate_t", [E, 4, P])
        r = sb("r", [P, 2, 4, P])
        stats = sb("stats", [P, 4, 6])
        mv = sb("mv", [P, 2, 4, 2])
        ve = sb("ve", [P, 2, 4])
        rstd = sb("rstd", [P, 2, 4])
        y = sb("y", [P, 2, 4, P])
        up_ps = [ps(f"up{i}", [P, 4, P]) for i in range(2)]
        up2_ps = [ps(f"up2_{i}", [P, 4, P]) for i in range(2)]
        down_ps = [ps(f"down{i}", [P, 4, P]) for i in range(2)]
        turn_ps = ps("turn", [P, 4, P])
        gate_ps = ps("gate", [P, 4, P])
        loaded = [sem(f"x_loaded{i}") for i in range(2)]
        stored = [sem(f"stored{i}") for i in range(2)]
        earlier_ready, xt_ready, xt_copied = sem("earlier_ready"), sem("xt_ready"), sem("xt_copied")
        logits_ready, logits_copied, ranked, shifted, exp_ready, gate_ready = (
            sem(n) for n in ("logits_ready", "logits_copied", "ranked", "shifted", "exp_ready", "gate_ready"))
        step_done = sem("gating_steps")
        gt_ready, gt_copied, bias_ready, bias_taken = sem("gt_ready"), sem("gt_copied"), sem("bias_ready"), sem("bias_taken")
        up_ready, act_ready, hid_ready, down_ready, gated, added = (
            sem(n) for n in ("up_ready", "act_ready", "hid_ready", "down_ready", "gated", "added"))
        summed, stats_ready, mean_ready, var_ready, rstd_ready, y_normed = (
            sem(n) for n in ("summed", "stats_ready", "mean_ready", "var_ready", "rstd_ready", "y_normed"))
        x_v = x_in.rearrange("(g n p) d -> g p n d", p=P, n=4)
        out_v = x_out.rearrange("(g n p) d -> g p n d", p=P, n=4)
        passed_dve = sem("passed_dve")
        U = E * FC
        G_STEPS = 9
        block = mk.block()

        def unit(g, u, less=0):
            v = (g.c * U + u + 1 - less)
            return v if g.static else g.j * (g.BODY * U) + v

        @block.sync
        def _(sp):
            def step(i):
                t = i + 2
                if t.exists():
                    if t.after(2):
                        sp.wait_ge(summed, t.count(less=2))
                    sp.dma_start(x[:, t.slot(2), :, :], x_v[t.n]).then_inc(loaded[t.slot(2)], 16)
                t = i + -1
                if t.exists():
                    sp.wait_ge(y_normed, t.count(4))
                    sp.dma_start(out_v[t.n], y[:, t.slot(2), :, :]).then_inc(stored[t.slot(2)], 16)
            skewed(sp, step, 2, 1, Group)
            for n in range(2):
                sp.wait_ge(stored[n], 16 * NT // 8)

        @block.gpsimd
        def _(pool):
            pool.memset(earlier[:, :, :], 1.0).then_inc(earlier_ready, 1)
            pool.wait_ge(earlier_ready, 1)
            pool.affine_select(out=earlier[:, :, :], in_=earlier[:, :, :], compare_op=ALU.is_gt, fill=0.0, base=0,
                               pattern=[[1, E], [-1, E]], channel_multiplier=0).then_inc(earlier_ready, 1)

            def step(i):
                if i.exists():
                    pool.wait_ge(var_ready, i.count())
                    if i.after(2):
                        pool.wait_ge(y_normed, i.count(4, less=2))
                    pool.tensor_tensor(rstd[:, i.slot(2), :], ve[:, i.slot(2), :], k["half"][:, :], ALU.pow).then_inc(rstd_ready, 1)
            skewed(pool, step, 0, 0, Group)

        @block.tensor
        def _(pe):
            def front(t, part):
                if not t.exists():
                    return
                if part == 0:
                    pe.wait_ge(loaded[t.slot(2)], t.uses(2) * 16)
                    if t.after(1):
                        pe.wait_ge(xt_copied, t.count(less=1))
                        if not top2:
                            pe.wait_ge(bias_taken, t.count(less=1))
                    for n in range(4):
                        tr = nc.tensor.transpose(turn_ps[:, n, :], x[:, t.slot(2), n, :], k["ident"][:, :])
                    tr.then_inc(xt_ready, 1)
                if part == 1:
                    pe.wait_ge(xt_copied, t.count())
                    if t.after(1):
                        pe.wait_ge(logits_copied, t.count(less=1))
                        if not top2:
                            pe.wait_ge(gt_copied, t.count(less=1))
                    for n in range(4):
                        mm = nc.tensor.matmul(gate_ps[:, n, 0:E], xt[:, t.slot(2), n, :], w_gate[:, :], start=True, stop=top2)
                        if not top2:
                            mm = nc.tensor.matmul(gate_ps[:, n, 0:E], k["ones"][:, :], b_gate[:, :], start=False, stop=True)
                    mm.then_inc(logits_ready, 1)
                if part == 2 and not top2:
                    pe.wait_ge(gate_ready, t.count())
                    for n in range(4):
                        tr = nc.tensor.transpose(gate_ps[0:E, n, :], gate[:, t.slot(2), n, :], k["ident"][:, :])
                    tr.then_inc(gt_ready, 1)
                if part == 3 and not top2:
                    pe.wait_ge(gt_copied, t.count())
                    for n in range(4):
                        mm = nc.tensor.matmul(turn_ps[:, n, :], gate_t[:, n, :], b_down[:, :], start=True, stop=True)
                    mm.then_inc(bias_ready, 1)

            def up(g, u):
                e, c = divmod(u, FC)
                if u >= 2 or g.after(1):
                    pe.wait_ge(hid_ready, unit(g, u, less=2))
                mm = nc.tensor.matmul(up_ps[u % 2][:, :, :], w_up[:, e, c, :], xt[:, g.slot(2), :, :], start=True, stop=True)
                if top2:
                    mm = nc.tensor.matmul(up2_ps[u % 2][:, :, :], w_up2[:, e, c, :], xt[:, g.slot(2), :, :], start=True, stop=True)
                mm.then_inc(up_ready, 1)

            def down(g, u):
                e, c = divmod(u, FC)
                pe.wait_ge(hid_ready, unit(g, u))
                if c == 0 and (e >= 2 or g.after(1)):
                    v = g.c * E + e - 1
                    pe.wait_ge(gated, v if g.static else g.j * (g.BODY * E) + v)
                for n in range(4):
                    mm = nc.tensor.matmul(down_ps[e % 2][:, n, :], hid[:, u % 2, n, :], w_down[:, e, c, :],
                                          start=(c == 0 and n == 0), stop=(c == FC - 1), skip_group_check=True)
                mm.then_inc(down_ready, 1)

            def step(i):
                if i.exists():
                    pe.wait_ge(gate_ready, i.count())
                    for u in range(U):
                        up(i, u)
                        if u:
                            down(i, u - 1)
                        for part, e in enumerate((1, 3, 5, 6)):
                            if u == e * FC:
                                front(i + 1, part)
                    down(i, U - 1)
                else:
                    for part in range(4):
                        front(i + 1, part)
            skewed(pe, step, 1, 0, Group)

        @block.scalar
        def _(act):
            def front(t, part):
                if not t.exists():
                    return
                if part == 0:
                    act.wait_ge(xt_ready, t.count())
                    if t.after(2):
                        act.wait_ge(up_ready, unit(t, U - 1, less=2 * U))
                        act.wait_ge(logits_ready, t.count(less=2))
                    act.copy(xt[:, t.slot(2), :, :], turn_ps[:, :, :]).then_inc(xt_copied, 1)
                if part == 1:
                    act.wait_ge(shifted, t.count())
                    if t.after(1):
                        act.wait_ge(gate_ready, t.count(less=1))
                    act.activation(ex[:, :, :], sh[:, :, :], ACT.Exp).then_inc(exp_ready, 1)
                if part == 2 and not top2:
                    act.wait_ge(gt_ready, t.count())
                    if t.after(1):
                        act.wait_ge(bias_ready, t.count(less=1))
                    act.copy(gate_t[:, :, :], gate_ps[0:E, :, :]).then_inc(gt_copied, 1)

            def step(i):
                if i.exists():
                    for u in range(U):
                        e, c = divmod(u, FC)
                        act.wait_ge(up_ready, unit(i, u))
                        if top2:
                            if u >= 2 or i.after(1):
                                act.wait_ge(hid_ready, unit(i, u, less=2))
                            act.activation(act1[:, u % 2, :, :], up_ps[u % 2][:, :, :], ACT.Silu).then_inc(act_ready, 1)
                        else:
                            if u >= 2 or i.after(1):
                                act.wait_ge(down_ready, unit(i, u, less=2))
                            act.activation(hid[:, u % 2, :, :], up_ps[u % 2][:, :, :], ACT.Relu, bias=b_up[:, u:u + 1])\
                                .then_inc(hid_ready, 1)
                        for part, e in enumerate((1, 3, 5)):
                            if u == e * FC:
                                front(i + 1, part)
                else:
                    for part in range(3):
                        front(i + 1, part)
            skewed(act, step, 1, 0, Group)

        @block.vector
        def _(dve):
            def chain(t, n):
                v = t.c * G_STEPS + n
                return v if t.static else t.j * (t.BODY * G_STEPS) + v

            def gating(t):
                if not t.exists():
                    return
                dve.wait_ge(logits_ready, t.count())
                dve.tensor_copy(logit[:, :, :], gate_ps[:, :, 0:E]).then_inc(logits_copied, 1)
                dve.wait_ge(logits_copied, t.count())
                dve.tensor_reduce(mx[:, :], logit[:, :, :], AX, ALU.max).then_inc(step_done, 1)
                dve.wait_ge(step_done, chain(t, 1))
                dve.tensor_tensor(sh[:, :, :], logit[:, :, :], mx[:, :].unsqueeze(2).to_broadcast([P, 4, E]), ALU.subtract)\
                    .then_inc(shifted, 1)
                src = logit
                if not top2:
                    dve.wait_ge(exp_ready, t.count())
                    src = ex
                for n in range(4):
                    one = src[:, n, :].unsqueeze(2).to_broadcast([P, E, E])
                    other = src[:, n:n + 1, :].to_broadcast([P, E, E])
                    dve.tensor_tensor(beats[:, n, :, :], other, one, ALU.is_gt)
                    tie = dve.tensor_tensor(ties[:, n, :, :], other, one, ALU.is_equal)
                tie.then_inc(step_done, 1)
                dve.wait_ge(step_done, chain(t, 2))
                for n in range(4):
                    tie = dve.tensor_tensor(ties[:, n, :, :], ties[:, n, :, :], earlier[:, :, :], ALU.mult)
                tie.then_inc(step_done, 1)
                dve.wait_ge(step_done, chain(t, 3))
                dve.tensor_tensor(beats[:, :, :, :], beats[:, :, :, :], ties[:, :, :, :], ALU.add).then_inc(step_done, 1)
                dve.wait_ge(step_done, chain(t, 4))
                dve.tensor_reduce(rank[:, :, :], beats[:, :, :, :], AX, ALU.add).then_inc(step_done, 1)
                dve.wait_ge(step_done, chain(t, 5))
                dve.wait_ge(exp_ready, t.count())
                dve.scalar_tensor_tensor(out=sel[:, :, :], in0=rank[:, :, :], scalar=1.5 if top2 else 0.5, in1=ex[:, :, :],
                                         op0=ALU.is_lt, op1=ALU.mult).then_inc(step_done, 1)
                dve.wait_ge(step_done, chain(t, 6))
                dve.tensor_reduce(z[:, :], (sel if top2 else ex)[:, :, :], AX, ALU.add).then_inc(step_done, 1)
                dve.wait_ge(step_done, chain(t, 7))
                dve.reciprocal(rz[:, :], z[:, :]).then_inc(step_done, 1)
                dve.wait_ge(step_done, chain(t, 8))
                dve.tensor_tensor(gate[:, t.slot(2), :, :], sel[:, :, :], rz[:, :].unsqueeze(2).to_broadcast([P, 4, E]), ALU.mult)\
                    .then_inc(step_done, 1)
                dve.wait_ge(step_done, chain(t, 9))
                dve.tensor_copy(rz[:, 0:1], rz[:, 1:2]).then_inc(gate_ready, 1)

            def bias(t):
                if t.exists() and not top2:
                    dve.wait_ge(bias_ready, t.count())
                    dve.tensor_copy(acc[:, t.slot(2), :, :], turn_ps[:, :, :]).then_inc(bias_taken, 1)

            def accumulate(g, e):
                dve.wait_ge(down_ready, unit(g, e * FC + FC - 1))
                if e == 0 and not top2:
                    dve.wait_ge(bias_taken, g.count())
                v = g.c * E + e
                prev = v if g.static else g.j * (g.BODY * E) + v
                if e or g.after(1):
                    dve.wait_ge(gated, prev)
                first = e == 0 and top2
                for n in range(4):
                    if first:
                        st = dve.tensor_scalar(acc[:, g.slot(2), n, :], down_ps[e % 2][:, n, :], gate[:, g.slot(2), n, e:e + 1], None, ALU.mult)
                    else:
                        st = dve.scalar_tensor_tensor(out=acc[:, g.slot(2), n, :], in0=down_ps[e % 2][:, n, :],
                                                      scalar=gate[:, g.slot(2), n, e:e + 1], in1=acc[:, g.slot(2), n, :],
                                                      op0=ALU.mult, op1=ALU.add)
                st.then_inc(gated, 1)

            def norm(t):
                if not t.exists():
                    return
                dve.wait_ge(rstd_ready, t.count())
                if t.after(2):
                    dve.wait_ge(stored[t.slot(2)], (t.uses(2) - 1) * 16)
                for n in range(4):
                    dve.tensor_scalar(y[:, t.slot(2), n, :], r[:, t.slot(2), n, :], mv[:, t.slot(2), n, 0:1],
                                      rstd[:, t.slot(2), n:n + 1], ALU.subtract, ALU.mult).then_inc(y_normed, 1)

            def step(i):
                if i.exists():
                    for u in range(U):
                        e, c = divmod(u, FC)
                        if top2:
                            dve.wait_ge(act_ready, unit(i, u))
                            if u >= 2 or i.after(1):
                                dve.wait_ge(down_ready, unit(i, u, less=2))
                            dve.tensor_tensor(hid[:, u % 2, :, :], up2_ps[u % 2][:, :, :], act1[:, u % 2, :, :], ALU.mult)\
                                .then_inc(hid_ready, 1)
                        if c == 1 and e:
                            accumulate(i, e - 1)
                        if u == FC:
                            norm(i + -1)
                        if u == 3 * FC:
                            gating(i + 1)
                        if u == 6 * FC:
                            bias(i + 1)
                    accumulate(i, E - 1)
                    dve.wait_ge(gated, i.count(E))
                    if i.after(2):
                        dve.wait_ge(y_normed, i.count(4, less=2))
                    dve.tensor_tensor(r[:, i.slot(2), :, :], x[:, i.slot(2), :, :], acc[:, i.slot(2), :, :], ALU.add).then_inc(summed, 1)
                    dve.wait_ge(summed, i.count())
                    for n in range(4):
                        dve.bn_stats(stats[:, n, :], r[:, i.slot(2), n, :]).then_inc(stats_ready, 1)
                    dve.wait_ge(stats_ready, i.count(4))
                    settle(dve, passed_dve)
                    for n in range(4):
                        ag = dve.bn_aggr(mv[:, i.slot(2), n, :], stats[:, n, :])
                    ag.then_inc(mean_ready, 1)
                    dve.wait_ge(mean_ready, i.count())
                    if i.after(2):
                        dve.wait_ge(rstd_ready, i.count(less=2))
                    dve.tensor_scalar(ve[:, i.slot(2), :], mv[:, i.slot(2), :, 1], LN_EPS, None, ALU.add).then_inc(var_ready, 1)
                elif i.c < 0:
                    gating(i + 1)
                    bias(i + 1)
                else:
                    norm(i + -1)
            dve.wait_ge(earlier_ready, 2)
            skewed(dve, step, 1, 1, Group)


ROW = 3 * S + 4
RMS_EPS, ETA_MIN = 1e-6, 1e-6
F = 64
N_MEM = F * D


def memory_products(nc, stage, k, x_in, a, rows_out, vk_out, q_out, w_out_t):
    with ExitStack() as ctx:
        mk = Maker(nc, ctx, stage)
        sb, ps, sem = mk.sb, mk.ps, mk.sem
        raw = sb("raw", [P, 4, D])
        w_k = sb("w_k", [P, F])
        w_q = sb("w_q", [P, F])
        w_v = sb("w_v", [P, D])
        w_norm = sb("w_norm", [P, 1])
        eta = sb("eta", [P, 1])
        eta_abs = sb("eta_abs", [P, 2])
        load_all(nc, stage, [(raw[0:F, 0, :], a["Wk"]), (raw[0:F, 1, :], a["Wq"]), (raw[:, 2, :], a["Wv"]), (raw[:, 3, :], a["Wout"]),
                             (w_norm[:, :], a["norm_weight"].rearrange("(d a) -> d a", a=1)),
                             (eta[0:F, :], a["eta"].rearrange("(f a) -> f a", a=1)),
                             (eta[F:P, :], a["eta"].rearrange("(f a) -> f a", a=1))])
        turn_blocks(nc, stage, k, [(raw[0:F, 0, :], w_k[:, :]), (raw[0:F, 1, :], w_q[:, :]), (raw[:, 2, :], w_v[:, :]),
                                   (raw[:, 3, :], w_out_t)])
        x = sb("x", [P, 4, D])
        sq = sb("sq", [P, D])
        ms = sb("ms", [P, 2, 1])
        mse = sb("mse", [P, 2, 1])
        rr = sb("rr", [P, 2, 1])
        xs = sb("xs", [P, 2, D])
        xt = sb("xt", [P, 2, P])
        low = sb("low", [P, 2, S])
        e = sb("e", [P, 2, S])
        kq = sb("kq", [P, 2, 2, S])
        ke = sb("ke", [P, 2, S])
        vt = sb("vt", [P, 2, P])
        vk = sb("vk", [S, 2, 2, D + F])
        row = sb("row", [P, 2, ROW])
        sums = sb("sums", [P, 2, 4])
        onesc = sb("onesc", [P, 1])
        t_ps, p_ps, vt_ps, v_ps, g_ps, ke_ps = (ps(n, [P, 512]) for n in ("t", "p", "vt", "v", "g", "ke"))
        loaded = [sem(f"x_loaded{i}") for i in range(4)]
        stored = [sem(f"stored{i}") for i in range(2)]
        (eta_ready, squares, mse_ready, rr_ready, xs_ready, xt_ready, xt_copied, proj_ready, low_ready, e_ready, kq_ready,
         ke_ready, v_copied, vt_copied, g_ready, ke_t_ready, ke_t_copied, row_copied, row_mult, row_p, row_ready) = (
            sem(n) for n in ("eta_ready", "squares", "mse_ready", "rr_ready", "xs_ready", "xt_ready", "xt_copied", "proj_ready",
                             "low_ready", "e_ready", "kq_ready", "ke_ready", "v_copied", "vt_copied", "g_ready", "ke_t_ready",
                             "ke_t_copied", "row_copied", "row_mult", "row_p", "row_ready"))
        x_v = x_in.rearrange("(n p) d -> n p d", p=P)
        passed_pe = sem("passed_pe")
        rows_v = rows_out.rearrange("(n p) r -> n p r", p=P)
        block = mk.block()

        @block.sync
        def _(sp):
            def step(i):
                t = i
                if t.exists():
                    sp.wait_ge(row_ready, t.count())
                    sp.wait_ge(ke_t_copied, t.count())
                    s2 = t.slot(2)
                    sp.dma_start(rows_v[t.n], row[:, s2, :]).then_inc(stored[s2], 16)
                    sp.dma_start(vk_out[t.n], vk[:, s2, :, :].rearrange("p a b -> p (a b)")).then_inc(stored[s2], 16)
                    sp.dma_start(q_out[t.n], kq[:, s2, 1, :]).then_inc(stored[s2], 16)
                t = i + 5
                if t.exists():
                    if t.after(4):
                        sp.wait_ge(xs_ready, t.count(less=4))
                    sp.dma_start(x[:, t.slot(4), :], x_v[t.n]).then_inc(loaded[t.slot(4)], 16)
            skewed(sp, step, 5, 0)
            for n in range(2):
                sp.wait_ge(stored[n], 3 * 16 * NT // 2)

        @block.gpsimd
        def _(pool):
            def step(i):
                t = i + 3
                if t.exists():
                    pool.wait_ge(mse_ready, t.count())
                    if t.after(2):
                        pool.wait_ge(xs_ready, t.count(less=2))
                    pool.tensor_tensor(rr[:, t.slot(2), :], mse[:, t.slot(2), :], k["half"][:, 0:1], ALU.pow).then_inc(rr_ready, 1)
            skewed(pool, step, 3, 0)

        @block.tensor
        def _(pe):
            def step(i):
                t = i
                if t.exists():
                    s2 = t.slot(2)
                    pe.wait_ge(ke_ready, t.count())
                    pe.wait_ge(vt_copied, t.count())
                    if t.after(1):
                        pe.wait_ge(row_p, t.count(less=1))
                    settle(pe, passed_pe)
                    for b in range(2):
                        rows = slice(b * S, (b + 1) * S)
                        key, ekey, val = kq[rows, s2, 0, :], ke[rows, s2, :], vt[:, s2, rows]
                        for col, lhs, rhs, width in ((0, key, ekey, S), (S, val, val, S), (2 * S, ekey, ekey, S),
                                                     (3 * S, key, onesc[rows, :], 1), (3 * S + 1, ekey, onesc[rows, :], 1),
                                                     (3 * S + 2, val, onesc[:, :], 1)):
                            mm = nc.tensor.matmul(g_ps[rows, col:col + width], lhs, rhs, start=True, stop=True)
                    mm.then_inc(g_ready, 1)
                    if t.after(1):
                        pe.wait_ge(ke_t_copied, t.count(less=1))
                    settle(pe, passed_pe)
                    nc.tensor.transpose(ke_ps[0:S, 0:P], ke[:, s2, :], k["ident"][:, :]).then_inc(ke_t_ready, 1)
                t = i + 1
                if t.exists():
                    s2 = t.slot(2)
                    pe.wait_ge(xt_copied, t.count())
                    if t.after(1):
                        pe.wait_ge(kq_ready, t.count(less=1))
                        pe.wait_ge(vt_copied, t.count(less=1))
                        pe.wait_ge(v_copied, t.count(less=1))
                    for col, w in ((0, w_k), (S, w_q)):
                        for b in range(2):
                            nc.tensor.matmul(p_ps[b * S:(b + 1) * S, col:col + S], w[:, :], xt[:, s2, b * S:(b + 1) * S], start=True, stop=True)
                    nc.tensor.matmul(vt_ps[:, 0:P], w_v[:, :], xt[:, s2, :], start=True, stop=True)
                    for b in range(2):
                        mm = nc.tensor.matmul(v_ps[0:S, b * D:(b + 1) * D], xt[:, s2, b * S:(b + 1) * S], w_v[:, :], start=True, stop=True)
                    mm.then_inc(proj_ready, 1)
                t = i + 2
                if t.exists():
                    pe.wait_ge(xs_ready, t.count())
                    if t.after(1):
                        pe.wait_ge(xt_copied, t.count(less=1))
                    nc.tensor.transpose(t_ps[:, 0:P], xs[:, t.slot(2), :], k["ident"][:, :]).then_inc(xt_ready, 1)
            pe.wait_ge(eta_ready, 4)
            skewed(pe, step, 3, 0)

        @block.scalar
        def _(act):
            def step(i):
                t = i
                if t.exists():
                    act.wait_ge(ke_t_ready, t.count())
                    act.copy(vk[:, t.slot(2), :, D:D + F], ke_ps[0:S, 0:P].rearrange("p (b f) -> p b f", b=2)).then_inc(ke_t_copied, 1)
                t = i + 1
                if t.exists():
                    s2 = t.slot(2)
                    act.wait_ge(low_ready, t.count())
                    if t.after(1):
                        act.wait_ge(kq_ready, t.count(less=1))
                    act.activation(e[:, :, :], low[:, :, :], ACT.Exp).then_inc(e_ready, 1)
                    act.wait_ge(proj_ready, t.count())
                    if t.after(2):
                        act.wait_ge(g_ready, t.count(less=2))
                    act.copy(vt[:, s2, :], vt_ps[:, 0:P]).then_inc(vt_copied, 1)
                    if t.after(2):
                        act.wait_ge(stored[s2], (t.uses(2) - 1) * 48)
                    act.copy(vk[:, s2, :, 0:D], v_ps[0:S, 0:2 * D].rearrange("p (b f) -> p b f", b=2)).then_inc(v_copied, 1)
                t = i + 2
                if t.exists():
                    act.wait_ge(xt_ready, t.count())
                    if t.after(2):
                        act.wait_ge(proj_ready, t.count(less=2))
                    act.mul(xt[:, t.slot(2), :], t_ps[:, 0:P], w_norm[:, 0:1]).then_inc(xt_copied, 1)
            skewed(act, step, 3, 0)

        @block.vector
        def _(dve):
            dve.memset(onesc[:, :], 1.0).then_inc(eta_ready, 1)
            dve.memset(row[:, :, :], 0.0).then_inc(eta_ready, 1)
            dve.tensor_scalar(eta_abs[:, 0:1], eta[:, :], -1.0, None, ALU.mult).then_inc(eta_ready, 1)
            dve.wait_ge(eta_ready, 3)
            dve.tensor_scalar(eta_abs[:, 1:2], eta[:, :], eta_abs[:, 0:1], ETA_MIN, ALU.max, ALU.max).then_inc(eta_ready, 1)
            dve.wait_ge(eta_ready, 4)

            def step(i):
                t = i + 3
                if t.exists():
                    s2 = t.slot(2)
                    dve.wait_ge(loaded[t.slot(4)], t.uses(4) * 16)
                    if t.after(1):
                        dve.wait_ge(squares, t.count(less=1))
                    dve.tensor_tensor_reduce(out=sq[:, :], in0=x[:, t.slot(4), :], in1=x[:, t.slot(4), :], scale=1.0 / D, scalar=0.0,
                                             op0=ALU.mult, op1=ALU.add, accum_out=ms[:, s2, :]).then_inc(squares, 1)
                    dve.wait_ge(squares, t.count())
                    if t.after(2):
                        dve.wait_ge(rr_ready, t.count(less=2))
                    dve.tensor_scalar(mse[:, s2, :], ms[:, s2, :], RMS_EPS, None, ALU.add).then_inc(mse_ready, 1)
                t = i + 1
                if t.exists():
                    s2 = t.slot(2)
                    dve.wait_ge(proj_ready, t.count())
                    if t.after(1):
                        dve.wait_ge(e_ready, t.count(less=1))
                    pq = p_ps[:, 0:2 * S].rearrange("p (a n) -> p a n", a=2)
                    dve.tensor_scalar(low[:, :, :], pq, 0.0, None, ALU.min).then_inc(low_ready, 1)
                t = i + 2
                if t.exists():
                    s2 = t.slot(2)
                    dve.wait_ge(rr_ready, t.count())
                    if t.after(2):
                        dve.wait_ge(xt_ready, t.count(less=2))
                    dve.tensor_scalar(xs[:, s2, :], x[:, t.slot(4), :], rr[:, s2, :], None, ALU.mult).then_inc(xs_ready, 1)
                t = i
                if t.exists():
                    s2 = t.slot(2)
                    dve.wait_ge(g_ready, t.count())
                    if t.after(2):
                        dve.wait_ge(stored[s2], (t.uses(2) - 1) * 48)
                    dve.tensor_copy(row[:, s2, 0:2 * S], g_ps[:, 0:2 * S]).then_inc(row_copied, 1)
                    if t.after(2):
                        dve.wait_ge(row_ready, t.count(less=2))
                    dve.tensor_copy(sums[:, s2, 0:3], g_ps[:, 3 * S:3 * S + 3]).then_inc(row_mult, 1)
                    dve.wait_ge(row_copied, t.count())
                    dve.wait_ge(row_mult, t.count())
                    dve.tensor_tensor(row[:, s2, 2 * S:3 * S], g_ps[:, 2 * S:3 * S], row[:, s2, S:2 * S], ALU.mult).then_inc(row_p, 1)
                    dve.tensor_scalar(row[:, s2, 3 * S + 1:3 * S + 2], sums[:, s2, 1:2], sums[:, s2, 2:3], None, ALU.mult)
                    dve.tensor_copy(row[:, s2, 3 * S:3 * S + 1], sums[:, s2, 0:1])
                    dve.tensor_copy(row[:, s2, 3 * S + 2:3 * S + 3], sums[:, s2, 2:3]).then_inc(row_ready, 1)
                t = i + 1
                if t.exists():
                    s2 = t.slot(2)
                    dve.wait_ge(e_ready, t.count())
                    if t.after(2):
                        dve.wait_ge(stored[s2], (t.uses(2) - 1) * 48)
                        dve.wait_ge(g_ready, t.count(less=2))
                    dve.scalar_tensor_tensor(out=kq[:, s2, :, :], in0=p_ps[:, 0:2 * S].rearrange("p (a n) -> p a n", a=2), scalar=0.0,
                                             in1=e[:, :, :], op0=ALU.max, op1=ALU.add).then_inc(kq_ready, 1)
                    dve.wait_ge(kq_ready, t.count())
                    if t.after(2):
                        dve.wait_ge(ke_t_ready, t.count(less=2))
                    dve.tensor_scalar(ke[:, s2, :], kq[:, s2, 0, :], eta_abs[:, 1:2], None, ALU.mult).then_inc(ke_ready, 1)
            skewed(dve, step, 3, 0)


def memory_recurrence(nc, stage, k, rows_in, coef, offset):
    with ExitStack() as ctx:
        mk = Maker(nc, ctx, stage)
        sb, sem = mk.sb, mk.sem
        g = sb("g", [P, S, ROW])
        w = sb("w", [P, S, S])
        prod = sb("prod", [P, S * S // 4])
        junk = sb("junk", [P, 3, S])
        quad = sb("quad", [P, S])
        part = sb("part", [P, 4, S])
        sv_neg2, p_n, p2, dd = (sb(n, [P, S]) for n in ("sv_neg2", "p_n", "p2", "dd"))
        v = {n: sb(n, [P, 1]) for n in ("mo", "m2", "pm", "q1", "a2", "i2", "gg", "h", "r2", "r2c", "y", "ry", "s2", "s", "h2", "nv", "ve",
                                        "z", "rz", "u", "u2", "rho", "mo2")}
        v = {n: t[:, :] for n, t in v.items()}
        N_CHUNK = 4
        loaded = [sem(f"rows_loaded{i}") for i in range(N_CHUNK)]
        link_sem, root_asked, root_ready = sem("steps"), sem("root_asked"), sem("root_ready")
        kk = lambda t, s: g[:, t, s]
        rows_v = rows_in.rearrange("(b t) r -> b t r", t=S)
        block = mk.block()

        @block.sync
        def _(sp):
            n = S // N_CHUNK
            for i in range(N_CHUNK):
                sp.dma_start(g[:, i * n:(i + 1) * n, :], rows_v[:, i * n:(i + 1) * n, :]).then_inc(loaded[i], 16)

        @block.scalar
        def _(act):
            for t in range(S):
                act.wait_ge(root_asked, 2 * t + 1)
                act.activation(v["y"], v["r2c"], ACT.Sqrt).then_inc(root_ready, 1)
                act.wait_ge(root_asked, 2 * t + 2)
                act.activation(v["z"], v["ve"], ACT.Sqrt).then_inc(root_ready, 1)

        @block.vector
        def _(dve):
            done = [0]

            def link(ins):
                done[0] += 1
                ins.then_inc(link_sem, 1)
                dve.wait_ge(link_sem, done[0])

            ts, stt, tt, ttr = dve.tensor_scalar, dve.scalar_tensor_tensor, dve.tensor_tensor, dve.tensor_tensor_reduce
            for s in loaded:
                dve.wait_ge(s, 16)
            ksum, pp, sv = (g[:, :, 3 * S + n] for n in range(3))
            link(ts(sv_neg2[:, :], sv, -2.0, None, ALU.mult))
            link(ts(p_n[:, :], pp, -1.0 / N_MEM, None, ALU.mult))
            link(ts(p2[:, :], pp, 2.0, None, ALU.mult))
            link(tt(dd[:, :], p_n[:, :], pp, ALU.mult))
            for t in range(S):
                last = tt(dd[:, t:t + 1], dd[:, t:t + 1], g[:, t, 2 * S + t:2 * S + t + 1], ALU.add)
            link(last)
            link(dve.memset(quad[:, :], 0.0))
            link(dve.memset(v["mo"], 0.0))
            link(dve.memset(v["m2"], 0.0))
            for t in range(S):
                col = slice(t, t + 1)
                rest = S - 1 - t
                vv_tt = g[:, t, S + t:S + t + 1]
                if t:
                    link(ttr(out=junk[:, 0, 0:t], in0=w[:, t, 0:t], in1=g[:, t, S:S + t], scale=-2.0, scalar=quad[:, col],
                             op0=ALU.mult, op1=ALU.add, accum_out=v["q1"]))
                    link(ttr(out=junk[:, 1, 0:t], in0=w[:, t, 0:t], in1=sv[:, 0:t], scale=2.0, scalar=sv_neg2[:, col],
                             op0=ALU.mult, op1=ALU.add, accum_out=v["a2"]))
                    link(ts(v["gg"], v["mo"], ksum[:, col], None, ALU.mult))
                    link(stt(out=v["h"], in0=v["gg"], scalar=float(D), in1=v["a2"], op0=ALU.mult, op1=ALU.add))
                    link(stt(out=v["r2"], in0=v["h"], scalar=v["gg"], in1=v["q1"], op0=ALU.mult, op1=ALU.add))
                    ask = ts(v["r2c"], v["r2"], vv_tt, 1e-30, ALU.add, ALU.max)
                else:
                    ask = ts(v["r2c"], vv_tt, 1e-30, None, ALU.max)
                ask.then_inc(root_asked, 1)
                if t:
                    link(ts(v["pm"], p2[:, col], v["mo"], None, ALU.mult))
                    link(ttr(out=junk[:, 2, 0:t], in0=coef[:, 0:t], in1=g[:, t, 2 * S:2 * S + t], scale=2.0, scalar=v["pm"],
                             op0=ALU.mult, op1=ALU.add, accum_out=v["i2"]))
                else:
                    link(dve.memset(v["i2"], 0.0))
                if t and rest:
                    pr = prod[:, 0:rest * t].rearrange("p (a b) -> p a b", b=t)
                    link(tt(pr, w[:, t + 1:S, 0:t], g[:, t:t + 1, S:S + t].to_broadcast([P, rest, t]), ALU.mult))
                    link(dve.tensor_reduce(part[:, 0, 0:rest], pr, AX, ALU.add))
                dve.wait_ge(root_ready, 2 * t + 1)
                link(dve.reciprocal(v["ry"], v["y"]))
                link(stt(out=v["s2"], in0=v["ry"], scalar=v["r2c"], in1=v["y"], op0=ALU.mult, op1=ALU.add))
                link(ts(v["s"], v["s2"], 0.5, None, ALU.mult))
                link(stt(out=v["h2"], in0=v["s"], scalar=dd[:, col], in1=v["i2"], op0=ALU.mult, op1=ALU.add))
                link(stt(out=v["nv"], in0=v["h2"], scalar=v["s"], in1=v["m2"], op0=ALU.mult, op1=ALU.add))
                ts(v["ve"], v["nv"], 1.0 / N_MEM, LN_EPS, ALU.mult, ALU.add).then_inc(root_asked, 1)
                link(dve.tensor_copy(coef[:, col], v["s"]))
                link(stt(out=v["mo2"], in0=v["s"], scalar=p_n[:, col], in1=v["mo"], op0=ALU.mult, op1=ALU.add))
                if rest:
                    nxt = w[:, t + 1:S, t]
                    link(ts(nxt, g[:, t + 1:S, t], v["s"], None, ALU.mult))
                    link(ts(part[:, 1, 0:rest], nxt, vv_tt, None, ALU.mult))
                    if t:
                        link(stt(out=part[:, 2, 0:rest], in0=part[:, 0, 0:rest], scalar=2.0, in1=part[:, 1, 0:rest],
                                 op0=ALU.mult, op1=ALU.add))
                    link(tt(part[:, 3, 0:rest], part[:, 2 if t else 1, 0:rest], nxt, ALU.mult))
                    link(tt(quad[:, t + 1:S], quad[:, t + 1:S], part[:, 3, 0:rest], ALU.add))
                dve.wait_ge(root_ready, 2 * t + 2)
                dve.wait_ge(root_asked, 2 * t + 2)
                link(dve.reciprocal(v["rz"], v["z"]))
                link(ts(v["u"], v["rz"], v["rz"], v["ve"], ALU.mult, ALU.mult))
                link(ts(v["u2"], v["u"], -0.5, 1.5, ALU.mult, ALU.add))
                link(ts(v["rho"], v["u2"], v["rz"], None, ALU.mult))
                ts(v["m2"], v["nv"], v["rho"], v["rho"], ALU.mult, ALU.mult)
                ts(v["mo"], v["mo2"], v["rho"], None, ALU.mult)
                last = ts(coef[:, 0:t + 1], coef[:, 0:t + 1], v["rho"], None, ALU.mult)
                if rest:
                    ts(quad[:, t + 1:S], quad[:, t + 1:S], v["rho"], v["rho"], ALU.mult, ALU.mult)
                    last = ts(w[:, t + 1:S, 0:t + 1], w[:, t + 1:S, 0:t + 1], v["rho"], None, ALU.mult)
                link(last)
            dve.tensor_copy(offset, v["mo"]).then_inc(link_sem, 1)


def memory_and_mixer(nc, stage, k, x_in, ctx_in, vk_in, q_in, w_out_t, coef, offset, x_out):
    with ExitStack() as ctx:
        mk = Maker(nc, ctx, stage)
        sb, ps, sem = mk.sb, mk.ps, mk.sem
        coef_t = sb("coef_t", [S, P])
        mine = sb("mine", [P, 2, NT])
        off_in = sb("off_in", [P, 2, NT])
        ones64 = sb("ones64", [P, F])
        off = sb("off", [P, NT])
        vk = sb("vk", [S, 2, 2, D + F])
        q_bd = sb("q_bd", [P, 2, 2, S])
        kc = sb("kc", [S, 2, 2, F])
        x = sb("x", [P, 4, D])
        c = sb("c", [P, 4, D])
        mem = sb("mem", [P, 2, D])
        read = sb("read", [P, 2, P])
        xm = sb("xm", [P, 4, D])
        xt = sb("xt", [P, 2, P])
        ct = sb("ct", [P, 2, P])
        g_bd = sb("g_bd", [P, 2, 2, S])
        r = [sb(f"r{n}", [P, 2, D]) for n in range(2)]
        stats = [sb(f"stats{n}", [P, 6]) for n in range(2)]
        mv = [sb(f"mv{n}", [P, 2, 2]) for n in range(2)]
        ve = [sb(f"ve{n}", [P, 2, 1]) for n in range(2)]
        rstd = [sb(f"rstd{n}", [P, 2, 1]) for n in range(2)]
        y = sb("y", [P, 2, D])
        m_ps, read_ps, out_ps, turn_ps, h_ps, mix_ps = (ps(n, [P, 512]) for n in ("m", "read", "out", "turn", "h", "mix"))
        (zeroed, mine_set, off_set, setup_ps, setup_copied, kc_ready, m_ready, m_copied, read_ready, read_copied, out_ready, turned, turn_copied,
         h_ready, g_ready, mix_ready) = (
            sem(n) for n in ("zeroed", "mine_set", "off_set", "setup_ps", "setup_copied", "kc_ready", "m_ready", "m_copied", "read_ready", "read_copied",
                             "out_ready", "turned", "turn_copied", "h_ready", "g_ready", "mix_ready"))
        summed, stats_ready, mean_ready, var_ready, rstd_ready, normed = (
            [sem(f"{n}{j}") for j in range(2)] for n in ("summed", "stats_ready", "mean_ready", "var_ready", "rstd_ready", "normed"))
        passed_dve, passed_pe = sem("passed_dve"), sem("passed_pe")
        vk_loaded = [sem(f"vk_loaded{i}") for i in range(2)]
        x_loaded = [sem(f"x_loaded{i}") for i in range(4)]
        c_loaded = [sem(f"c_loaded{i}") for i in range(4)]
        stored = [sem(f"stored{i}") for i in range(2)]
        x_v, c_v, out_v = (t.rearrange("(n p) d -> n p d", p=P) for t in (x_in, ctx_in, x_out))
        block = mk.block()

        @block.sync
        def _(sp):
            sp.wait_ge(zeroed, 3)

            def step(i):
                t = i + -1
                if t.exists():
                    sp.wait_ge(normed[1], t.count())
                    sp.dma_start(out_v[t.n], y[:, t.slot(2), :]).then_inc(stored[t.slot(2)], 16)
                t = i + 6
                if t.exists():
                    s2 = t.slot(2)
                    if t.after(2):
                        sp.wait_ge(m_ready, t.count(less=2))
                        sp.wait_ge(read_ready, t.count(less=2))
                    sp.dma_start(vk[:, s2, :, :].rearrange("p a b -> p (a b)"), vk_in[t.n]).then_inc(vk_loaded[s2], 16)
                    for b in range(2):
                        sp.dma_start(q_bd[b * S:(b + 1) * S, s2, b, :], q_in[t.n, b * S:(b + 1) * S, :]).then_inc(vk_loaded[s2], 16)
                t = i + 5
                if t.exists():
                    if t.after(4):
                        sp.wait_ge(summed[0], t.count(less=4))
                    sp.dma_start(x[:, t.slot(4), :], x_v[t.n]).then_inc(x_loaded[t.slot(4)], 16)
                t = i + 3
                if t.exists():
                    if t.after(4):
                        sp.wait_ge(mix_ready, t.count(less=4))
                    sp.dma_start(c[:, t.slot(4), :], c_v[t.n]).then_inc(c_loaded[t.slot(4)], 16)
            skewed(sp, step, 6, 1)
            for n in range(2):
                sp.wait_ge(stored[n], 16 * NT // 2)

        @block.gpsimd
        def _(pool):
            pool.memset(mine[:, :, :], 0.0).then_inc(mine_set, 1)
            pool.wait_ge(mine_set, 1)
            pool.affine_select(out=mine[:, :, :], in_=mine[:, :, :], compare_op=ALU.not_equal, fill=1.0, base=0,
                               pattern=[[-1, 2], [-2, NT]], channel_multiplier=1).then_inc(mine_set, 1)

            def step(i):
                for n, t in ((0, i + 3), (1, i)):
                    if t.exists():
                        s2 = t.slot(2)
                        pool.wait_ge(var_ready[n], t.count())
                        if t.after(2):
                            pool.wait_ge(normed[n], t.count(less=2))
                        pool.tensor_tensor(rstd[n][:, s2, :], ve[n][:, s2, :], k["half"][:, 0:1], ALU.pow).then_inc(rstd_ready[n], 1)
            skewed(pool, step, 6, 1)

        @block.tensor
        def _(pe):
            pe.wait_ge(zeroed, 3)
            pe.wait_ge(off_set, 1)
            nc.tensor.transpose(m_ps[0:S, 0:P], coef[:, :], k["ident"][:, :])
            for b in range(2):
                mm = nc.tensor.matmul(h_ps[b * S:(b + 1) * S, 0:NT], ones64[:, :], off_in[:, b, :], start=True, stop=True)
            mm.then_inc(setup_ps, 1)
            pe.wait_ge(setup_copied, 2)

            def step(i):
                t = i + 3
                if t.exists():
                    pe.wait_ge(read_copied, t.count())
                    if t.after(1):
                        pe.wait_ge(summed[0], t.count(less=1))
                    nc.tensor.matmul(out_ps[:, 0:D], read[:, t.slot(2), :], w_out_t, start=True, stop=True).then_inc(out_ready, 1)
                t = i + 1
                if t.exists():
                    pe.wait_ge(turn_copied, t.count())
                    if t.after(1):
                        pe.wait_ge(g_ready, t.count(less=1))
                    nc.tensor.matmul(h_ps[:, 0:P], ct[:, t.slot(2), :], xt[:, t.slot(2), :], start=True, stop=True).then_inc(h_ready, 1)
                t = i + 5
                if t.exists():
                    s2 = t.slot(2)
                    pe.wait_ge(kc_ready, t.count())
                    if t.after(1):
                        pe.wait_ge(m_copied, t.count(less=1))
                    settle(pe, passed_pe)
                    for b in range(2):
                        mm = nc.tensor.matmul(m_ps[b * F:(b + 1) * F, 0:D], kc[:, s2, b, :], vk[:, s2, b, 0:D], start=True, stop=True)
                    mm.then_inc(m_ready, 1)
                t = i
                if t.exists():
                    pe.wait_ge(g_ready, t.count())
                    if t.after(1):
                        pe.wait_ge(summed[1], t.count(less=1))
                    nc.tensor.matmul(mix_ps[:, 0:D], g_bd[:, t.slot(2), :, :], c[:, t.slot(4), :], start=True, stop=True).then_inc(mix_ready, 1)
                t = i + 4
                if t.exists():
                    pe.wait_ge(m_copied, t.count())
                    if t.after(1):
                        pe.wait_ge(read_copied, t.count(less=1))
                    nc.tensor.matmul(read_ps[:, 0:P], mem[:, t.slot(2), :], q_bd[:, t.slot(2), :, :], start=True, stop=True)\
                        .then_inc(read_ready, 1)
                t = i + 2
                if t.exists():
                    pe.wait_ge(c_loaded[t.slot(4)], t.uses(4) * 16)
                    pe.wait_ge(normed[0], t.count())
                    if t.after(1):
                        pe.wait_ge(turn_copied, t.count(less=1))
                    nc.tensor.transpose(turn_ps[:, P:2 * P], c[:, t.slot(4), :], k["ident"][:, :])
                    nc.tensor.transpose(turn_ps[:, 0:P], xm[:, t.slot(4), :], k["ident"][:, :]).then_inc(turned, 1)
            skewed(pe, step, 6, 0)

        @block.scalar
        def _(act):
            act.wait_ge(setup_ps, 1)
            act.copy(coef_t[:, :], m_ps[0:S, 0:P]).then_inc(setup_copied, 1)
            act.copy(off[:, :], h_ps[:, 0:NT]).then_inc(setup_copied, 1)
            act.wait_ge(setup_copied, 2)

            def step(i):
                t = i + 1
                if t.exists():
                    act.wait_ge(h_ready, t.count())
                    if t.after(2):
                        act.wait_ge(mix_ready, t.count(less=2))
                    for b in range(2):
                        rows = slice(b * S, (b + 1) * S)
                        ge = act.activation(g_bd[rows, t.slot(2), b, :], h_ps[rows, rows], ACT.Gelu_apprx_tanh)
                    ge.then_inc(g_ready, 1)
                t = i + 5
                if t.exists():
                    act.wait_ge(m_ready, t.count())
                    if t.after(2):
                        act.wait_ge(read_ready, t.count(less=2))
                    act.activation(mem[:, t.slot(2), :], m_ps[:, 0:D], ACT.Identity, bias=off[:, bass.ds(t.n, 1)]).then_inc(m_copied, 1)
                t = i + 4
                if t.exists():
                    act.wait_ge(read_ready, t.count())
                    if t.after(2):
                        act.wait_ge(out_ready, t.count(less=2))
                    act.copy(read[:, t.slot(2), :], read_ps[:, 0:P]).then_inc(read_copied, 1)
                t = i + 2
                if t.exists():
                    act.wait_ge(turned, t.count())
                    if t.after(2):
                        act.wait_ge(h_ready, t.count(less=2))
                    act.copy(xt[:, t.slot(2), :], turn_ps[:, 0:P])
                    act.copy(ct[:, t.slot(2), :], turn_ps[:, P:2 * P]).then_inc(turn_copied, 1)
            skewed(act, step, 6, 0)

        @block.vector
        def _(dve):
            dve.memset(q_bd[:, :, :, :], 0.0).then_inc(zeroed, 1)
            dve.memset(g_bd[:, :, :, :], 0.0).then_inc(zeroed, 1)
            dve.memset(ones64[:, :], 1.0).then_inc(zeroed, 1)
            dve.wait_ge(mine_set, 2)
            dve.tensor_scalar(off_in[:, :, :], mine[:, :, :], offset, None, ALU.mult).then_inc(off_set, 1)
            dve.wait_ge(setup_copied, 2)

            def add_norm(n, t, res, src):
                s2 = t.slot(2)
                if t.after(2):
                    dve.wait_ge(normed[n], t.count(less=2))
                dve.scalar_tensor_tensor(out=r[n][:, s2, :], in0=res, scalar=2.0 if n == 0 else 1.0, in1=src, op0=ALU.mult, op1=ALU.add)\
                    .then_inc(summed[n], 1)
                dve.wait_ge(summed[n], t.count())
                dve.bn_stats(stats[n][:, :], r[n][:, s2, :]).then_inc(stats_ready[n], 1)
                dve.wait_ge(stats_ready[n], t.count())
                settle(dve, passed_dve)
                dve.bn_aggr(mv[n][:, s2, :], stats[n][:, :]).then_inc(mean_ready[n], 1)
                dve.wait_ge(mean_ready[n], t.count())
                if t.after(2):
                    dve.wait_ge(rstd_ready[n], t.count(less=2))
                dve.tensor_scalar(ve[n][:, s2, :], mv[n][:, s2, 1:2], LN_EPS, None, ALU.add).then_inc(var_ready[n], 1)

            def norm(n, t, dst):
                s2 = t.slot(2)
                dve.wait_ge(rstd_ready[n], t.count())
                dve.tensor_scalar(dst, r[n][:, s2, :], mv[n][:, s2, 0:1], rstd[n][:, s2, :], ALU.subtract, ALU.mult)\
                    .then_inc(normed[n], 1)

            def step(i):
                t = i + 2
                if t.exists():
                    if t.after(4):
                        dve.wait_ge(summed[1], t.count(less=4))
                    norm(0, t, xm[:, t.slot(4), :])
                t = i + 3
                if t.exists():
                    dve.wait_ge(out_ready, t.count())
                    dve.wait_ge(x_loaded[t.slot(4)], t.uses(4) * 16)
                    add_norm(0, t, x[:, t.slot(4), :], out_ps[:, 0:D])
                t = i + 5
                if t.exists():
                    s2 = t.slot(2)
                    dve.wait_ge(vk_loaded[s2], t.uses(2) * 48)
                    if t.after(2):
                        dve.wait_ge(m_ready, t.count(less=2))
                    first = t.n * 2
                    dve.tensor_tensor(kc[:, s2, :, :], vk[:, s2, :, D:D + F],
                                      coef_t[:, bass.ds(first, 2)].unsqueeze(2).to_broadcast([S, 2, F]), ALU.mult).then_inc(kc_ready, 1)
                t = i + -1
                if t.exists():
                    if t.after(2):
                        dve.wait_ge(stored[t.slot(2)], (t.uses(2) - 1) * 16)
                    norm(1, t, y[:, t.slot(2), :])
                t = i
                if t.exists():
                    dve.wait_ge(mix_ready, t.count())
                    add_norm(1, t, xm[:, t.slot(4), :], mix_ps[:, 0:D])
            skewed(dve, step, 6, 1)


def build(nc, a, out):
    flat = lambda t: t.rearrange("b s d -> (b s) d")
    x1 = nc.dram_tensor("x1", (B * S, D), F32, kind="Internal").ap()
    x2 = nc.dram_tensor("x2", (B * S, D), F32, kind="Internal").ap()
    with ExitStack() as ctx:
        k = constants(nc, Maker(nc, ctx, "k"))
        wqkv, bqkv = a["L0_attn_W_qkv"], a["L0_attn_b_qkv"]
        w = {"wo": a["L0_attn_W_o"], "bo": a["L0_attn_b_o"]}
        for n, name in enumerate("qkv"):
            w["w" + name], w["b" + name] = wqkv[n * D:(n + 1) * D, :], bqkv[n * D:(n + 1) * D]
        attention(nc, "self", k, flat(a["x"]), None, None, w, x1)
        w = {m + name: a[f"L0_xattn_{m.upper() if m == 'w' else m}{name}"] for m in "wb" for name in "qkvo"}
        mask = a["mask_Bx1x1xS2_if1"].rearrange("b u v s -> (b u v) s")
        attention(nc, "cross", k, x1, flat(a["ctx_1024"]), mask, w, x2)
        ffn = {n: a["L0_ffn_" + n] for n in ("Wg", "W1", "W2", "W3")}
        experts(nc, "ffn0", k, x2, ffn, x1, top2=True)
        mem = {n: a["L1_attn_" + n] for n in ("norm_weight", "Wk", "Wv", "Wq", "eta", "Wout")}
        rows = nc.dram_tensor("memory_rows", (B * S, ROW), F32, kind="Internal").ap()
        vk = nc.dram_tensor("memory_vk", (NT, S, 2 * (D + F)), F32, kind="Internal").ap()
        q = nc.dram_tensor("memory_q", (NT, P, S), F32, kind="Internal").ap()
        with ExitStack() as mem_ctx:
            mm = Maker(nc, mem_ctx, "mem_state")
            w_out_t, coef, offset = mm.sb("w_out_t", [P, D]), mm.sb("coef", [P, S]), mm.sb("offset", [P, 1])
            memory_products(nc, "products", k, x1, mem, rows, vk, q, w_out_t[:, :])
            memory_recurrence(nc, "recur", k, rows, coef, offset[:, :])
            memory_and_mixer(nc, "mixer", k, x1, flat(a["ctx_1024"]), vk, q, w_out_t[:, :], coef, offset[:, :], x2)
        ffn = {n: a["L1_ffn_" + n] for n in ("Wr", "br", "W1", "b1", "W2", "b2")}
        experts(nc, "ffn1", k, x2, ffn, flat(out), top2=False)


INPUTS = ["x", "ctx_1024", "mask_Bx1x1xS2_if1",
          "L0_attn_W_qkv", "L0_attn_b_qkv", "L0_attn_W_o", "L0_attn_b_o",
          "L0_xattn_Wq", "L0_xattn_bq", "L0_xattn_Wk", "L0_xattn_bk", "L0_xattn_Wv", "L0_xattn_bv",
          "L0_xattn_Wo", "L0_xattn_bo",
          "L0_ffn_Wg", "L0_ffn_W1", "L0_ffn_W2", "L0_ffn_W3",
          "L1_attn_norm_weight", "L1_attn_Wk", "L1_attn_Wv", "L1_attn_Wq", "L1_attn_eta", "L1_attn_Wout",
          "L1_ffn_Wr", "L1_ffn_br", "L1_ffn_W1", "L1_ffn_b1", "L1_ffn_W2", "L1_ffn_b2"]


def kernel(**inputs):
    import numpy as _np
    import concourse.bacc as _bacc
    from concourse.bass_utils import run_bass_kernel_spmd as _run

    nc = _bacc.Bacc("TRN2", target_bir_lowering=False, num_devices=1)
    arrays, aps = {}, {}
    for name in INPUTS:
        v = _np.ascontiguousarray(inputs[name])
        arrays[f"in_{name}"] = v
        aps[name] = nc.dram_tensor(f"in_{name}", v.shape, mybir.dt.from_np(v.dtype), kind="ExternalInput").ap()
    out = nc.dram_tensor("decoded", (B, S, D), F32, kind="ExternalOutput").ap()
    build(nc, aps, out)
    r = _run(nc, [arrays], core_ids=[0])
    return r.results[0]["decoded"]
```

```python
from contextlib import ExitStack

import concourse.bass as bass
from concourse import mybir

F32 = mybir.dt.float32
BF16 = mybir.dt.bfloat16
I32 = mybir.dt.int32
U32 = mybir.dt.uint32
ALU = mybir.AluOpType
ACT = mybir.ActivationFunctionType
AX = mybir.AxisListType.X

P = 128
B, S, D = 128, 64, 128
NT = B * S // P
NH, HD = 16, 8
UNROLL = 4
NEG = -1.0e30
LN_EPS = 1e-5


class Tile:
    BODY, ALL = UNROLL, NT

    def __init__(self, j, c):
        self.j, self.c = j, c

    def __add__(self, k):
        return type(self)(self.j, self.c + k)

    def count(self, per=1, less=0):
        k = (self.c + 1 - less) * per
        return k if self.static else self.j * (self.BODY * per) + k

    @property
    def static(self):
        return isinstance(self.j, int)

    @property
    def n(self):
        return self.c if self.static else self.j * self.BODY + self.c

    def slot(self, n):
        return self.c % n

    def uses(self, n):
        k = self.c // n + 1
        return k if self.static else self.j * (self.BODY // n) + k

    def exists(self):
        return not self.static or 0 <= self.c < self.ALL

    def after(self, k):
        return not self.static or self.c >= k


class Group(Tile):
    BODY, ALL = 2, NT // 4


class Quad(Group):
    BODY = 4


class Sorted1(Tile):
    BODY, ALL = 8, NT + 8


class Sorted2(Sorted1):
    ALL = 2 * NT + 8


class Eights(Tile):
    BODY = 8


def four(t):
    g = t.c // 4
    return (g if t.static else t.j * 2 + g), g % 2, (g // 2 + 1 if t.static else t.j + (g // 2 + 1))


def skewed(eng, step, before, after, kind=Tile, peeled=4):
    first = max(1, peeled // kind.BODY)
    for c in range(-before, first * kind.BODY):
        step(kind(0, c))
    last = kind.ALL // kind.BODY - -(-before // kind.BODY)
    with eng.Fori(first, last) as j:
        for c in range(kind.BODY):
            step(kind(j, c))
    for c in range(last * kind.BODY, kind.ALL + after):
        step(kind(0, c))


class Maker:

    def __init__(self, nc, ctx, stage):
        self.nc, self.ctx, self.stage = nc, ctx, stage
        self.sems = []

    def sb(self, name, shape, dt=F32):
        return self.ctx.enter_context(self.nc.sbuf_tensor(f"{self.stage}_{name}", shape, dt))

    def ps(self, name, shape, dt=F32):
        return self.ctx.enter_context(self.nc.psum_tensor(f"{self.stage}_{name}_ps", shape, dt))

    def sem(self, name):
        self.sems.append(self.ctx.enter_context(self.nc.semaphore(f"{self.stage}_{name}")))
        return self.sems[-1]

    def block(self):
        self.ctx.callback(self.zero)
        return self.ctx.enter_context(self.nc.Block())

    def zero(self):
        with self.nc.Block() as block:

            @block.sync
            def _(sp):
                for s in self.sems:
                    sp.sem_clear(s)


def settle(eng, passed):
    eng.sem_inc(passed, 1)


def constants(nc, mk):
    k = {
        "ident": mk.sb("ident", [P, P]),
        "ident_bf": mk.sb("ident_bf", [P, P], BF16),
        "head_mask": mk.sb("head_mask", [P, 8]),
        "head_mask2": mk.sb("head_mask2", [P, 2, 8]),
        "causal": mk.sb("causal", [P, 8, S], BF16),
        "pick": mk.sb("pick", [2, 2, S], BF16),
        "ones": mk.sb("ones", [1, P]),
        "half": mk.sb("half", [P, 4]),
    }
    cleared, stamped, drawn = mk.sem("cleared"), mk.sem("stamped"), mk.sem("drawn")
    with nc.Block() as block:

        @block.gpsimd
        def _(pool):
            for n, v in (("ident", 0.0), ("ident_bf", 0.0), ("pick", 0.0), ("causal", 0.0),
                         ("head_mask2", 1.0), ("ones", 1.0), ("half", -0.5)):
                pool.memset(k[n][tuple(slice(None) for _ in k[n].shape)], v).then_inc(cleared, 1)
            pool.wait_ge(cleared, 7)
            for m in (k["ident"], k["ident_bf"]):
                pool.affine_select(out=m[:, :], in_=m[:, :], compare_op=ALU.not_equal, fill=1.0,
                                   base=0, pattern=[[-1, P]], channel_multiplier=1).then_inc(stamped, 1)
            pool.affine_select(out=k["pick"][:, :, :], in_=k["pick"][:, :, :], compare_op=ALU.not_equal,
                               fill=1.0, base=0, pattern=[[-1, 2], [0, S]], channel_multiplier=1)\
                .then_inc(stamped, 1)
            for b in range(2):
                rows = k["causal"][b * S:(b + 1) * S, :, :]
                pool.wait_ge(stamped, 3 + b)
                pool.affine_select(out=rows, in_=rows, compare_op=ALU.is_ge, fill=NEG, base=0,
                                   pattern=[[0, 8], [-1, S]], channel_multiplier=1).then_inc(stamped, 1)
            m = k["head_mask2"][:, :, :]
            pool.wait_ge(stamped, 5)
            pool.affine_select(out=m, in_=m, compare_op=ALU.is_ge, fill=0.0, base=0,
                               pattern=[[-S, 2], [-HD, 8]], channel_multiplier=1).then_inc(stamped, 1)
            pool.wait_ge(stamped, 6)
            pool.affine_select(out=m, in_=m, compare_op=ALU.is_ge, fill=0.0, base=HD - 1,
                               pattern=[[S, 2], [HD, 8]], channel_multiplier=-1).then_inc(stamped, 1)
            pool.wait_ge(stamped, 7)
            pool.tensor_tensor(k["head_mask"][:, :], k["head_mask2"][:, 0, :], k["head_mask2"][:, 1, :],
                               ALU.add).then_inc(drawn, 1)
    return k


def fill(nc, mk, xs):
    zeros = mk.sb("zeros", [P, 8 * D])
    zeros_set, filled = mk.sem("zeros_set"), mk.sem("xs_filled")
    with nc.Block() as block:

        @block.vector
        def _(dve):
            dve.memset(zeros[:, :], 0.0).then_inc(zeros_set, 1)

        @block.sync
        def _(sp):
            sp.wait_ge(zeros_set, 1)
            n = Sorted2.ALL // 8
            sp.dma_start(xs.rearrange("(p n r) d -> p n (r d)", p=P, r=8),
                         zeros[:, :].unsqueeze(1).to_broadcast([P, n, 8 * D])).then_inc(filled, 16)
    return filled


def attention(nc, stage, k, x_in, ctx_in, mask_in, w, x_out):
    cross = ctx_in is not None
    scale = float(HD) ** -0.5
    with ExitStack() as ctx:
        mk = Maker(nc, ctx, stage)
        sb, ps, sem = mk.sb, mk.ps, mk.sem
        w_raw = sb("w_raw", [P, 4, P])
        w_t = sb("w_t", [P, 4, P])
        b_row = sb("b_row", [1, P])
        b_cols = sb("b_cols", [P, 2, 2])
        bv_col = sb("bv_col", [P, 1])
        bo_all = sb("bo_all", [P, P])
        x = sb("x", [P, 2, P])
        c = sb("c", [P, 2, P])
        xr = sb("xr", [P, 2, P])
        xt = sb("xt", [P, 2, P])
        ct = sb("ct", [P, 2, P])
        q_bd = sb("q_bd", [P, 2, 2, 2, S])
        kt = sb("kt", [P, 2, 2, S])
        k_ex = sb("k_ex", [P, 2, 2, 8, S])
        v_bd = sb("v_bd", [P, 4, 8, 2, 18])
        prob = sb("prob", [P, 2, NH, S])
        prob_t = sb("prob_t", [P, 8, P])
        top = sb("top", [P, 2, NH])
        rden = sb("rden", [P, 8, 2])
        o = sb("o", [P, 8, 2, HD])
        ot = sb("ot", [P, P])
        r = sb("r", [P, 2, P])
        stats = sb("stats", [P, 6])
        mv = sb("mv", [P, 2, 2])
        ve = sb("ve", [P, 2, 1])
        rstd = sb("rstd", [P, 2, 1])
        y = sb("y", [P, 2, P])
        mask_i = sb("mask_i", [2, NT, S], I32)
        mask_n = sb("mask_n", [2, NT, S], BF16)

        s_ps = [ps(f"s_ps{i}", [P, NH, S]) for i in range(2)]
        pt_ps = [ps(f"pt_ps{i}", [P, 4, P]) for i in range(2)]
        front = ps("front", [P, 512])
        back = ps("back", [P, 512])
        fq = front[:, 0:128]
        fk = front[:, 128:256]
        fv = front[:, 256:384].rearrange("p (b n) -> p b n", b=2)
        pv = back[:, 0:288].rearrange("p (a b n) -> p a b n", a=8, b=2)
        b_ot, b_y = (back[:, n * P:(n + 1) * P] for n in (2, 3))
        b_xt, b_ct = (front[:, n * P:(n + 1) * P] for n in (0, 1))

        weights_in, w_psum, w_ready, bo_psum = sem("weights_in"), sem("w_psum"), sem("w_ready"), sem("bo_psum")
        zeroed, ones_set, mask_ready = sem("zeroed"), sem("ones_set"), sem("mask_ready")
        x_in_sem = [sem(f"x_loaded{i}") for i in range(2)]
        c_in_sem = [sem(f"ctx_loaded{i}") for i in range(2)]
        xr_in_sem = [sem(f"residual_loaded{i}") for i in range(2)]
        stored = [sem(f"stored{i}") for i in range(2)]
        xt_ready, xt_copied = sem("xt_ready"), sem("xt_copied")
        qkv_ready, q_copied, k_copied, v_copied = sem("qkv_ready"), sem("q_copied"), sem("k_copied"), sem("v_copied")
        keys_expanded, s_ready, top_ready, shifted = sem("keys_expanded"), sem("s_ready"), sem("top_ready"), sem("shifted")
        probs_ready, pt_ready, pt_copied, pv_ready = sem("probs_ready"), sem("pt_ready"), sem("pt_copied"), sem("pv_ready")
        inverse_ready, o_ready, ot_ready, ot_copied = sem("inverse_ready"), sem("o_ready"), sem("ot_ready"), sem("ot_copied")
        y_ready, residual_biased, summed, stats_ready = sem("y_ready"), sem("residual_biased"), sem("summed"), sem("stats_ready")
        mean_ready, var_ready, rstd_ready, y_normed = sem("mean_ready"), sem("var_ready"), sem("rstd_ready"), sem("y_normed")

        passed_dve = sem("passed_dve")

        names = ("q", "k", "v", "o")
        x_v = x_in.rearrange("(n p) d -> n p d", p=P)
        c_v = ctx_in.rearrange("(n p) d -> n p d", p=P) if cross else None
        out_v = x_out.rearrange("(n p) d -> n p d", p=P)
        n_weight_dmas = 14

        block = mk.block()

        @block.sync
        def _(sp):
            for n, name in enumerate(names):
                dst = w_t if cross else w_raw
                sp.dma_start(dst[:, n, :], w["w" + name]).then_inc(weights_in, 16)
            sp.dma_start(b_row[:, :], w["bo"].rearrange("(a n) -> a n", a=1)).then_inc(weights_in, 16)
            for n, name in enumerate(("q", "k")):
                for b in range(2):
                    for h in range(2):
                        sp.dma_start(b_cols[b * S:(b + 1) * S, n, h:h + 1],
                                     w["b" + name][h * S:(h + 1) * S].rearrange("(f a) -> f a", a=1)).then_inc(weights_in, 16)
            sp.dma_start(bv_col[:, :], w["bv"].rearrange("(n a) -> n a", a=1)).then_inc(weights_in, 16)
            if cross:
                sp.dma_start(mask_i[:, :, :], mask_in.rearrange("(i b) s -> b i s", b=2)).then_inc(mask_ready, 16)

            def step(i):
                t = i
                if t.exists():
                    if t.after(2):
                        sp.wait_ge(summed, t.count(less=2))
                    sp.dma_start(xr[:, t.slot(2), :], x_v[t.n]).then_inc(xr_in_sem[t.slot(2)], 16)
                t = i + -3
                if t.exists():
                    sp.wait_ge(y_normed, t.count())
                    sp.dma_start(out_v[t.n], y[:, t.slot(2), :]).then_inc(stored[t.slot(2)], 16)
                t = i + 6
                if t.exists():
                    if t.after(2):
                        sp.wait_ge(xt_ready, t.count(less=2))
                    sp.dma_start(x[:, t.slot(2), :], x_v[t.n]).then_inc(x_in_sem[t.slot(2)], 16)
                    if cross:
                        sp.dma_start(c[:, t.slot(2), :], c_v[t.n]).then_inc(c_in_sem[t.slot(2)], 16)
            skewed(sp, step, 6, 3, peeled=8)
            for n in range(2):
                sp.wait_ge(stored[n], 16 * NT // 2)

        @block.gpsimd
        def _(pool):
            def step(i):
                t = i + -1
                if t.exists():
                    pool.wait_ge(xr_in_sem[t.slot(2)], t.uses(2) * 16)
                    pool.tensor_tensor(xr[:, t.slot(2), :], xr[:, t.slot(2), :], bo_all[:, :], ALU.add)\
                        .then_inc(residual_biased, 1)
                t = i + -2
                if t.exists():
                    pool.wait_ge(var_ready, t.count())
                    if t.after(2):
                        pool.wait_ge(y_normed, t.count(less=2))
                    pool.tensor_tensor(rstd[:, t.slot(2), :], ve[:, t.slot(2), :], k["half"][:, 0:1], ALU.pow)\
                        .then_inc(rstd_ready, 1)
                t = i + 3
                if t.exists():
                    pool.wait_ge(k_copied, t.count())
                    if t.after(2):
                        pool.wait_ge(s_ready, t.count(less=2))
                    for h in range(2):
                        ex = pool.tensor_tensor(
                            k_ex[:, t.slot(2), h, :, :],
                            kt[:, t.slot(2), h:h + 1, :].to_broadcast([P, 8, S]),
                            k["head_mask"][:, :].unsqueeze(2).to_broadcast([P, 8, S]), ALU.mult)
                        ex.then_inc(keys_expanded, 1)
            pool.wait_ge(w_ready, 2)
            skewed(pool, step, 4, 2, peeled=8)

        @block.tensor
        def _(pe):
            pe.wait_ge(weights_in, 16 * n_weight_dmas)
            if not cross:
                for n in range(4):
                    wt = nc.tensor.transpose(front[:, n * P:(n + 1) * P], w_raw[:, n, :], k["ident"][:, :])
                wt.then_inc(w_psum, 1)
            nc.tensor.matmul(back[:, 0:P], k["ones"][:, :], b_row[:, :], start=True, stop=True).then_inc(bo_psum, 1)
            pe.wait_ge(w_ready, 2)

            def step(i):
                t = i + -1
                if t.exists():
                    pe.wait_ge(pt_copied, t.count(2))
                    if t.after(1):
                        pe.wait_ge(summed, t.count(less=1))
                    for n in range(8):
                        mm = nc.tensor.matmul(pv[:, n, :, :], prob_t[:, n, :], v_bd[:, t.slot(4), n, :, :], start=True, stop=True)
                    mm.then_inc(pv_ready, 1)
                t = i
                if t.exists():
                    pe.wait_ge(probs_ready, t.count())
                    for h in range(2):
                        if t.after(1):
                            pe.wait_ge(pt_copied, t.count(2, less=1))
                        for n in range(4):
                            a = 2 * (4 * h + n)
                            tr = nc.tensor.transpose(pt_ps[h][:, n, :], prob[:, t.slot(2), a:a + 2, :], k["ident"][:, :])
                        tr.then_inc(pt_ready, 1)
                t = i + 2
                if t.exists():
                    pe.wait_ge(keys_expanded, t.count(2) - 1)
                    pe.wait_ge(q_copied, t.count())
                    if t.after(2):
                        pe.wait_ge(shifted, t.count(less=2))
                    if cross:
                        pe.wait_ge(mask_ready, 17)
                    h = 0
                    dst = s_ps[t.slot(2)][:, 8 * h:8 * h + 8, :]
                    nc.tensor.matmul(dst, q_bd[:, t.slot(2), h, :, :], k_ex[:, t.slot(2), h, :, :], start=True, stop=False)
                    if cross:
                        mm = nc.tensor.matmul(dst, k["pick"][:, :, :], mask_n[:, bass.ds(t.n, 1), :].to_broadcast([2, 8, S]),
                                              start=False, stop=True)
                    else:
                        mm = nc.tensor.matmul(dst, k["ident_bf"][:, :], k["causal"][:, :, :], start=False, stop=True)
                t = i + 4
                if t.exists():
                    pe.wait_ge(x_in_sem[t.slot(2)], t.uses(2) * 16)
                    if t.after(1):
                        pe.wait_ge(xt_copied, t.count(less=1))
                    if t.after(2):
                        pe.wait_ge(q_copied, t.count(less=2))
                        pe.wait_ge(v_copied, t.count(less=2))
                    tr = nc.tensor.transpose(b_xt, x[:, t.slot(2), :], k["ident"][:, :])
                    if cross:
                        pe.wait_ge(c_in_sem[t.slot(2)], t.uses(2) * 16)
                        tr = nc.tensor.transpose(b_ct, c[:, t.slot(2), :], k["ident"][:, :])
                    tr.then_inc(xt_ready, 1)
                t = i + -1
                if t.exists():
                    pe.wait_ge(o_ready, t.count())
                    nc.tensor.transpose(b_ot, o[:, :, :, :], k["ident"][:, :]).then_inc(ot_ready, 1)
                t = i + 2
                if t.exists():
                    h = 1
                    pe.wait_ge(keys_expanded, t.count(2))
                    dst = s_ps[t.slot(2)][:, 8 * h:8 * h + 8, :]
                    nc.tensor.matmul(dst, q_bd[:, t.slot(2), h, :, :], k_ex[:, t.slot(2), h, :, :], start=True, stop=False)
                    if cross:
                        mm = nc.tensor.matmul(dst, k["pick"][:, :, :], mask_n[:, bass.ds(t.n, 1), :].to_broadcast([2, 8, S]),
                                              start=False, stop=True)
                    else:
                        mm = nc.tensor.matmul(dst, k["ident_bf"][:, :], k["causal"][:, :, :], start=False, stop=True)
                    mm.then_inc(s_ready, 1)
                t = i + -1
                if t.exists():
                    pe.wait_ge(ot_copied, t.count())
                    nc.tensor.matmul(b_y, ot[:, :], w_t[:, 3, :], start=True, stop=True).then_inc(y_ready, 1)
                t = i + 3
                if t.exists():
                    u = t + 1
                    pe.wait_ge(xt_copied, u.count() if u.exists() else NT)
                    if t.after(1):
                        pe.wait_ge(q_copied, t.count(less=1))
                        pe.wait_ge(v_copied, t.count(less=1))
                    xq = xt[:, t.slot(2), :]
                    xk = ct[:, t.slot(2), :] if cross else xq
                    for n, (src, dst) in enumerate(((xq, fq), (xk, fk))):
                        for h in range(2):
                            for b in range(2):
                                part = dst[b * S:(b + 1) * S, h * S:(h + 1) * S]
                                nc.tensor.matmul(part, w_t[:, n, h * S:(h + 1) * S], src[:, b * S:(b + 1) * S], start=True, stop=True)
                    wv = w_t[:, 2, :].rearrange("p (a h d) -> p a h d", h=2, d=HD)
                    for b in range(2):
                        for h in range(2):
                            mm = nc.tensor.matmul(fv[h * S:(h + 1) * S, b, :], xk[:, b * S:(b + 1) * S], wv[:, :, h, :], start=True, stop=True)
                    mm.then_inc(qkv_ready, 1)
            skewed(pe, step, 4, 1, peeled=8)

        @block.scalar
        def _(act):
            act.wait_ge(bo_psum, 1)
            if not cross:
                act.wait_ge(w_psum, 1)
                act.copy(w_t[:, :, :], front[:, :].rearrange("p (a n) -> p a n", a=4)).then_inc(w_ready, 1)
            else:
                act.copy(bo_all[:, 0:1], back[:, 0:1]).then_inc(w_ready, 1)
            act.wait_ge(w_ready, 1)
            act.copy(bo_all[:, :], back[:, 0:P]).then_inc(w_ready, 1)
            act.wait_ge(zeroed, 3)
            act.wait_ge(w_ready, 2)

            def step(i):
                t = i + 1
                if t.exists():
                    act.wait_ge(shifted, t.count())
                    act.activation(prob[:, t.slot(2), :, :], prob[:, t.slot(2), :, :], ACT.Exp, scale=scale)\
                        .then_inc(probs_ready, 1)
                t = i
                if t.exists():
                    for h in range(2):
                        act.wait_ge(pt_ready, t.count(2) - 1 + h)
                        if t.after(1):
                            act.wait_ge(pv_ready, t.count(less=1))
                        act.copy(prob_t[:, 4 * h:4 * h + 4, :], pt_ps[h][:, :, :]).then_inc(pt_copied, 1)
                t = i + 4
                if t.exists():
                    act.wait_ge(xt_ready, t.count())
                    if t.after(2):
                        act.wait_ge(qkv_ready, t.count(less=2))
                    cp = act.copy(xt[:, t.slot(2), :], b_xt)
                    if cross:
                        cp = act.copy(ct[:, t.slot(2), :], b_ct)
                    cp.then_inc(xt_copied, 1)
                t = i + -1
                if t.exists():
                    act.wait_ge(ot_ready, t.count())
                    if t.after(1):
                        act.wait_ge(y_ready, t.count(less=1))
                    act.activation(ot[:, :], b_ot, ACT.Identity, bias=bv_col[:, 0:1]).then_inc(ot_copied, 1)
                t = i + 3
                if t.exists():
                    act.wait_ge(qkv_ready, t.count())
                    if t.after(2):
                        act.wait_ge(keys_expanded, t.count(2, less=2))
                    for h in range(2):
                        cp = act.activation(kt[:, t.slot(2), h, :], fk[:, h * S:(h + 1) * S], ACT.Identity, bias=b_cols[:, 1, h:h + 1])
                    cp.then_inc(k_copied, 1)
                    if t.after(2):
                        act.wait_ge(s_ready, t.count(less=2))
                    for b in range(2):
                        rows = slice(b * S, (b + 1) * S)
                        for h in range(2):
                            cp = act.activation(q_bd[rows, t.slot(2), h, b, :], fq[rows, h * S:(h + 1) * S], ACT.Identity,
                                                bias=b_cols[rows, 0, h:h + 1])
                    cp.then_inc(q_copied, 1)
                    if t.after(4):
                        act.wait_ge(pv_ready, t.count(less=4))
                    for h in range(2):
                        rows = slice(h * S, (h + 1) * S)
                        cp = act.copy(v_bd[rows, t.slot(4), :, :, HD * h:HD * h + HD].rearrange("p a b d -> p b a d"),
                                      fv[rows, :, :].rearrange("p b (a d) -> p b a d", d=HD))
                    cp.then_inc(v_copied, 1)
            skewed(act, step, 4, 1, peeled=8)

        @block.vector
        def _(dve):
            dve.memset(q_bd[:, :, :, :, :], 0.0).then_inc(zeroed, 1)
            dve.memset(v_bd[:, :, :, :, :], 0.0).then_inc(zeroed, 1)
            dve.wait_ge(zeroed, 2)
            for h in range(2):
                one = dve.memset(v_bd[h * S:(h + 1) * S, :, :, :, 16 + h:17 + h], 1.0)
            one.then_inc(zeroed, 1)
            if cross:
                dve.wait_ge(mask_ready, 16)
                dve.tensor_scalar(mask_n[:, :, :], mask_i[:, :, :], 0.0, NEG, ALU.is_equal, ALU.mult).then_inc(mask_ready, 1)

            def step(i):
                t = i + -1
                if t.exists():
                    dve.wait_ge(pv_ready, t.count())
                    if t.after(1):
                        dve.wait_ge(o_ready, t.count(less=1))
                    for b in range(2):
                        rows = slice(b * S, (b + 1) * S)
                        rc = dve.reciprocal(rden[rows, :, :], pv[rows, :, b, 16:18])
                    rc.then_inc(inverse_ready, 1)
                    dve.wait_ge(inverse_ready, t.count())
                    if t.after(1):
                        dve.wait_ge(ot_ready, t.count(less=1))
                    for b in range(2):
                        rows = slice(b * S, (b + 1) * S)
                        mu = dve.tensor_tensor(o[rows, :, :, :], pv[rows, :, b, 0:16].rearrange("p a (h d) -> p a h d", h=2),
                                               rden[rows, :, :].unsqueeze(3).to_broadcast([S, 8, 2, HD]), ALU.mult)
                    mu.then_inc(o_ready, 1)
                t = i + -2
                if t.exists():
                    dve.wait_ge(summed, t.count())
                    dve.bn_stats(stats[:, :], r[:, t.slot(2), :]).then_inc(stats_ready, 1)
                    dve.wait_ge(stats_ready, t.count())
                    settle(dve, passed_dve)
                    dve.bn_aggr(mv[:, t.slot(2), :], stats[:, :]).then_inc(mean_ready, 1)
                    dve.wait_ge(mean_ready, t.count())
                    if t.after(2):
                        dve.wait_ge(rstd_ready, t.count(less=2))
                    dve.tensor_scalar(ve[:, t.slot(2), :], mv[:, t.slot(2), 1:2], LN_EPS, None, ALU.add).then_inc(var_ready, 1)
                t = i + -3
                if t.exists():
                    dve.wait_ge(rstd_ready, t.count())
                    if t.after(2):
                        dve.wait_ge(stored[t.slot(2)], (t.uses(2) - 1) * 16)
                    dve.tensor_scalar(y[:, t.slot(2), :], r[:, t.slot(2), :], mv[:, t.slot(2), 0:1], rstd[:, t.slot(2), :],
                                      ALU.subtract, ALU.mult).then_inc(y_normed, 1)
                t = i + -1
                if t.exists():
                    dve.wait_ge(y_ready, t.count())
                    dve.wait_ge(residual_biased, t.count())
                    if t.after(2):
                        dve.wait_ge(y_normed, t.count(less=2))
                    dve.tensor_tensor(r[:, t.slot(2), :], b_y, xr[:, t.slot(2), :], ALU.add).then_inc(summed, 1)
                t = i + 2
                if t.exists():
                    dve.wait_ge(s_ready, t.count())
                    if t.after(2):
                        dve.wait_ge(shifted, t.count(less=2))
                    dve.tensor_reduce(top[:, t.slot(2), :], s_ps[t.slot(2)][:, :, :], AX, ALU.max).then_inc(top_ready, 1)
                    dve.wait_ge(top_ready, t.count())
                    if t.after(2):
                        dve.wait_ge(pt_ready, t.count(2, less=2))
                    dve.tensor_tensor(prob[:, t.slot(2), :, :], s_ps[t.slot(2)][:, :, :],
                                      top[:, t.slot(2), :].unsqueeze(2).to_broadcast([P, NH, S]), ALU.subtract)\
                        .then_inc(shifted, 1)
            skewed(dve, step, 4, 3, peeled=8)


def turn_blocks(nc, stage, k, blocks):
    with ExitStack() as ctx:
        mk = Maker(nc, ctx, stage + "_turn")
        banks = [mk.ps(f"bank{i}", [P, 4, P]) for i in range(4)]
        turned, copied = mk.sem("turned"), mk.sem("copied")
        block = mk.block()

        @block.tensor
        def _(pe):
            for n, (src, dst) in enumerate(blocks):
                if n >= 4:
                    pe.wait_ge(copied, n - 3)
                rows, cols = src.shape
                nc.tensor.transpose(banks[n % 4][0:cols, 0, 0:rows], src, k["ident"][0:rows, 0:rows]).then_inc(turned, 1)

        @block.scalar
        def _(act):
            for n, (src, dst) in enumerate(blocks):
                rows, cols = src.shape
                act.wait_ge(turned, n + 1)
                act.copy(dst, banks[n % 4][0:cols, 0, 0:rows]).then_inc(copied, 1)


def load_all(nc, stage, pairs):
    with ExitStack() as ctx:
        mk = Maker(nc, ctx, stage + "_load")
        loaded = mk.sem("loaded")
        block = mk.block()

        @block.sync
        def _(sp):
            for dst, src in pairs:
                sp.dma_start(dst, src).then_inc(loaded, 16)
            sp.wait_ge(loaded, 16 * len(pairs))


def link_to(eng, sem):
    done = [0]

    def link(ins):
        done[0] += 1
        ins.then_inc(sem, 1)
        eng.wait_ge(sem, done[0])
    return link


def experts(nc, stage, k, x_in, a, x_out, top2, xs, ys, xs_filled, pool_dmas):
    E = 8
    K = 2 if top2 else 1
    FC = 2 if top2 else 4
    kind = Sorted2 if top2 else Sorted1
    T = kind.ALL
    H = 512
    with ExitStack() as ctx:
        mk = Maker(nc, ctx, stage)
        sb = mk.sb
        w_up = sb("w_up", [P, E, H])
        w_down = sb("w_down", [P, E, FC, P])
        x_all = sb("x_all", [P, NT, D])
        dest = sb("dest", [P, K, NT], U32)
        gate = sb("gate", [P, K, NT])
        expert_of = sb("expert_of", [1, T], I32)
        b_up = None if top2 else sb("b_up", [P, E, H])
        b_down = None if top2 else sb("b_down", [P, E, D])
        route(nc, stage, k, x_in, a, top2, xs, xs_filled, pool_dmas[0], T, w_up, w_down, b_up, b_down, x_all, dest, gate,
              expert_of)
        run_experts(nc, stage, k, top2, kind, xs, ys, w_up, w_down, b_up, b_down, expert_of)
        combine(nc, stage, k, K, ys, dest, gate, x_all, x_out, pool_dmas[1])


def route(nc, stage, k, x_in, a, top2, xs, xs_filled, scattered, T, w_up, w_down, b_up, b_down, x_all, dest, gate, expert_of):
    E, K, FC, H = 8, 2 if top2 else 1, 2 if top2 else 4, 512
    with ExitStack() as ctx:
        mk = Maker(nc, ctx, stage + "_route")
        sb, ps, sem = mk.sb, mk.ps, mk.sem
        w_gate = sb("w_gate", [P, E])
        b_gate = None if top2 else sb("b_gate", [P, E])
        raw = {n: sb("raw_" + n, [P, E, FC, P]) for n in ("W1", "W2", "W3")} if top2 else {}
        raw_gate = sb("raw_gate", [E, P]) if top2 else None
        x = sb("x", [P, 4, 4, D])
        xt = sb("xt", [P, 2, 4, P])
        before = sb("before", [P, P], BF16)
        all_ones = sb("all_ones", [P, P], BF16)
        order = sb("order", [P, E])
        steps128 = sb("steps128", [P, NT])
        tile_no = sb("tile_no", [1, T])
        big = {n: sb(n, [P, NT, E]) for n in ("logit", "shifted", "ex", "rest", "equal", "ranked", "pos", "even", "odd", "total")}
        sel = sb("sel", [P, K, NT, E])
        sel_bf = sb("sel_bf", [P, NT, E], BF16)
        mx = sb("mx", [P, 3, NT])
        first = sb("first", [P, NT])
        small = {n: sb(n, [P, NT]) for n in ("diff", "e2", "z", "rz")}
        fits = sb("fits", [P, E, NT])
        ends = sb("ends", [P, 2, E])
        n_tiles = sb("n_tiles", [P, E])
        base = sb("base", [P, E])
        dest_f = sb("dest_f", [P, K, NT])
        passed = sb("passed", [1, T, E])
        expert_f = sb("expert_f", [1, 2, T])
        turn_ps = [ps(f"turn{i}", [P, 4, P]) for i in range(2)]
        logits_ps = ps("logits", [P, NT, E])
        before_ps, total_ps = ps("before", [P, NT, E]), ps("total", [P, NT, E])
        earlier = 0 if top2 else 16 * 2 * NT
        weights_in, gate_in, made = sem("weights_in"), sem("gate_in"), sem("made")
        loaded = [sem(f"x_loaded{i}") for i in range(4)]
        x_kept, xt_ready, xt_copied, logits_ready = sem("x_kept"), sem("xt_ready"), sem("xt_copied"), sem("logits_ready")
        gate_turned, gate_copied = sem("gate_turned"), sem("gate_copied")
        exp_asked, exp_ready, selected, counted = sem("exp_asked"), sem("exp_ready"), sem("selected"), sem("counted")
        routed, link_sem = sem("routed"), sem("chain")
        w_turned, w_copied = sem("w_turned"), sem("w_copied")
        x_v = x_in.rearrange("(g n p) d -> g p n d", p=P, n=4)
        blocks = []
        if top2:
            up_v = w_up[:, :, :].rearrange("p e (s c n) -> p e s c n", s=2, n=P)
            for e in range(E):
                for c in range(FC):
                    blocks += [(raw["W1"][:, e, c, :], up_v[:, e, 0, c, :]), (raw["W2"][:, e, c, :], up_v[:, e, 1, c, :]),
                               (raw["W3"][:, e, c, :], w_down[:, e, c, :])]
        block = mk.block()

        @block.sync
        def _(sp):
            if top2:
                sp.dma_start(raw_gate[:, :], a["Wg"]).then_inc(gate_in, 16)
            else:
                sp.dma_start(w_gate[:, :], a["Wr"]).then_inc(gate_in, 16)
                sp.dma_start(b_gate[:, :], a["br"].rearrange("(a e) -> a e", a=1).to_broadcast([P, E])).then_inc(gate_in, 16)

            def step(i):
                if i.exists():
                    if i.after(4):
                        sp.wait_ge(xt_ready, i.count(less=4))
                        sp.wait_ge(x_kept, i.count(less=4))
                    sp.dma_start(x[:, i.slot(4), :, :], x_v[i.n]).then_inc(loaded[i.slot(4)], 16)
            skewed(sp, step, 0, 0, Quad)
            if top2:
                sp.dma_start(raw["W1"][:, :, :, :], a["W1"].rearrange("e (c f) d -> f e c d", f=P)).then_inc(weights_in, 16)
                sp.dma_start(raw["W2"][:, :, :, :], a["W2"].rearrange("e (c f) d -> f e c d", f=P)).then_inc(weights_in, 16)
                sp.dma_start(raw["W3"][:, :, :, :], a["W3"].rearrange("e d (c f) -> d e c f", f=P)).then_inc(weights_in, 16)
            else:
                sp.dma_start(w_up[:, :, :], a["W1"].rearrange("e h f -> h e f")).then_inc(weights_in, 16)
                sp.dma_start(w_down[:, :, :, :], a["W2"].rearrange("e (c f) h -> f e c h", f=P)).then_inc(weights_in, 16)
                sp.dma_start(b_up[:, :, :].rearrange("p e h -> p (e h)"),
                             a["b1"].rearrange("(a e) h -> a (e h)", a=1).to_broadcast([P, E * H])).then_inc(weights_in, 16)
                sp.dma_start(b_down[:, :, :].rearrange("p e h -> p (e h)"),
                             a["b2"].rearrange("(a e) h -> a (e h)", a=1).to_broadcast([P, E * D])).then_inc(weights_in, 16)
            sp.wait_ge(weights_in, 48 if top2 else 64)

        @block.gpsimd
        def _(pool):
            pool.memset(before[:, :], 1.0).then_inc(made, 1)
            pool.memset(all_ones[:, :], 1.0).then_inc(made, 1)
            pool.iota(order[:, :], pattern=[[-1, E]], base=E, channel_multiplier=0, allow_small_or_imprecise_dtypes=True).then_inc(made, 1)
            pool.iota(steps128[:, :], pattern=[[P, NT]], base=0, channel_multiplier=0, allow_small_or_imprecise_dtypes=True).then_inc(made, 1)
            pool.iota(tile_no[:, :], pattern=[[1, T]], base=0, channel_multiplier=0, allow_small_or_imprecise_dtypes=True).then_inc(made, 1)
            pool.wait_ge(made, 5)
            pool.affine_select(out=before[:, :], in_=before[:, :], compare_op=ALU.is_gt, fill=0.0, base=0,
                               pattern=[[1, P]], channel_multiplier=-1).then_inc(made, 1)
            pool.wait_ge(x_kept, NT // 4)
            pool.wait_ge(routed, 1)
            pool.wait_ge(xs_filled, 16)
            for r in range(K):
                for t in range(NT):
                    pool.indirect_dma_start(xs, bass.IndirectOffsetOnAxis(ap=dest[:, r, t:t + 1], axis=0), x_all[:, t, :], None)\
                        .then_inc(scattered, 16)
            pool.wait_ge(scattered, 16 * K * NT + earlier)

        @block.tensor
        def _(pe):
            pe.wait_ge(gate_in, 16 if top2 else 32)
            if top2:
                nc.tensor.transpose(before_ps[:, :, :].rearrange("p a b -> p (a b)")[:, 0:E], raw_gate[:, :], k["ident"][0:E, 0:E])\
                    .then_inc(gate_turned, 1)
                pe.wait_ge(gate_copied, 1)

            def step(i):
                t = i + 1
                if t.exists():
                    pe.wait_ge(loaded[t.slot(4)], t.uses(4) * 16)
                    if t.after(2):
                        pe.wait_ge(xt_copied, t.count(less=2))
                    for n in range(4):
                        tr = nc.tensor.transpose(turn_ps[t.slot(2)][:, n, :], x[:, t.slot(4), n, :], k["ident"][:, :])
                    tr.then_inc(xt_ready, 1)
                t = i
                if t.exists():
                    pe.wait_ge(xt_copied, t.count())
                    for n in range(4):
                        tile = t.n * 4 + n
                        mm = nc.tensor.matmul(logits_ps[:, bass.ds(tile, 1), :], xt[:, t.slot(2), n, :], w_gate[:, :], start=True, stop=True)
                    mm.then_inc(logits_ready, 1)
            skewed(pe, step, 1, 0, Quad)
            pe.wait_ge(made, 6)
            pe.wait_ge(selected, 1)
            nc.tensor.matmul(total_ps[:, :, :], all_ones[:, :], sel_bf[:, :, :], start=True, stop=True)
            nc.tensor.matmul(before_ps[:, :, :], before[:, :], sel_bf[:, :, :], start=True, stop=True).then_inc(counted, 1)
            if blocks:
                pe.wait_ge(weights_in, 48)
            for n, (src, dst) in enumerate(blocks):
                if n >= 2:
                    pe.wait_ge(w_copied, n - 1)
                nc.tensor.transpose(turn_ps[n % 2][:, 0, :], src, k["ident"][:, :]).then_inc(w_turned, 1)

        @block.scalar
        def _(act):
            if top2:
                act.wait_ge(gate_turned, 1)
                act.copy(w_gate[:, :], before_ps[:, :, :].rearrange("p a b -> p (a b)")[:, 0:E]).then_inc(gate_copied, 1)

            def step(i):
                if i.exists():
                    act.wait_ge(xt_ready, i.count())
                    if i.after(2):
                        act.wait_ge(logits_ready, i.count(less=2))
                    act.copy(xt[:, i.slot(2), :, :], turn_ps[i.slot(2)][:, :, :]).then_inc(xt_copied, 1)
            skewed(act, step, 0, 0, Quad)
            act.wait_ge(exp_asked, 1)
            if top2:
                act.activation(small["e2"][:, :], small["diff"][:, :], ACT.Exp).then_inc(exp_ready, 1)
            else:
                act.activation(big["ex"][:, :, :], big["shifted"][:, :, :], ACT.Exp).then_inc(exp_ready, 1)
            for n, (src, dst) in enumerate(blocks):
                act.wait_ge(w_turned, n + 1)
                act.copy(dst, turn_ps[n % 2][:, 0, :]).then_inc(w_copied, 1)

        @block.vector
        def _(dve):
            link = link_to(dve, link_sem)
            tt, ts, stt, red = dve.tensor_tensor, dve.tensor_scalar, dve.scalar_tensor_tensor, dve.tensor_reduce
            full = lambda n: big[n][:, :, :]
            wide = lambda v: v.unsqueeze(2).to_broadcast([P, NT, E])
            rows = lambda v: v.unsqueeze(1).to_broadcast([P, NT, E])

            def choose(r, src):
                link(red(mx[:, r, :], src, AX, ALU.max))
                link(tt(full("equal"), src, wide(mx[:, r, :]), ALU.is_equal))
                link(tt(full("ranked"), full("equal"), rows(order[:, :]), ALU.mult))
                link(red(first[:, :], full("ranked"), AX, ALU.max))
                link(tt(sel[:, r, :, :], full("ranked"), wide(first[:, :]), ALU.is_equal))

            def step(i):
                if i.exists():
                    dve.wait_ge(loaded[i.slot(4)], i.uses(4) * 16)
                    first_tile = i.n * 4
                    dve.tensor_copy(x_all[:, bass.ds(first_tile, 4), :], x[:, i.slot(4), :, :]).then_inc(x_kept, 1)
            skewed(dve, step, 0, 0, Quad)
            dve.wait_ge(made, 6)
            dve.wait_ge(logits_ready, NT // 4)
            if top2:
                link(dve.tensor_copy(full("logit"), logits_ps[:, :, :]))
                choose(0, full("logit"))
                link(ts(full("rest"), sel[:, 0, :, :], -1.0, 1.0, ALU.mult, ALU.add))
                link(tt(full("ex"), full("rest"), full("logit"), ALU.mult))
                link(stt(out=full("rest"), in0=sel[:, 0, :, :], scalar=-3.0e38, in1=full("ex"), op0=ALU.mult, op1=ALU.add))
                choose(1, full("rest"))
                tt(small["diff"][:, :], mx[:, 1, :], mx[:, 0, :], ALU.subtract).then_inc(exp_asked, 1)
                tt(sel_bf[:, :, :], sel[:, 0, :, :], sel[:, 1, :, :], ALU.add).then_inc(selected, 1)
            else:
                dve.wait_ge(gate_in, 32)
                link(tt(full("logit"), logits_ps[:, :, :], rows(b_gate[:, :]), ALU.add))
                link(red(mx[:, 2, :], full("logit"), AX, ALU.max))
                tt(full("shifted"), full("logit"), wide(mx[:, 2, :]), ALU.subtract).then_inc(exp_asked, 1)
                dve.wait_ge(exp_ready, 1)
                choose(0, full("ex"))
                dve.tensor_copy(sel_bf[:, :, :], sel[:, 0, :, :]).then_inc(selected, 1)
                link(red(small["z"][:, :], full("ex"), AX, ALU.add))
                link(dve.reciprocal(small["rz"][:, :], small["z"][:, :]))
                link(tt(gate[:, 0, :], mx[:, 0, :], small["rz"][:, :], ALU.mult))
            dve.wait_ge(counted, 1)
            link(dve.tensor_copy(full("total"), total_ps[:, :, :]))
            src, stride, spare = "total", 1, ["even", "odd"]
            while stride < NT:
                dst = spare[0]
                dve.tensor_copy(big[dst][:, 0:stride, :], big[src][:, 0:stride, :])
                link(tt(big[dst][:, stride:, :], big[src][:, stride:, :], big[src][:, :NT - stride, :], ALU.add))
                src, stride, spare = dst, 2 * stride, spare[::-1]
            counts = big[src][:, NT - 1, :]
            link(tt(fits[:, :, :], counts.unsqueeze(2).to_broadcast([P, E, NT]),
                    steps128[:, :].unsqueeze(1).to_broadcast([P, E, NT]), ALU.is_gt))
            link(red(n_tiles[:, :], fits[:, :, :], AX, ALU.add))
            link(dve.tensor_copy(ends[:, 0, :], n_tiles[:, :]))
            now, stride = 0, 1
            while stride < E:
                dve.tensor_copy(ends[:, 1 - now, 0:stride], ends[:, now, 0:stride])
                link(tt(ends[:, 1 - now, stride:], ends[:, now, stride:], ends[:, now, :E - stride], ALU.add))
                now, stride = 1 - now, 2 * stride
            link(tt(base[:, :], ends[:, now, :], n_tiles[:, :], ALU.subtract))
            link(ts(base[:, :], base[:, :], float(P), None, ALU.mult))
            link(tt(full("pos"), big[src][:, :, :], full("total"), ALU.subtract))
            link(tt(full("pos"), full("pos"), before_ps[:, :, :], ALU.add))
            link(tt(full("pos"), full("pos"), rows(base[:, :]), ALU.add))
            for r in range(K):
                link(tt(full("equal"), full("pos"), sel[:, r, :, :], ALU.mult))
                link(red(dest_f[:, r, :], full("equal"), AX, ALU.add))
            dve.tensor_copy(dest[:, :, :], dest_f[:, :, :]).then_inc(routed, 1)
            link(tt(passed[:, :, :], tile_no[:, :].unsqueeze(2).to_broadcast([1, T, E]),
                    ends[0:1, now:now + 1, :].to_broadcast([1, T, E]), ALU.is_ge))
            link(red(expert_f[:, 0, :], passed[:, :, :], AX, ALU.add))
            link(ts(expert_f[:, 1, :], expert_f[:, 0, :], float(E - 1), None, ALU.min))
            link(dve.tensor_copy(expert_of[:, :], expert_f[:, 1, :]))
            if top2:
                dve.wait_ge(exp_ready, 1)
                link(ts(small["z"][:, :], small["e2"][:, :], 1.0, None, ALU.add))
                link(dve.reciprocal(gate[:, 0, :], small["z"][:, :]))
                link(tt(gate[:, 1, :], small["e2"][:, :], gate[:, 0, :], ALU.mult))


def run_experts(nc, stage, k, top2, kind, xs, ys, w_up, w_down, b_up, b_down, expert_of):
    FC, H = 2 if top2 else 4, 512
    HID = FC * P
    with ExitStack() as ctx:
        mk = Maker(nc, ctx, stage + "_run")
        sb, ps, sem = mk.sb, mk.ps, mk.sem
        x = sb("x", [P, 2, 4, D])
        y = sb("y", [P, 2, 4, D])
        xt = sb("xt", [P, 2, P])
        act1 = sb("act1", [P, 2, HID]) if top2 else None
        h = sb("h", [P, 2, HID])
        ht = sb("ht", [P, 2, FC, P])
        xt_ps, up_ps, ht_ps, y_ps = ([ps(f"{n}{i}", [P, 512]) for i in range(2)] for n in ("xt", "up", "ht", "y"))
        loaded = [sem(f"x_loaded{i}") for i in range(2)]
        stored = [sem(f"stored{i}") for i in range(2)]
        x_turned, x_copied, up_ready, silu_ready, h_ready, h_turned, h_copied, down_ready, y_copied = (
            sem(n) for n in ("x_turned", "x_copied", "up_ready", "silu_ready", "h_ready", "h_turned", "h_copied", "down_ready", "y_copied"))
        xs_v, ys_v = (t[0:kind.ALL * P, :].rearrange("(g n p) d -> g p n d", p=P, n=4) for t in (xs, ys))
        block = mk.block()

        @block.sync
        def _(sp):
            def step(i):
                t = i + -1
                if t.exists() and t.c % 4 == 3:
                    n, slot, uses = four(t)
                    sp.wait_ge(y_copied, t.count())
                    sp.dma_start(ys_v[n], y[:, slot, :, :]).then_inc(stored[slot], 16)
                t = i + 8
                if t.exists() and t.c % 4 == 0:
                    n, slot, uses = four(t)
                    if t.after(8):
                        sp.wait_ge(x_turned, t.count(less=5))
                    sp.dma_start(x[:, slot, :, :], xs_v[n]).then_inc(loaded[slot], 16)
            skewed(sp, step, 8, 1, kind)
            for s in stored:
                sp.wait_ge(s, 16 * kind.ALL // 8)

        @block.tensor
        def _(pe):
            def step(i):
                t = i + 3
                if t.exists():
                    n, slot, uses = four(t)
                    if t.c % 4 == 0:
                        pe.wait_ge(loaded[slot], uses * 16)
                    if t.after(2):
                        pe.wait_ge(x_copied, t.count(less=2))
                    nc.tensor.transpose(xt_ps[t.slot(2)][:, 0:P], x[:, slot, t.c % 4, :], k["ident"][:, :]).then_inc(x_turned, 1)
                t = i + 2
                if t.exists():
                    e = pe.value_load(expert_of[0:1, bass.ds(t.n, 1)], min_val=0, max_val=7)
                    pe.wait_ge(x_copied, t.count())
                    if t.after(2):
                        pe.wait_ge(h_ready, t.count(less=2))
                    nc.tensor.matmul(up_ps[t.slot(2)][:, :], xt[:, t.slot(2), :], w_up[:, bass.ds(e, 1), :], start=True, stop=True)\
                        .then_inc(up_ready, 1)
                t = i + 1
                if t.exists():
                    pe.wait_ge(h_ready, t.count())
                    if t.after(2):
                        pe.wait_ge(h_copied, t.count(less=2))
                    for c in range(FC):
                        tr = nc.tensor.transpose(ht_ps[t.slot(2)][:, c * P:(c + 1) * P], h[:, t.slot(2), c * P:(c + 1) * P], k["ident"][:, :])
                    tr.then_inc(h_turned, 1)
                t = i
                if t.exists():
                    e = pe.value_load(expert_of[0:1, bass.ds(t.n, 1)], min_val=0, max_val=7)
                    pe.wait_ge(h_copied, t.count())
                    if t.after(2):
                        pe.wait_ge(y_copied, t.count(less=2))
                    for c in range(FC):
                        mm = nc.tensor.matmul(y_ps[t.slot(2)][:, 0:D], ht[:, t.slot(2), c, :], w_down[:, bass.ds(e, 1), c, :],
                                              start=(c == 0), stop=(c == FC - 1))
                    mm.then_inc(down_ready, 1)
            skewed(pe, step, 3, 0, kind)

        @block.scalar
        def _(act):
            def step(i):
                t = i + 3
                if t.exists():
                    act.wait_ge(x_turned, t.count())
                    if t.after(2):
                        act.wait_ge(up_ready, t.count(less=2))
                    act.copy(xt[:, t.slot(2), :], xt_ps[t.slot(2)][:, 0:P]).then_inc(x_copied, 1)
                t = i + 2
                if t.exists() and top2:
                    act.wait_ge(up_ready, t.count())
                    if t.after(2):
                        act.wait_ge(h_ready, t.count(less=2))
                    act.activation(act1[:, t.slot(2), :], up_ps[t.slot(2)][:, 0:HID], ACT.Silu).then_inc(silu_ready, 1)
                t = i + 1
                if t.exists():
                    act.wait_ge(h_turned, t.count())
                    if t.after(2):
                        act.wait_ge(down_ready, t.count(less=2))
                    act.activation(ht[:, t.slot(2), :, :].rearrange("p c n -> p (c n)"), ht_ps[t.slot(2)][:, 0:HID],
                                   ACT.Copy if top2 else ACT.Relu).then_inc(h_copied, 1)
            skewed(act, step, 3, 0, kind)

        @block.vector
        def _(dve):
            def step(i):
                t = i + 2
                if t.exists():
                    s2 = t.slot(2)
                    e = None if top2 else dve.value_load(expert_of[0:1, bass.ds(t.n, 1)], min_val=0, max_val=7)
                    dve.wait_ge(silu_ready if top2 else up_ready, t.count())
                    if t.after(2):
                        dve.wait_ge(h_turned, t.count(less=2))
                    if top2:
                        dve.tensor_tensor(h[:, s2, :], up_ps[s2][:, HID:2 * HID], act1[:, s2, :], ALU.mult).then_inc(h_ready, 1)
                    else:
                        dve.tensor_tensor(h[:, s2, :], up_ps[s2][:, :], b_up[:, bass.ds(e, 1), :].rearrange("p a n -> p (a n)"), ALU.add)\
                            .then_inc(h_ready, 1)
                t = i
                if t.exists():
                    n, slot, uses = four(t)
                    e = None if top2 else dve.value_load(expert_of[0:1, bass.ds(t.n, 1)], min_val=0, max_val=7)
                    dve.wait_ge(down_ready, t.count())
                    if t.c % 4 == 0 and t.after(8):
                        dve.wait_ge(stored[slot], (uses - 1) * 16)
                    if top2:
                        dve.tensor_copy(y[:, slot, t.c % 4, :], y_ps[t.slot(2)][:, 0:D]).then_inc(y_copied, 1)
                    else:
                        dve.tensor_tensor(y[:, slot, t.c % 4, :], y_ps[t.slot(2)][:, 0:D],
                                          b_down[:, bass.ds(e, 1), :].rearrange("p a n -> p (a n)"), ALU.add).then_inc(y_copied, 1)
            skewed(dve, step, 3, 0, kind)


def combine(nc, stage, k, K, ys, dest, gate, x_all, x_out, gathered):
    with ExitStack() as ctx:
        mk = Maker(nc, ctx, stage + "_combine")
        sb, sem = mk.sb, mk.sem
        yg = sb("yg", [P, 2, 4, K, D])
        r1 = sb("r1", [P, 4, D])
        r = sb("r", [P, 2, 4, D])
        stats = sb("stats", [P, 4, 6])
        mv = sb("mv", [P, 2, 4, 2])
        ve = sb("ve", [P, 2, 4])
        rstd = sb("rstd", [P, 2, 4])
        out = sb("out", [P, 2, 4, D])
        earlier = 0 if K == 2 else 16 * 2 * NT // 2
        stored = [sem(f"stored{i}") for i in range(2)]
        partly, summed, stats_ready, mean_ready, var_ready, rstd_ready, normed, passed_dve = (
            sem(n) for n in ("partly", "summed", "stats_ready", "mean_ready", "var_ready", "rstd_ready", "normed", "passed_dve"))
        out_v = x_out.rearrange("(g n p) d -> g p n d", p=P, n=4)
        block = mk.block()

        @block.sync
        def _(sp):
            def step(i):
                if i.exists():
                    sp.wait_ge(normed, i.count())
                    sp.dma_start(out_v[i.n], out[:, i.slot(2), :, :]).then_inc(stored[i.slot(2)], 16)
            skewed(sp, step, 0, 0, Group)
            for s in stored:
                sp.wait_ge(s, 16 * NT // 8)

        @block.gpsimd
        def _(pool):
            for g in range(NT // 4 + 1):
                if g < NT // 4:
                    if g >= 2:
                        pool.wait_ge(summed, g - 1)
                    for n in range(4):
                        for r_ in range(K):
                            t = 4 * g + n
                            pool.indirect_dma_start(yg[:, g % 2, n, r_, :], None, ys, bass.IndirectOffsetOnAxis(ap=dest[:, r_, t:t + 1], axis=0))\
                                .then_inc(gathered[g % 2], 16)
                if g:
                    pool.wait_ge(var_ready, g)
                    if g > 2:
                        pool.wait_ge(normed, g - 2)
                    pool.tensor_tensor(rstd[:, (g - 1) % 2, :], ve[:, (g - 1) % 2, :], k["half"][:, :], ALU.pow).then_inc(rstd_ready, 1)

        @block.vector
        def _(dve):
            def step(i):
                t = i
                if t.exists():
                    s2 = t.slot(2)
                    dve.wait_ge(gathered[s2], t.uses(2) * 64 * K + earlier)
                    if t.after(2):
                        dve.wait_ge(normed, t.count(less=2))
                    if t.after(1) and K == 2:
                        dve.wait_ge(summed, t.count(less=1))
                    for m in range(K):
                        dst = r[:, s2, :, :] if m == K - 1 else r1[:, :, :]
                        src = r1 if m else None
                        for n in range(4):
                            tile = t.n * 4 + n
                            base = r1[:, n, :] if m else x_all[:, bass.ds(tile, 1), :].rearrange("p a d -> p (a d)")
                            st = dve.scalar_tensor_tensor(out=dst[:, n, :], in0=yg[:, s2, n, m, :], scalar=gate[:, m, bass.ds(tile, 1)],
                                                          in1=base, op0=ALU.mult, op1=ALU.add)
                        if m < K - 1:
                            st.then_inc(partly, 1)
                            dve.wait_ge(partly, t.count())
                    st.then_inc(summed, 1)
                    dve.wait_ge(summed, t.count())
                    if t.after(1):
                        dve.wait_ge(mean_ready, t.count(less=1))
                    for n in range(4):
                        bs = dve.bn_stats(stats[:, n, :], r[:, s2, n, :])
                    bs.then_inc(stats_ready, 1)
                    dve.wait_ge(stats_ready, t.count())
                    settle(dve, passed_dve)
                    for n in range(4):
                        ag = dve.bn_aggr(mv[:, s2, n, :], stats[:, n, :])
                    ag.then_inc(mean_ready, 1)
                    dve.wait_ge(mean_ready, t.count())
                    if t.after(2):
                        dve.wait_ge(rstd_ready, t.count(less=2))
                    dve.tensor_scalar(ve[:, s2, :], mv[:, s2, :, 1], LN_EPS, None, ALU.add).then_inc(var_ready, 1)
                t = i + -1
                if t.exists():
                    s2 = t.slot(2)
                    dve.wait_ge(rstd_ready, t.count())
                    if t.after(2):
                        dve.wait_ge(stored[s2], (t.uses(2) - 1) * 16)
                    for n in range(4):
                        no = dve.tensor_scalar(out[:, s2, n, :], r[:, s2, n, :], mv[:, s2, n, 0:1],
                                               rstd[:, s2, n:n + 1], ALU.subtract, ALU.mult)
                    no.then_inc(normed, 1)
            skewed(dve, step, 0, 1, Group)


KK, VV, PP = 0, S + 1, 2 * (S + 1)
ROW = 3 * (S + 1)
RMS_EPS, ETA_MIN = 1e-6, 1e-6
F = 64
N_MEM = float(F * D)


def memory_products(nc, stage, k, x_in, a, rows_out, k_all, v_all, qt_all, eta_col, w_out_t):
    with ExitStack() as ctx:
        mk = Maker(nc, ctx, stage)
        sb, ps, sem = mk.sb, mk.ps, mk.sem
        raw = sb("raw", [P, 4, D])
        w_all = sb("w_all", [P, 2 * F + D])
        w_norm = sb("w_norm", [P, 1])
        eta = sb("eta", [P, 1])
        eta_neg = sb("eta_neg", [P, 1])
        load_all(nc, stage, [(raw[0:F, 0, :], a["Wk"]), (raw[0:F, 1, :], a["Wq"]), (raw[:, 2, :], a["Wv"]), (raw[:, 3, :], a["Wout"]),
                             (w_norm[:, :], a["norm_weight"].rearrange("(d a) -> d a", a=1)),
                             (eta[0:F, :], a["eta"].rearrange("(f a) -> f a", a=1)),
                             (eta[F:P, :], a["eta"].rearrange("(f a) -> f a", a=1))])
        turn_blocks(nc, stage, k, [(raw[0:F, 0, :], w_all[:, 0:F]), (raw[0:F, 1, :], w_all[:, F:2 * F]), (raw[:, 2, :], w_all[:, 2 * F:]),
                                   (raw[:, 3, :], w_out_t)])
        x = sb("x", [P, 2, 4, D])
        sq = sb("sq", [P, D])
        ms = sb("ms", [P, 4, 1])
        mse = sb("mse", [P, 4, 1])
        rr = sb("rr", [P, 4, 1])
        xs = sb("xs", [P, 2, D])
        xt = sb("xt", [P, 2, P])
        low = sb("low", [P, 2, 2 * F])
        e = sb("e", [P, 2, 2 * F])
        kq = sb("kq", [P, 2, 2, F])
        q_bd = sb("q_bd", [P, 2, 2, F])
        own_batch = sb("own_batch", [P, 2])
        kt = sb("kt", [F, 2, P])
        ket = sb("ket", [F, 2, 2, S + 1])
        vt = sb("vt", [P, 2, 2, S + 1])
        row = sb("row", [P, 2, 4, ROW])
        t_ps, p_ps, vt_ps, k_ps, q_ps = (ps(n, [P, 512]) for n in ("t", "p", "vt", "k", "q"))
        g_ps = [ps(f"g{i}", [P, 512]) for i in range(2)]
        loaded = [sem(f"x_loaded{i}") for i in range(2)]
        stored = [sem(f"stored{i}") for i in range(2)]
        (eta_ready, squares, mse_ready, rr_ready, xs_ready, xt_ready, xt_copied, proj_ready, low_ready, e_ready, kq_ready,
         k_kept, q_spread, k_turned, q_turned, k_copied, q_copied, ke_ready, v_copied, vt_copied, g_ready, row_copied, row_ready) = (
            sem(n) for n in ("eta_ready", "squares", "mse_ready", "rr_ready", "xs_ready", "xt_ready", "xt_copied", "proj_ready",
                             "low_ready", "e_ready", "kq_ready", "k_kept", "q_spread", "k_turned",
                             "q_turned", "k_copied", "q_copied", "ke_ready", "v_copied",
                             "vt_copied", "g_ready", "row_copied", "row_ready"))
        x_v = x_in.rearrange("(g n p) d -> g p n d", p=P, n=4)
        rows_v = rows_out.rearrange("(g n p) r -> g p n r", p=P, n=4)
        passed_pe = sem("passed_pe")
        kind = Eights
        block = mk.block()

        @block.sync
        def _(sp):
            def step(i):
                t = i + -1
                if t.exists() and t.c % 4 == 3:
                    n, slot, uses = four(t)
                    sp.wait_ge(row_ready, t.count())
                    sp.wait_ge(row_copied, t.count())
                    sp.dma_start(rows_v[n], row[:, slot, :, :]).then_inc(stored[slot], 16)
                t = i + 11
                if t.exists() and t.c % 4 == 0:
                    n, slot, uses = four(t)
                    if t.after(8):
                        sp.wait_ge(xs_ready, t.count(less=5))
                    sp.dma_start(x[:, slot, :, :], x_v[n]).then_inc(loaded[slot], 16)
            skewed(sp, step, 11, 1, kind)
            for s in stored:
                sp.wait_ge(s, 16 * NT // 8)

        @block.gpsimd
        def _(pool):
            def step(i):
                t = i
                if t.exists():
                    s2 = t.slot(2)
                    pool.wait_ge(kq_ready, t.count())
                    if t.after(2):
                        pool.wait_ge(q_turned, t.count(less=2))
                    pool.tensor_tensor(q_bd[:, s2, :, :], kq[:, s2, 1:2, :].to_broadcast([P, 2, F]),
                                       own_batch[:, :].unsqueeze(2).to_broadcast([P, 2, F]), ALU.mult).then_inc(q_spread, 1)
                    pool.tensor_copy(k_all[:, bass.ds(t.n, 1), :], kq[:, s2, 0:1, :]).then_inc(k_kept, 1)
                t = i + 4
                if t.exists():
                    pool.wait_ge(mse_ready, t.count())
                    if t.after(4):
                        pool.wait_ge(xs_ready, t.count(less=4))
                    pool.tensor_tensor(rr[:, t.slot(4), :], mse[:, t.slot(4), :], k["half"][:, 0:1], ALU.pow).then_inc(rr_ready, 1)
            pool.wait_ge(eta_ready, 7)
            skewed(pool, step, 4, 0, kind)

        @block.tensor
        def _(pe):
            def step(i):
                t = i
                if t.exists():
                    pe.wait_ge(kq_ready, t.count())
                    if t.after(1):
                        pe.wait_ge(ke_ready, t.count(less=1))
                    settle(pe, passed_pe)
                    nc.tensor.transpose(k_ps[0:F, 0:P], kq[:, t.slot(2), 0, :], k["ident"][:, :]).then_inc(k_turned, 1)
                t = i + 2
                if t.exists():
                    pe.wait_ge(xs_ready, t.count())
                    if t.after(1):
                        pe.wait_ge(xt_copied, t.count(less=1))
                    nc.tensor.transpose(t_ps[:, 0:P], xs[:, t.slot(2), :], k["ident"][:, :]).then_inc(xt_ready, 1)
                t = i + 1
                if t.exists():
                    s2 = t.slot(2)
                    pe.wait_ge(xt_copied, t.count())
                    if t.after(1):
                        pe.wait_ge(kq_ready, t.count(less=1))
                        pe.wait_ge(vt_copied, t.count(less=1))
                        pe.wait_ge(v_copied, t.count(less=1))
                    nc.tensor.matmul(p_ps[:, 0:2 * F], xt[:, s2, :], w_all[:, 0:2 * F], start=True, stop=True)
                    nc.tensor.matmul(vt_ps[:, P:P + D], xt[:, s2, :], w_all[:, 2 * F:], start=True, stop=True)
                    nc.tensor.matmul(vt_ps[:, 0:P], w_all[:, 2 * F:], xt[:, s2, :], start=True, stop=True).then_inc(proj_ready, 1)
                t = i
                if t.exists():
                    pe.wait_ge(q_spread, t.count())
                    if t.after(1):
                        pe.wait_ge(q_copied, t.count(less=1))
                    nc.tensor.transpose(q_ps[:, 0:P], q_bd[:, t.slot(2), :, :], k["ident"][:, :]).then_inc(q_turned, 1)
                t = i
                if t.exists():
                    s2 = t.slot(2)
                    pe.wait_ge(k_copied, t.count())
                    pe.wait_ge(ke_ready, t.count())
                    pe.wait_ge(vt_copied, t.count())
                    if t.after(2):
                        pe.wait_ge(row_ready, t.count(less=2))
                        pe.wait_ge(row_copied, t.count(less=2))
                    settle(pe, passed_pe)
                    for n in range(3):
                        for b in range(2):
                            rows = slice(b * S, (b + 1) * S)
                            lhs, rhs = ((kt[:, s2, rows], ket[:, s2, b, :]), (vt[:, s2, b, 0:S], vt[:, s2, b, :]),
                                        (ket[:, s2, b, 0:S], ket[:, s2, b, :]))[n]
                            mm = nc.tensor.matmul(g_ps[s2][rows, n * (S + 1):(n + 1) * (S + 1)], lhs, rhs, start=True, stop=True)
                    mm.then_inc(g_ready, 1)
            pe.wait_ge(eta_ready, 5)
            skewed(pe, step, 3, 0, kind)

        @block.scalar
        def _(act):
            def step(i):
                t = i
                if t.exists():
                    act.wait_ge(k_turned, t.count())
                    if t.after(2):
                        act.wait_ge(g_ready, t.count(less=2))
                    act.copy(kt[:, t.slot(2), :], k_ps[0:F, 0:P]).then_inc(k_copied, 1)
                t = i + 2
                if t.exists():
                    act.wait_ge(xt_ready, t.count())
                    if t.after(2):
                        act.wait_ge(proj_ready, t.count(less=2))
                    act.mul(xt[:, t.slot(2), :], t_ps[:, 0:P], w_norm[:, 0:1]).then_inc(xt_copied, 1)
                t = i + 1
                if t.exists():
                    s2 = t.slot(2)
                    act.wait_ge(proj_ready, t.count())
                    if t.after(2):
                        act.wait_ge(g_ready, t.count(less=2))
                    act.copy(vt[:, s2, :, 0:S], vt_ps[:, 0:P].rearrange("p (b s) -> p b s", b=2)).then_inc(vt_copied, 1)
                    act.wait_ge(low_ready, t.count())
                    if t.after(2):
                        act.wait_ge(kq_ready, t.count(less=2))
                    act.activation(e[:, s2, :], low[:, s2, :], ACT.Exp).then_inc(e_ready, 1)
                    act.copy(v_all[:, bass.ds(t.n, 1), :], vt_ps[:, P:P + D]).then_inc(v_copied, 1)
                t = i
                if t.exists():
                    act.wait_ge(q_turned, t.count())
                    act.copy(qt_all[:, bass.ds(t.n, 1), :], q_ps[:, 0:P]).then_inc(q_copied, 1)
            act.wait_ge(eta_ready, 5)
            skewed(act, step, 3, 0, kind)

        @block.vector
        def _(dve):
            dve.memset(vt[:, :, :, :], 1.0).then_inc(eta_ready, 1)
            dve.memset(ket[:, :, :, :], 1.0).then_inc(eta_ready, 1)
            dve.memset(own_batch[:, :], 0.0).then_inc(eta_ready, 1)
            dve.tensor_scalar(eta_neg[:, :], eta[:, :], -1.0, None, ALU.mult).then_inc(eta_ready, 1)
            dve.wait_ge(eta_ready, 4)
            dve.tensor_scalar(eta_col, eta[:, :], eta_neg[:, :], ETA_MIN, ALU.max, ALU.max).then_inc(eta_ready, 1)
            dve.wait_ge(eta_ready, 5)
            for b in range(2):
                dve.memset(own_batch[b * S:(b + 1) * S, b:b + 1], 1.0).then_inc(eta_ready, 1)

            def step(i):
                t = i + -1
                if t.exists():
                    n, slot, uses = four(t)
                    s2 = t.slot(2)
                    dve.wait_ge(g_ready, t.count())
                    if t.c % 4 == 0 and t.after(8):
                        dve.wait_ge(stored[slot], (uses - 1) * 16)
                    dst = row[:, slot, t.c % 4, :]
                    dve.tensor_copy(dst[:, 0:PP], g_ps[s2][:, 0:PP]).then_inc(row_copied, 1)
                    dve.wait_ge(row_copied, t.count())
                    dve.tensor_tensor(dst[:, PP:ROW], g_ps[s2][:, PP:ROW], dst[:, VV:PP], ALU.mult).then_inc(row_ready, 1)
                t = i
                if t.exists():
                    dve.wait_ge(k_copied, t.count())
                    if t.after(2):
                        dve.wait_ge(g_ready, t.count(less=2))
                    dve.tensor_scalar(ket[:, t.slot(2), :, 0:S], k_ps[0:F, 0:P].rearrange("p (b s) -> p b s", b=2),
                                      eta_col[0:F, :], None, ALU.mult).then_inc(ke_ready, 1)
                t = i + 4
                if t.exists():
                    n, slot, uses = four(t)
                    s4 = t.slot(4)
                    if t.c % 4 == 0:
                        dve.wait_ge(loaded[slot], uses * 16)
                    if t.after(1):
                        dve.wait_ge(squares, t.count(less=1))
                    dve.tensor_tensor_reduce(out=sq[:, :], in0=x[:, slot, t.c % 4, :], in1=x[:, slot, t.c % 4, :], scale=1.0 / D, scalar=0.0,
                                             op0=ALU.mult, op1=ALU.add, accum_out=ms[:, s4, :]).then_inc(squares, 1)
                t = i + 3
                if t.exists():
                    n, slot, uses = four(t)
                    s4 = t.slot(4)
                    dve.wait_ge(rr_ready, t.count())
                    if t.after(2):
                        dve.wait_ge(xt_ready, t.count(less=2))
                    dve.tensor_scalar(xs[:, t.slot(2), :], x[:, slot, t.c % 4, :], rr[:, s4, :], None, ALU.mult).then_inc(xs_ready, 1)
                t = i + 4
                if t.exists():
                    s4 = t.slot(4)
                    dve.wait_ge(squares, t.count())
                    if t.after(4):
                        dve.wait_ge(rr_ready, t.count(less=4))
                    dve.tensor_scalar(mse[:, s4, :], ms[:, s4, :], RMS_EPS, None, ALU.add).then_inc(mse_ready, 1)
                t = i + 1
                if t.exists():
                    dve.wait_ge(proj_ready, t.count())
                    if t.after(2):
                        dve.wait_ge(e_ready, t.count(less=2))
                    dve.tensor_scalar(low[:, t.slot(2), :], p_ps[:, 0:2 * F], 0.0, None, ALU.min).then_inc(low_ready, 1)
                t = i + 1
                if t.exists():
                    dve.wait_ge(e_ready, t.count())
                    if t.after(2):
                        dve.wait_ge(k_turned, t.count(less=2))
                        dve.wait_ge(k_kept, t.count(less=2))
                    dve.scalar_tensor_tensor(out=kq[:, t.slot(2), :, :], in0=p_ps[:, 0:2 * F].rearrange("p (a f) -> p a f", a=2), scalar=0.0,
                                             in1=e[:, t.slot(2), :].rearrange("p (a f) -> p a f", a=2), op0=ALU.max, op1=ALU.add).then_inc(kq_ready, 1)
            skewed(dve, step, 4, 1, kind)


def memory_recurrence(nc, stage, k, rows_in, coef, offset):
    with ExitStack() as ctx:
        mk = Maker(nc, ctx, stage)
        sb, sem = mk.sb, mk.sem
        g = sb("g", [P, S, ROW])
        w = sb("w", [P, S, S])
        prod = sb("prod", [P, S * S // 4])
        junk = sb("junk", [P, 3, S])
        quad = sb("quad", [P, S])
        part = sb("part", [P, 4, S])
        sv_neg2, p_n, p2, dd = (sb(n, [P, S]) for n in ("sv_neg2", "p_n", "p2", "dd"))
        v = {n: sb(n, [P, 1]) for n in ("mo", "m2", "pm", "q1", "a2", "i2", "gg", "h", "r2", "r2c", "y", "ry", "s2", "s", "h2", "nv", "ve",
                                        "z", "rz", "u", "u2", "rho", "mo2")}
        v = {n: t[:, :] for n, t in v.items()}
        N_CHUNK = 4
        loaded = [sem(f"rows_loaded{i}") for i in range(N_CHUNK)]
        link_sem, root_asked, root_ready = sem("steps"), sem("root_asked"), sem("root_ready")
        kk = lambda t, s: g[:, t, s]
        rows_v = rows_in.rearrange("(b t) r -> b t r", t=S)
        block = mk.block()

        @block.sync
        def _(sp):
            n = S // N_CHUNK
            for i in range(N_CHUNK):
                sp.dma_start(g[:, i * n:(i + 1) * n, :], rows_v[:, i * n:(i + 1) * n, :]).then_inc(loaded[i], 16)

        @block.scalar
        def _(act):
            for t in range(S):
                act.wait_ge(root_asked, 2 * t + 1)
                act.activation(v["y"], v["r2c"], ACT.Sqrt).then_inc(root_ready, 1)
                act.wait_ge(root_asked, 2 * t + 2)
                act.activation(v["z"], v["ve"], ACT.Sqrt).then_inc(root_ready, 1)

        @block.vector
        def _(dve):
            done = [0]

            def link(ins):
                done[0] += 1
                ins.then_inc(link_sem, 1)
                dve.wait_ge(link_sem, done[0])

            ts, stt, tt, ttr = dve.tensor_scalar, dve.scalar_tensor_tensor, dve.tensor_tensor, dve.tensor_tensor_reduce
            for s in loaded:
                dve.wait_ge(s, 16)
            ksum, pp, sv = (g[:, :, n + S] for n in (KK, PP, VV))
            link(ts(sv_neg2[:, :], sv, -2.0, None, ALU.mult))
            link(ts(p_n[:, :], pp, -1.0 / N_MEM, None, ALU.mult))
            link(ts(p2[:, :], pp, 2.0, None, ALU.mult))
            link(tt(dd[:, :], p_n[:, :], pp, ALU.mult))
            for t in range(S):
                last = tt(dd[:, t:t + 1], dd[:, t:t + 1], g[:, t, PP + t:PP + t + 1], ALU.add)
            link(last)
            link(dve.memset(quad[:, :], 0.0))
            link(dve.memset(v["mo"], 0.0))
            link(dve.memset(v["m2"], 0.0))
            for t in range(S):
                col = slice(t, t + 1)
                rest = S - 1 - t
                vv_tt = g[:, t, VV + t:VV + t + 1]
                if t:
                    link(ttr(out=junk[:, 0, 0:t], in0=w[:, t, 0:t], in1=g[:, t, VV:VV + t], scale=-2.0, scalar=quad[:, col],
                             op0=ALU.mult, op1=ALU.add, accum_out=v["q1"]))
                    link(ttr(out=junk[:, 1, 0:t], in0=w[:, t, 0:t], in1=sv[:, 0:t], scale=2.0, scalar=sv_neg2[:, col],
                             op0=ALU.mult, op1=ALU.add, accum_out=v["a2"]))
                    link(ts(v["gg"], v["mo"], ksum[:, col], None, ALU.mult))
                    link(stt(out=v["h"], in0=v["gg"], scalar=float(D), in1=v["a2"], op0=ALU.mult, op1=ALU.add))
                    link(stt(out=v["r2"], in0=v["h"], scalar=v["gg"], in1=v["q1"], op0=ALU.mult, op1=ALU.add))
                    ask = ts(v["r2c"], v["r2"], vv_tt, 1e-30, ALU.add, ALU.max)
                else:
                    ask = ts(v["r2c"], vv_tt, 1e-30, None, ALU.max)
                ask.then_inc(root_asked, 1)
                if t:
                    link(ts(v["pm"], p2[:, col], v["mo"], None, ALU.mult))
                    link(ttr(out=junk[:, 2, 0:t], in0=coef[:, 0:t], in1=g[:, t, PP:PP + t], scale=2.0, scalar=v["pm"],
                             op0=ALU.mult, op1=ALU.add, accum_out=v["i2"]))
                else:
                    link(dve.memset(v["i2"], 0.0))
                if t and rest:
                    pr = prod[:, 0:rest * t].rearrange("p (a b) -> p a b", b=t)
                    link(tt(pr, w[:, t + 1:S, 0:t], g[:, t:t + 1, VV:VV + t].to_broadcast([P, rest, t]), ALU.mult))
                    link(dve.tensor_reduce(part[:, 0, 0:rest], pr, AX, ALU.add))
                dve.wait_ge(root_ready, 2 * t + 1)
                link(dve.reciprocal(v["ry"], v["y"]))
                link(stt(out=v["s2"], in0=v["ry"], scalar=v["r2c"], in1=v["y"], op0=ALU.mult, op1=ALU.add))
                link(ts(v["s"], v["s2"], 0.5, None, ALU.mult))
                link(stt(out=v["h2"], in0=v["s"], scalar=dd[:, col], in1=v["i2"], op0=ALU.mult, op1=ALU.add))
                link(stt(out=v["nv"], in0=v["h2"], scalar=v["s"], in1=v["m2"], op0=ALU.mult, op1=ALU.add))
                ts(v["ve"], v["nv"], 1.0 / N_MEM, LN_EPS, ALU.mult, ALU.add).then_inc(root_asked, 1)
                link(dve.tensor_copy(coef[:, col], v["s"]))
                link(stt(out=v["mo2"], in0=v["s"], scalar=p_n[:, col], in1=v["mo"], op0=ALU.mult, op1=ALU.add))
                if rest:
                    nxt = w[:, t + 1:S, t]
                    link(ts(nxt, g[:, t + 1:S, t], v["s"], None, ALU.mult))
                    link(ts(part[:, 1, 0:rest], nxt, vv_tt, None, ALU.mult))
                    if t:
                        link(stt(out=part[:, 2, 0:rest], in0=part[:, 0, 0:rest], scalar=2.0, in1=part[:, 1, 0:rest],
                                 op0=ALU.mult, op1=ALU.add))
                    link(tt(part[:, 3, 0:rest], part[:, 2 if t else 1, 0:rest], nxt, ALU.mult))
                    link(tt(quad[:, t + 1:S], quad[:, t + 1:S], part[:, 3, 0:rest], ALU.add))
                dve.wait_ge(root_ready, 2 * t + 2)
                dve.wait_ge(root_asked, 2 * t + 2)
                link(dve.reciprocal(v["rz"], v["z"]))
                link(ts(v["u"], v["rz"], v["rz"], v["ve"], ALU.mult, ALU.mult))
                link(ts(v["u2"], v["u"], -0.5, 1.5, ALU.mult, ALU.add))
                link(ts(v["rho"], v["u2"], v["rz"], None, ALU.mult))
                ts(v["m2"], v["nv"], v["rho"], v["rho"], ALU.mult, ALU.mult)
                ts(v["mo"], v["mo2"], v["rho"], None, ALU.mult)
                last = ts(coef[:, 0:t + 1], coef[:, 0:t + 1], v["rho"], None, ALU.mult)
                if rest:
                    ts(quad[:, t + 1:S], quad[:, t + 1:S], v["rho"], v["rho"], ALU.mult, ALU.mult)
                    last = ts(w[:, t + 1:S, 0:t + 1], w[:, t + 1:S, 0:t + 1], v["rho"], None, ALU.mult)
                link(last)
            dve.tensor_copy(offset, v["mo"]).then_inc(link_sem, 1)


def memory_and_mixer(nc, stage, k, x_in, ctx_in, k_all, v_all, qt_all, eta_col, w_out_t, coef, offset, x_out):
    with ExitStack() as ctx:
        mk = Maker(nc, ctx, stage)
        sb, ps, sem = mk.sb, mk.ps, mk.sem
        coef_t = sb("coef_t", [P, 2, NT])
        mine = sb("mine", [P, 2, NT])
        off_in = sb("off_in", [P, 2, NT])
        ones64 = sb("ones64", [P, F])
        off = sb("off", [P, NT])
        kc_bd = sb("kc_bd", [P, 2, 2, F])
        x = sb("x", [P, 2, 4, D])
        c = sb("c", [P, 2, 4, D])
        mem = sb("mem", [P, 2, D])
        read = sb("read", [P, 2, P])
        xm = sb("xm", [P, 4, D])
        xct = sb("xct", [P, 2, 2, P])
        g_bd = sb("g_bd", [P, 2, 2, S])
        r = [sb(f"r{n}", [P, 2, D]) for n in range(2)]
        stats = [sb(f"stats{n}", [P, 6]) for n in range(2)]
        mv = [sb(f"mv{n}", [P, 2, 2]) for n in range(2)]
        ve = [sb(f"ve{n}", [P, 2, 1]) for n in range(2)]
        rstd = [sb(f"rstd{n}", [P, 2, 1]) for n in range(2)]
        y = sb("y", [P, 2, 4, D])
        m_ps, read_ps, out_ps, turn_ps, h_ps, mix_ps = (ps(n, [P, 512]) for n in ("m", "read", "out", "turn", "h", "mix"))
        (zeroed, mine_set, off_set, setup_ps, setup_copied, kc_ready, m_ready, m_copied, read_ready, read_copied, out_ready, turned, turn_copied,
         h_ready, g_ready, mix_ready) = (
            sem(n) for n in ("zeroed", "mine_set", "off_set", "setup_ps", "setup_copied", "kc_ready", "m_ready", "m_copied", "read_ready", "read_copied",
                             "out_ready", "turned", "turn_copied", "h_ready", "g_ready", "mix_ready"))
        summed, stats_ready, mean_ready, var_ready, rstd_ready, normed = (
            [sem(f"{n}{j}") for j in range(2)] for n in ("summed", "stats_ready", "mean_ready", "var_ready", "rstd_ready", "normed"))
        passed_dve, passed_pe, passed_pool = sem("passed_dve"), sem("passed_pe"), sem("passed_pool")
        x_loaded = [sem(f"x_loaded{i}") for i in range(2)]
        c_loaded = [sem(f"c_loaded{i}") for i in range(2)]
        stored = [sem(f"stored{i}") for i in range(2)]
        x_v, c_v, out_v = (t.rearrange("(g n p) d -> g p n d", p=P, n=4) for t in (x_in, ctx_in, x_out))
        block = mk.block()

        @block.sync
        def _(sp):
            def step(i):
                t = i + -1
                if t.exists() and t.c % 4 == 3:
                    n, slot, uses = four(t)
                    sp.wait_ge(normed[1], t.count())
                    sp.dma_start(out_v[n], y[:, slot, :, :]).then_inc(stored[slot], 16)
                t = i + 8
                if t.exists() and t.c % 4 == 0:
                    n, slot, uses = four(t)
                    if t.after(8):
                        sp.wait_ge(summed[0], t.count(less=5))
                    sp.dma_start(x[:, slot, :, :], x_v[n]).then_inc(x_loaded[slot], 16)
                t = i + 4
                if t.exists() and t.c % 4 == 0:
                    n, slot, uses = four(t)
                    if t.after(8):
                        sp.wait_ge(mix_ready, t.count(less=5))
                    sp.dma_start(c[:, slot, :, :], c_v[n]).then_inc(c_loaded[slot], 16)
            skewed(sp, step, 8, 1, Eights)
            for n in range(2):
                sp.wait_ge(stored[n], 16 * NT // 8)

        @block.gpsimd
        def _(pool):
            pool.memset(mine[:, :, :], 0.0).then_inc(mine_set, 1)
            pool.wait_ge(mine_set, 1)
            pool.affine_select(out=mine[:, :, :], in_=mine[:, :, :], compare_op=ALU.not_equal, fill=1.0, base=0,
                               pattern=[[-1, 2], [-2, NT]], channel_multiplier=1).then_inc(mine_set, 1)

            pool.wait_ge(setup_copied, 2)

            def step(i):
                t = i + 6
                if t.exists():
                    s2 = t.slot(2)
                    if t.after(2):
                        pool.wait_ge(m_ready, t.count(less=2))
                    settle(pool, passed_pool)
                    pool.tensor_tensor(kc_bd[:, s2, :, :], k_all[:, bass.ds(t.n, 1), :].to_broadcast([P, 2, F]),
                                       coef_t[:, :, bass.ds(t.n, 1)].to_broadcast([P, 2, F]), ALU.mult).then_inc(kc_ready, 1)
                for n, t in ((0, i + 3), (1, i)):
                    if t.exists():
                        s2 = t.slot(2)
                        pool.wait_ge(var_ready[n], t.count())
                        if t.after(2):
                            pool.wait_ge(normed[n], t.count(less=2))
                        pool.tensor_tensor(rstd[n][:, s2, :], ve[n][:, s2, :], k["half"][:, 0:1], ALU.pow).then_inc(rstd_ready[n], 1)
            skewed(pool, step, 6, 1, Eights)

        @block.tensor
        def _(pe):
            pe.wait_ge(zeroed, 3)
            pe.wait_ge(off_set, 1)
            pe.wait_ge(mine_set, 2)
            for b in range(2):
                nc.tensor.matmul(m_ps[b * S:(b + 1) * S, 0:NT], coef[:, :], mine[:, b, :], start=True, stop=True)
            for b in range(2):
                mm = nc.tensor.matmul(h_ps[b * S:(b + 1) * S, 0:NT], ones64[:, :], off_in[:, b, :], start=True, stop=True)
            mm.then_inc(setup_ps, 1)
            pe.wait_ge(setup_copied, 2)

            def step(i):
                t = i + 3
                if t.exists():
                    pe.wait_ge(read_copied, t.count())
                    if t.after(1):
                        pe.wait_ge(summed[0], t.count(less=1))
                    nc.tensor.matmul(out_ps[:, 0:D], read[:, t.slot(2), :], w_out_t, start=True, stop=True).then_inc(out_ready, 1)
                t = i + 1
                if t.exists():
                    pe.wait_ge(turn_copied, t.count())
                    if t.after(1):
                        pe.wait_ge(g_ready, t.count(less=1))
                    nc.tensor.matmul(h_ps[:, 0:P], xct[:, t.slot(2), 1, :], xct[:, t.slot(2), 0, :], start=True, stop=True).then_inc(h_ready, 1)
                t = i + 5
                if t.exists():
                    s2 = t.slot(2)
                    pe.wait_ge(kc_ready, t.count())
                    if t.after(1):
                        pe.wait_ge(m_copied, t.count(less=1))
                    settle(pe, passed_pe)
                    nc.tensor.matmul(m_ps[:, 0:D], kc_bd[:, s2, :, :], v_all[:, bass.ds(t.n, 1), :], start=True, stop=True).then_inc(m_ready, 1)
                t = i
                if t.exists():
                    n, slot, uses = four(t)
                    pe.wait_ge(g_ready, t.count())
                    if t.after(1):
                        pe.wait_ge(summed[1], t.count(less=1))
                    nc.tensor.matmul(mix_ps[:, 0:D], g_bd[:, t.slot(2), :, :], c[:, slot, t.c % 4, :], start=True, stop=True).then_inc(mix_ready, 1)
                t = i + 4
                if t.exists():
                    pe.wait_ge(m_copied, t.count())
                    if t.after(1):
                        pe.wait_ge(read_copied, t.count(less=1))
                    settle(pe, passed_pe)
                    nc.tensor.matmul(read_ps[:, 0:P], mem[:, t.slot(2), :], qt_all[:, bass.ds(t.n, 1), :], start=True, stop=True)\
                        .then_inc(read_ready, 1)
                t = i + 2
                if t.exists():
                    n, slot, uses = four(t)
                    if t.c % 4 == 0:
                        pe.wait_ge(c_loaded[slot], uses * 16)
                    pe.wait_ge(normed[0], t.count())
                    if t.after(1):
                        pe.wait_ge(turn_copied, t.count(less=1))
                    nc.tensor.transpose(turn_ps[:, P:2 * P], c[:, slot, t.c % 4, :], k["ident"][:, :])
                    nc.tensor.transpose(turn_ps[:, 0:P], xm[:, t.slot(4), :], k["ident"][:, :]).then_inc(turned, 1)
            skewed(pe, step, 6, 0, Eights)

        @block.scalar
        def _(act):
            act.wait_ge(setup_ps, 1)
            act.wait_ge(zeroed, 3)
            for b in range(2):
                rows = slice(b * S, (b + 1) * S)
                cp = act.copy(coef_t[rows, b, :], m_ps[rows, 0:NT])
            cp.then_inc(setup_copied, 1)
            act.copy(off[:, :], h_ps[:, 0:NT]).then_inc(setup_copied, 1)
            act.wait_ge(setup_copied, 2)

            def step(i):
                t = i + 1
                if t.exists():
                    act.wait_ge(h_ready, t.count())
                    if t.after(2):
                        act.wait_ge(mix_ready, t.count(less=2))
                    for b in range(2):
                        rows = slice(b * S, (b + 1) * S)
                        ge = act.activation(g_bd[rows, t.slot(2), b, :], h_ps[rows, rows], ACT.Gelu_apprx_tanh)
                    ge.then_inc(g_ready, 1)
                t = i + 5
                if t.exists():
                    act.wait_ge(m_ready, t.count())
                    if t.after(2):
                        act.wait_ge(read_ready, t.count(less=2))
                    act.activation(mem[:, t.slot(2), :], m_ps[:, 0:D], ACT.Identity, scale=eta_col,
                                   bias=off[:, bass.ds(t.n, 1)]).then_inc(m_copied, 1)
                t = i + 4
                if t.exists():
                    act.wait_ge(read_ready, t.count())
                    if t.after(2):
                        act.wait_ge(out_ready, t.count(less=2))
                    act.copy(read[:, t.slot(2), :], read_ps[:, 0:P]).then_inc(read_copied, 1)
                t = i + 2
                if t.exists():
                    act.wait_ge(turned, t.count())
                    if t.after(2):
                        act.wait_ge(h_ready, t.count(less=2))
                    act.copy(xct[:, t.slot(2), :, :], turn_ps[:, 0:2 * P].rearrange("p (a n) -> p a n", a=2)).then_inc(turn_copied, 1)
            skewed(act, step, 6, 0, Eights)

        @block.vector
        def _(dve):
            dve.memset(coef_t[:, :, :], 0.0).then_inc(zeroed, 1)
            dve.memset(g_bd[:, :, :, :], 0.0).then_inc(zeroed, 1)
            dve.memset(ones64[:, :], 1.0).then_inc(zeroed, 1)
            dve.wait_ge(mine_set, 2)
            dve.tensor_scalar(off_in[:, :, :], mine[:, :, :], offset, None, ALU.mult).then_inc(off_set, 1)
            dve.wait_ge(setup_copied, 2)

            def add_norm(n, t, res, src):
                s2 = t.slot(2)
                if t.after(2):
                    dve.wait_ge(normed[n], t.count(less=2))
                dve.scalar_tensor_tensor(out=r[n][:, s2, :], in0=res, scalar=2.0 if n == 0 else 1.0, in1=src, op0=ALU.mult, op1=ALU.add)\
                    .then_inc(summed[n], 1)
                dve.wait_ge(summed[n], t.count())
                dve.bn_stats(stats[n][:, :], r[n][:, s2, :]).then_inc(stats_ready[n], 1)
                dve.wait_ge(stats_ready[n], t.count())
                settle(dve, passed_dve)
                dve.bn_aggr(mv[n][:, s2, :], stats[n][:, :]).then_inc(mean_ready[n], 1)
                dve.wait_ge(mean_ready[n], t.count())
                if t.after(2):
                    dve.wait_ge(rstd_ready[n], t.count(less=2))
                dve.tensor_scalar(ve[n][:, s2, :], mv[n][:, s2, 1:2], LN_EPS, None, ALU.add).then_inc(var_ready[n], 1)

            def norm(n, t, dst):
                s2 = t.slot(2)
                dve.wait_ge(rstd_ready[n], t.count())
                dve.tensor_scalar(dst, r[n][:, s2, :], mv[n][:, s2, 0:1], rstd[n][:, s2, :], ALU.subtract, ALU.mult)\
                    .then_inc(normed[n], 1)

            def step(i):
                t = i + 2
                if t.exists():
                    if t.after(4):
                        dve.wait_ge(summed[1], t.count(less=4))
                    norm(0, t, xm[:, t.slot(4), :])
                t = i + 3
                if t.exists():
                    dve.wait_ge(out_ready, t.count())
                    n, slot, uses = four(t)
                    dve.wait_ge(x_loaded[slot], uses * 16)
                    add_norm(0, t, x[:, slot, t.c % 4, :], out_ps[:, 0:D])
                t = i + -1
                if t.exists():
                    n, slot, uses = four(t)
                    if t.c % 4 == 0 and t.after(8):
                        dve.wait_ge(stored[slot], (uses - 1) * 16)
                    norm(1, t, y[:, slot, t.c % 4, :])
                t = i
                if t.exists():
                    dve.wait_ge(mix_ready, t.count())
                    add_norm(1, t, xm[:, t.slot(4), :], mix_ps[:, 0:D])
            skewed(dve, step, 6, 1, Eights)


def build(nc, a, out):
    flat = lambda t: t.rearrange("b s d -> (b s) d")
    x1 = nc.dram_tensor("x1", (B * S, D), F32, kind="Internal").ap()
    x2 = nc.dram_tensor("x2", (B * S, D), F32, kind="Internal").ap()
    with ExitStack() as ctx:
        k = constants(nc, Maker(nc, ctx, "k"))
        xs = nc.dram_tensor("tokens_by_expert", (Sorted2.ALL * P, D), F32, kind="Internal").ap()
        ys = nc.dram_tensor("expert_outputs", (Sorted2.ALL * P, D), F32, kind="Internal").ap()
        mk = Maker(nc, ctx, "experts")
        pool_dmas = [mk.sem("scattered"), [mk.sem("gathered0"), mk.sem("gathered1")]]
        xs_filled = fill(nc, Maker(nc, ctx, "fill"), xs)
        wqkv, bqkv = a["L0_attn_W_qkv"], a["L0_attn_b_qkv"]
        w = {"wo": a["L0_attn_W_o"], "bo": a["L0_attn_b_o"]}
        for n, name in enumerate("qkv"):
            w["w" + name], w["b" + name] = wqkv[n * D:(n + 1) * D, :], bqkv[n * D:(n + 1) * D]
        attention(nc, "self", k, flat(a["x"]), None, None, w, x1)
        w = {m + name: a[f"L0_xattn_{m.upper() if m == 'w' else m}{name}"] for m in "wb" for name in "qkvo"}
        mask = a["mask_Bx1x1xS2_if1"].rearrange("b u v s -> (b u v) s")
        attention(nc, "cross", k, x1, flat(a["ctx_1024"]), mask, w, x2)
        ffn = {n: a["L0_ffn_" + n] for n in ("Wg", "W1", "W2", "W3")}
        experts(nc, "ffn0", k, x2, ffn, x1, True, xs, ys, xs_filled, pool_dmas)
        mem = {n: a["L1_attn_" + n] for n in ("norm_weight", "Wk", "Wv", "Wq", "eta", "Wout")}
        rows = nc.dram_tensor("memory_rows", (B * S, ROW), F32, kind="Internal").ap()
        with ExitStack() as mem_ctx:
            mm = Maker(nc, mem_ctx, "mem_state")
            w_out_t, coef, offset, eta = mm.sb("w_out_t", [P, D]), mm.sb("coef", [P, S]), mm.sb("offset", [P, 1]), mm.sb("eta", [P, 1])
            k_all, v_all, qt_all = mm.sb("k_all", [P, NT, F]), mm.sb("v_all", [P, NT, D]), mm.sb("qt_all", [P, NT, P])
            memory_products(nc, "products", k, x1, mem, rows, k_all, v_all, qt_all, eta[:, :], w_out_t[:, :])
            memory_recurrence(nc, "recur", k, rows, coef, offset[:, :])
            memory_and_mixer(nc, "mixer", k, x1, flat(a["ctx_1024"]), k_all, v_all, qt_all, eta[:, :], w_out_t[:, :], coef, offset[:, :], x2)
        ffn = {n: a["L1_ffn_" + n] for n in ("Wr", "br", "W1", "b1", "W2", "b2")}
        experts(nc, "ffn1", k, x2, ffn, flat(out), False, xs, ys, xs_filled, pool_dmas)


INPUTS = ["x", "ctx_1024", "mask_Bx1x1xS2_if1",
          "L0_attn_W_qkv", "L0_attn_b_qkv", "L0_attn_W_o", "L0_attn_b_o",
          "L0_xattn_Wq", "L0_xattn_bq", "L0_xattn_Wk", "L0_xattn_bk", "L0_xattn_Wv", "L0_xattn_bv",
          "L0_xattn_Wo", "L0_xattn_bo",
          "L0_ffn_Wg", "L0_ffn_W1", "L0_ffn_W2", "L0_ffn_W3",
          "L1_attn_norm_weight", "L1_attn_Wk", "L1_attn_Wv", "L1_attn_Wq", "L1_attn_eta", "L1_attn_Wout",
          "L1_ffn_Wr", "L1_ffn_br", "L1_ffn_W1", "L1_ffn_b1", "L1_ffn_W2", "L1_ffn_b2"]


def kernel(**inputs):
    import numpy as _np
    import concourse.bacc as _bacc
    from concourse.bass_utils import run_bass_kernel_spmd as _run

    nc = _bacc.Bacc("TRN2", target_bir_lowering=False, num_devices=1)
    arrays, aps = {}, {}
    for name in INPUTS:
        v = _np.ascontiguousarray(inputs[name])
        arrays[f"in_{name}"] = v
        aps[name] = nc.dram_tensor(f"in_{name}", v.shape, mybir.dt.from_np(v.dtype), kind="ExternalInput").ap()
    out = nc.dram_tensor("decoded", (B, S, D), F32, kind="ExternalOutput").ap()
    build(nc, aps, out)
    r = _run(nc, [arrays], core_ids=[0])
    return r.results[0]["decoded"]
```

```python
from contextlib import ExitStack

import concourse.bass as bass
from concourse import mybir

F32 = mybir.dt.float32
BF16 = mybir.dt.bfloat16
I32 = mybir.dt.int32
U32 = mybir.dt.uint32
ALU = mybir.AluOpType
ACT = mybir.ActivationFunctionType
AX = mybir.AxisListType.X

P = 128
B, S, D = 128, 64, 128
NT = B * S // P
HALF = NT // 2
NH, HD = 16, 8
UNROLL = 4
NEG = -1.0e30
LN_EPS = 1e-5


class Tile:
    BODY, ALL = UNROLL, NT

    def __init__(self, j, c):
        self.j, self.c = j, c

    def __add__(self, k):
        return type(self)(self.j, self.c + k)

    def count(self, per=1, less=0):
        k = (self.c + 1 - less) * per
        return k if self.static else self.j * (self.BODY * per) + k

    @property
    def static(self):
        return isinstance(self.j, int)

    @property
    def n(self):
        return self.c if self.static else self.j * self.BODY + self.c

    def slot(self, n):
        return self.c % n

    def uses(self, n):
        k = self.c // n + 1
        return k if self.static else self.j * (self.BODY // n) + k

    def exists(self):
        return not self.static or 0 <= self.c < self.ALL

    def after(self, k):
        return not self.static or self.c >= k


class Group(Tile):
    BODY, ALL = 2, NT // 4


class Quad(Group):
    BODY = 4


class Sorted1(Tile):
    BODY, ALL = 8, NT + 16


class Sorted2(Sorted1):
    ALL = 2 * NT + 16


class Eights(Tile):
    BODY = 8


def four(t):
    g = t.c // 4
    return (g if t.static else t.j * 2 + g), g % 2, (g // 2 + 1 if t.static else t.j + (g // 2 + 1))


def skewed(eng, step, before, after, kind=Tile, peeled=4, pause=None):
    first = max(1, peeled // kind.BODY)
    for c in range(-before, first * kind.BODY):
        step(kind(0, c))
    last = kind.ALL // kind.BODY - -(-before // kind.BODY)
    middle = pause[0] // kind.BODY if pause else last
    for begin, end in ((first, middle), (middle, last)):
        if begin < end:
            with eng.Fori(begin, end) as j:
                for c in range(kind.BODY):
                    step(kind(j, c))
        if pause and end == middle:
            pause[1]()
    for c in range(last * kind.BODY, kind.ALL + after):
        step(kind(0, c))


class Maker:

    def __init__(self, nc, ctx, stage):
        self.nc, self.ctx, self.stage = nc, ctx, stage
        self.sems = []

    def sb(self, name, shape, dt=F32):
        return self.ctx.enter_context(self.nc.sbuf_tensor(f"{self.stage}_{name}", shape, dt))

    def ps(self, name, shape, dt=F32):
        return self.ctx.enter_context(self.nc.psum_tensor(f"{self.stage}_{name}_ps", shape, dt))

    def sem(self, name):
        self.sems.append(self.ctx.enter_context(self.nc.semaphore(f"{self.stage}_{name}")))
        return self.sems[-1]

    def block(self):
        self.ctx.callback(self.zero)
        return self.ctx.enter_context(self.nc.Block())

    def zero(self):
        with self.nc.Block() as block:

            @block.sync
            def _(sp):
                for s in self.sems:
                    sp.sem_clear(s)


def settle(eng, passed):
    eng.sem_inc(passed, 1)


def constants(nc, mk):
    k = {
        "ident": mk.sb("ident", [P, P]),
        "ident_bf": mk.sb("ident_bf", [P, P], BF16),
        "head_mask": mk.sb("head_mask", [P, 8]),
        "head_mask2": mk.sb("head_mask2", [P, 2, 8]),
        "causal": mk.sb("causal", [P, 8, S], BF16),
        "pick": mk.sb("pick", [2, 2, S], BF16),
        "ones": mk.sb("ones", [1, P]),
        "half": mk.sb("half", [P, 4]),
    }
    cleared, stamped, drawn = mk.sem("cleared"), mk.sem("stamped"), mk.sem("drawn")
    with nc.Block() as block:

        @block.gpsimd
        def _(pool):
            for n, v in (("ident", 0.0), ("ident_bf", 0.0), ("pick", 0.0), ("causal", 0.0),
                         ("head_mask2", 1.0), ("ones", 1.0), ("half", -0.5)):
                pool.memset(k[n][tuple(slice(None) for _ in k[n].shape)], v).then_inc(cleared, 1)
            pool.wait_ge(cleared, 7)
            for m in (k["ident"], k["ident_bf"]):
                pool.affine_select(out=m[:, :], in_=m[:, :], compare_op=ALU.not_equal, fill=1.0,
                                   base=0, pattern=[[-1, P]], channel_multiplier=1).then_inc(stamped, 1)
            pool.affine_select(out=k["pick"][:, :, :], in_=k["pick"][:, :, :], compare_op=ALU.not_equal,
                               fill=1.0, base=0, pattern=[[-1, 2], [0, S]], channel_multiplier=1)\
                .then_inc(stamped, 1)
            for b in range(2):
                rows = k["causal"][b * S:(b + 1) * S, :, :]
                pool.wait_ge(stamped, 3 + b)
                pool.affine_select(out=rows, in_=rows, compare_op=ALU.is_ge, fill=NEG, base=0,
                                   pattern=[[0, 8], [-1, S]], channel_multiplier=1).then_inc(stamped, 1)
            m = k["head_mask2"][:, :, :]
            pool.wait_ge(stamped, 5)
            pool.affine_select(out=m, in_=m, compare_op=ALU.is_ge, fill=0.0, base=0,
                               pattern=[[-S, 2], [-HD, 8]], channel_multiplier=1).then_inc(stamped, 1)
            pool.wait_ge(stamped, 6)
            pool.affine_select(out=m, in_=m, compare_op=ALU.is_ge, fill=0.0, base=HD - 1,
                               pattern=[[S, 2], [HD, 8]], channel_multiplier=-1).then_inc(stamped, 1)
            pool.wait_ge(stamped, 7)
            pool.tensor_tensor(k["head_mask"][:, :], k["head_mask2"][:, 0, :], k["head_mask2"][:, 1, :],
                               ALU.add).then_inc(drawn, 1)
    return k


def zeros_for(nc, mk, xs):
    zeros = mk.sb("zeros", [P, D])
    zeros_set, filled = mk.sem("zeros_set"), mk.sem("xs_filled")
    with nc.Block() as block:

        @block.vector
        def _(dve):
            dve.memset(zeros[:, :], 0.0).then_inc(zeros_set, 1)
    return {"zeros": zeros, "set": zeros_set, "filled": filled, "xs": [half.rearrange("(n p) d -> n p d", p=P) for half in xs]}


def attention(nc, stage, k, x_in, ctx_in, mask_in, w, x_out, fill=None):
    cross = ctx_in is not None
    scale = float(HD) ** -0.5
    with ExitStack() as ctx:
        mk = Maker(nc, ctx, stage)
        sb, ps, sem = mk.sb, mk.ps, mk.sem
        w_raw = sb("w_raw", [P, 4, P])
        w_t = sb("w_t", [P, 4, P])
        b_row = sb("b_row", [1, P])
        b_cols = sb("b_cols", [P, 2, 2])
        bv_col = sb("bv_col", [P, 1])
        bo_all = sb("bo_all", [P, P])
        x = sb("x", [P, 2, P])
        c = sb("c", [P, 2, P])
        xr = sb("xr", [P, 2, P])
        xt = sb("xt", [P, 2, P])
        ct = sb("ct", [P, 2, P])
        q_bd = sb("q_bd", [P, 2, 2, 2, S])
        kt = sb("kt", [P, 2, 2, S])
        k_ex = sb("k_ex", [P, 2, 2, 8, S])
        v_bd = sb("v_bd", [P, 4, 8, 2, 18])
        prob = sb("prob", [P, 2, NH, S])
        prob_t = sb("prob_t", [P, 8, P])
        top = sb("top", [P, 2, NH])
        rden = sb("rden", [P, 8, 2])
        o = sb("o", [P, 8, 2, HD])
        ot = sb("ot", [P, P])
        r = sb("r", [P, 2, P])
        stats = sb("stats", [P, 6])
        mv = sb("mv", [P, 2, 2])
        ve = sb("ve", [P, 2, 1])
        rstd = sb("rstd", [P, 2, 1])
        y = sb("y", [P, 2, P])
        mask_i = sb("mask_i", [2, NT, S], I32)
        mask_n = sb("mask_n", [2, NT, S], BF16)

        s_ps = [ps(f"s_ps{i}", [P, NH, S]) for i in range(2)]
        pt_ps = [ps(f"pt_ps{i}", [P, 4, P]) for i in range(2)]
        front = ps("front", [P, 512])
        back = ps("back", [P, 512])
        fq = front[:, 0:128]
        fk = front[:, 128:256]
        fv = front[:, 256:384].rearrange("p (b n) -> p b n", b=2)
        pv = back[:, 0:288].rearrange("p (a b n) -> p a b n", a=8, b=2)
        b_ot, b_y = (back[:, n * P:(n + 1) * P] for n in (2, 3))
        b_xt, b_ct = (front[:, n * P:(n + 1) * P] for n in (0, 1))

        weights_in, w_psum, w_ready, bo_psum = sem("weights_in"), sem("w_psum"), sem("w_ready"), sem("bo_psum")
        zeroed, mask_ready = sem("zeroed"), sem("mask_ready")
        x_in_sem = [sem(f"x_loaded{i}") for i in range(2)]
        c_in_sem = [sem(f"ctx_loaded{i}") for i in range(2)]
        xr_in_sem = [sem(f"residual_loaded{i}") for i in range(2)]
        stored = [sem(f"stored{i}") for i in range(2)]
        xt_ready, xt_copied = sem("xt_ready"), sem("xt_copied")
        qkv_ready, q_copied, k_copied, v_copied = sem("qkv_ready"), sem("q_copied"), sem("k_copied"), sem("v_copied")
        keys_expanded, s_ready, top_ready, shifted = sem("keys_expanded"), sem("s_ready"), sem("top_ready"), sem("shifted")
        probs_ready, pt_ready, pt_copied, pv_ready = sem("probs_ready"), sem("pt_ready"), sem("pt_copied"), sem("pv_ready")
        inverse_ready, o_ready, ot_ready, ot_copied = sem("inverse_ready"), sem("o_ready"), sem("ot_ready"), sem("ot_copied")
        y_ready, residual_biased, summed, stats_ready = sem("y_ready"), sem("residual_biased"), sem("summed"), sem("stats_ready")
        mean_ready, var_ready, rstd_ready, y_normed = sem("mean_ready"), sem("var_ready"), sem("rstd_ready"), sem("y_normed")

        passed_dve = sem("passed_dve")

        names = ("q", "k", "v", "o")
        x_v = x_in.rearrange("(n p) d -> n p d", p=P)
        c_v = ctx_in.rearrange("(n p) d -> n p d", p=P) if cross else None
        out_v = x_out.rearrange("(n p) d -> n p d", p=P)
        n_weight_dmas = 14

        block = mk.block()

        @block.sync
        def _(sp):
            for n, name in enumerate(names):
                dst = w_t if cross else w_raw
                sp.dma_start(dst[:, n, :], w["w" + name]).then_inc(weights_in, 16)
            sp.dma_start(b_row[:, :], w["bo"].rearrange("(a n) -> a n", a=1)).then_inc(weights_in, 16)
            for n, name in enumerate(("q", "k")):
                for b in range(2):
                    for h in range(2):
                        sp.dma_start(b_cols[b * S:(b + 1) * S, n, h:h + 1],
                                     w["b" + name][h * S:(h + 1) * S].rearrange("(f a) -> f a", a=1)).then_inc(weights_in, 16)
            sp.dma_start(bv_col[:, :], w["bv"].rearrange("(n a) -> n a", a=1)).then_inc(weights_in, 16)
            if cross:
                sp.dma_start(mask_i[:, :, :], mask_in.rearrange("(i b) s -> b i s", b=2)).then_inc(mask_ready, 16)

            if fill:
                sp.wait_ge(fill["set"], 1)

            def step(i):
                t = i
                if t.exists() and fill:
                    for half in fill["xs"]:
                        sp.dma_start(half[t.n], fill["zeros"][:, :]).then_inc(fill["filled"], 16)
                if t.exists():
                    if t.after(2):
                        sp.wait_ge(summed, t.count(less=2))
                    sp.dma_start(xr[:, t.slot(2), :], x_v[t.n]).then_inc(xr_in_sem[t.slot(2)], 16)
                t = i + -3
                if t.exists():
                    sp.wait_ge(y_normed, t.count())
                    sp.dma_start(out_v[t.n], y[:, t.slot(2), :]).then_inc(stored[t.slot(2)], 16)
                t = i + 6
                if t.exists():
                    if t.after(2):
                        sp.wait_ge(xt_ready, t.count(less=2))
                    sp.dma_start(x[:, t.slot(2), :], x_v[t.n]).then_inc(x_in_sem[t.slot(2)], 16)
                    if cross:
                        sp.dma_start(c[:, t.slot(2), :], c_v[t.n]).then_inc(c_in_sem[t.slot(2)], 16)
            skewed(sp, step, 6, 3, peeled=8)
            if fill:
                for n in range(NT, Sorted2.ALL // 2):
                    for half in fill["xs"]:
                        sp.dma_start(half[n], fill["zeros"][:, :]).then_inc(fill["filled"], 16)
            for n in range(2):
                sp.wait_ge(stored[n], 16 * NT // 2)

        @block.gpsimd
        def _(pool):
            def step(i):
                t = i + -1
                if t.exists():
                    pool.wait_ge(xr_in_sem[t.slot(2)], t.uses(2) * 16)
                    pool.tensor_tensor(xr[:, t.slot(2), :], xr[:, t.slot(2), :], bo_all[:, :], ALU.add)\
                        .then_inc(residual_biased, 1)
                t = i + -2
                if t.exists():
                    pool.wait_ge(var_ready, t.count())
                    if t.after(2):
                        pool.wait_ge(y_normed, t.count(less=2))
                    pool.tensor_tensor(rstd[:, t.slot(2), :], ve[:, t.slot(2), :], k["half"][:, 0:1], ALU.pow)\
                        .then_inc(rstd_ready, 1)
                t = i + 3
                if t.exists():
                    pool.wait_ge(k_copied, t.count())
                    if t.after(2):
                        pool.wait_ge(s_ready, t.count(less=2))
                    for h in range(2):
                        ex = pool.tensor_tensor(
                            k_ex[:, t.slot(2), h, :, :],
                            kt[:, t.slot(2), h:h + 1, :].to_broadcast([P, 8, S]),
                            k["head_mask"][:, :].unsqueeze(2).to_broadcast([P, 8, S]), ALU.mult)
                        ex.then_inc(keys_expanded, 1)
            pool.wait_ge(w_ready, 2)
            skewed(pool, step, 4, 2, peeled=8)

        @block.tensor
        def _(pe):
            pe.wait_ge(weights_in, 16 * n_weight_dmas)
            if not cross:
                for n in range(4):
                    wt = nc.tensor.transpose(front[:, n * P:(n + 1) * P], w_raw[:, n, :], k["ident"][:, :])
                wt.then_inc(w_psum, 1)
            nc.tensor.matmul(back[:, 0:P], k["ones"][:, :], b_row[:, :], start=True, stop=True).then_inc(bo_psum, 1)
            pe.wait_ge(w_ready, 2)

            def step(i):
                t = i + -1
                if t.exists():
                    pe.wait_ge(pt_copied, t.count(2))
                    if t.after(1):
                        pe.wait_ge(summed, t.count(less=1))
                    for n in range(8):
                        mm = nc.tensor.matmul(pv[:, n, :, :], prob_t[:, n, :], v_bd[:, t.slot(4), n, :, :], start=True, stop=True)
                    mm.then_inc(pv_ready, 1)
                t = i
                if t.exists():
                    pe.wait_ge(probs_ready, t.count())
                    for h in range(2):
                        if t.after(1):
                            pe.wait_ge(pt_copied, t.count(2, less=1))
                        for n in range(4):
                            a = 2 * (4 * h + n)
                            tr = nc.tensor.transpose(pt_ps[h][:, n, :], prob[:, t.slot(2), a:a + 2, :], k["ident"][:, :])
                        tr.then_inc(pt_ready, 1)
                t = i + 2
                if t.exists():
                    pe.wait_ge(keys_expanded, t.count(2) - 1)
                    pe.wait_ge(q_copied, t.count())
                    if t.after(2):
                        pe.wait_ge(shifted, t.count(less=2))
                    if cross:
                        pe.wait_ge(mask_ready, 17)
                    h = 0
                    dst = s_ps[t.slot(2)][:, 8 * h:8 * h + 8, :]
                    nc.tensor.matmul(dst, q_bd[:, t.slot(2), h, :, :], k_ex[:, t.slot(2), h, :, :], start=True, stop=False)
                    if cross:
                        mm = nc.tensor.matmul(dst, k["pick"][:, :, :], mask_n[:, bass.ds(t.n, 1), :].to_broadcast([2, 8, S]),
                                              start=False, stop=True)
                    else:
                        mm = nc.tensor.matmul(dst, k["ident_bf"][:, :], k["causal"][:, :, :], start=False, stop=True)
                t = i + 4
                if t.exists():
                    pe.wait_ge(x_in_sem[t.slot(2)], t.uses(2) * 16)
                    if t.after(1):
                        pe.wait_ge(xt_copied, t.count(less=1))
                    if t.after(2):
                        pe.wait_ge(q_copied, t.count(less=2))
                        pe.wait_ge(v_copied, t.count(less=2))
                    tr = nc.tensor.transpose(b_xt, x[:, t.slot(2), :], k["ident"][:, :])
                    if cross:
                        pe.wait_ge(c_in_sem[t.slot(2)], t.uses(2) * 16)
                        tr = nc.tensor.transpose(b_ct, c[:, t.slot(2), :], k["ident"][:, :])
                    tr.then_inc(xt_ready, 1)
                t = i + -1
                if t.exists():
                    pe.wait_ge(o_ready, t.count())
                    nc.tensor.transpose(b_ot, o[:, :, :, :], k["ident"][:, :]).then_inc(ot_ready, 1)
                t = i + 2
                if t.exists():
                    h = 1
                    pe.wait_ge(keys_expanded, t.count(2))
                    dst = s_ps[t.slot(2)][:, 8 * h:8 * h + 8, :]
                    nc.tensor.matmul(dst, q_bd[:, t.slot(2), h, :, :], k_ex[:, t.slot(2), h, :, :], start=True, stop=False)
                    if cross:
                        mm = nc.tensor.matmul(dst, k["pick"][:, :, :], mask_n[:, bass.ds(t.n, 1), :].to_broadcast([2, 8, S]),
                                              start=False, stop=True)
                    else:
                        mm = nc.tensor.matmul(dst, k["ident_bf"][:, :], k["causal"][:, :, :], start=False, stop=True)
                    mm.then_inc(s_ready, 1)
                t = i + -1
                if t.exists():
                    pe.wait_ge(ot_copied, t.count())
                    nc.tensor.matmul(b_y, ot[:, :], w_t[:, 3, :], start=True, stop=True).then_inc(y_ready, 1)
                t = i + 3
                if t.exists():
                    u = t + 1
                    pe.wait_ge(xt_copied, u.count() if u.exists() else NT)
                    if t.after(1):
                        pe.wait_ge(q_copied, t.count(less=1))
                        pe.wait_ge(v_copied, t.count(less=1))
                    xq = xt[:, t.slot(2), :]
                    xk = ct[:, t.slot(2), :] if cross else xq
                    for n, (src, dst) in enumerate(((xq, fq), (xk, fk))):
                        for h in range(2):
                            for b in range(2):
                                part = dst[b * S:(b + 1) * S, h * S:(h + 1) * S]
                                nc.tensor.matmul(part, w_t[:, n, h * S:(h + 1) * S], src[:, b * S:(b + 1) * S], start=True, stop=True)
                    wv = w_t[:, 2, :].rearrange("p (a h d) -> p a h d", h=2, d=HD)
                    for b in range(2):
                        for h in range(2):
                            mm = nc.tensor.matmul(fv[h * S:(h + 1) * S, b, :], xk[:, b * S:(b + 1) * S], wv[:, :, h, :], start=True, stop=True)
                    mm.then_inc(qkv_ready, 1)
            skewed(pe, step, 4, 1, peeled=8)

        @block.scalar
        def _(act):
            act.wait_ge(bo_psum, 1)
            if not cross:
                act.wait_ge(w_psum, 1)
                act.copy(w_t[:, :, :], front[:, :].rearrange("p (a n) -> p a n", a=4)).then_inc(w_ready, 1)
            else:
                act.copy(bo_all[:, 0:1], back[:, 0:1]).then_inc(w_ready, 1)
            act.wait_ge(w_ready, 1)
            act.copy(bo_all[:, :], back[:, 0:P]).then_inc(w_ready, 1)
            act.wait_ge(zeroed, 3)
            act.wait_ge(w_ready, 2)

            def step(i):
                t = i + 1
                if t.exists():
                    act.wait_ge(shifted, t.count())
                    act.activation(prob[:, t.slot(2), :, :], prob[:, t.slot(2), :, :], ACT.Exp, scale=scale)\
                        .then_inc(probs_ready, 1)
                t = i
                if t.exists():
                    for h in range(2):
                        act.wait_ge(pt_ready, t.count(2) - 1 + h)
                        if t.after(1):
                            act.wait_ge(pv_ready, t.count(less=1))
                        act.copy(prob_t[:, 4 * h:4 * h + 4, :], pt_ps[h][:, :, :]).then_inc(pt_copied, 1)
                t = i + 4
                if t.exists():
                    act.wait_ge(xt_ready, t.count())
                    if t.after(2):
                        act.wait_ge(qkv_ready, t.count(less=2))
                    cp = act.copy(xt[:, t.slot(2), :], b_xt)
                    if cross:
                        cp = act.copy(ct[:, t.slot(2), :], b_ct)
                    cp.then_inc(xt_copied, 1)
                t = i + -1
                if t.exists():
                    act.wait_ge(ot_ready, t.count())
                    if t.after(1):
                        act.wait_ge(y_ready, t.count(less=1))
                    act.activation(ot[:, :], b_ot, ACT.Identity, bias=bv_col[:, 0:1]).then_inc(ot_copied, 1)
                t = i + 3
                if t.exists():
                    act.wait_ge(qkv_ready, t.count())
                    if t.after(2):
                        act.wait_ge(keys_expanded, t.count(2, less=2))
                    for h in range(2):
                        cp = act.activation(kt[:, t.slot(2), h, :], fk[:, h * S:(h + 1) * S], ACT.Identity, bias=b_cols[:, 1, h:h + 1])
                    cp.then_inc(k_copied, 1)
                    if t.after(2):
                        act.wait_ge(s_ready, t.count(less=2))
                    for b in range(2):
                        rows = slice(b * S, (b + 1) * S)
                        for h in range(2):
                            cp = act.activation(q_bd[rows, t.slot(2), h, b, :], fq[rows, h * S:(h + 1) * S], ACT.Identity,
                                                bias=b_cols[rows, 0, h:h + 1])
                    cp.then_inc(q_copied, 1)
                    if t.after(4):
                        act.wait_ge(pv_ready, t.count(less=4))
                    for h in range(2):
                        rows = slice(h * S, (h + 1) * S)
                        cp = act.copy(v_bd[rows, t.slot(4), :, :, HD * h:HD * h + HD].rearrange("p a b d -> p b a d"),
                                      fv[rows, :, :].rearrange("p b (a d) -> p b a d", d=HD))
                    cp.then_inc(v_copied, 1)
            skewed(act, step, 4, 1, peeled=8)

        @block.vector
        def _(dve):
            dve.memset(q_bd[:, :, :, :, :], 0.0).then_inc(zeroed, 1)
            dve.memset(v_bd[:, :, :, :, :], 0.0).then_inc(zeroed, 1)
            dve.wait_ge(zeroed, 2)
            for h in range(2):
                one = dve.memset(v_bd[h * S:(h + 1) * S, :, :, :, 16 + h:17 + h], 1.0)
            one.then_inc(zeroed, 1)
            if cross:
                dve.wait_ge(mask_ready, 16)
                dve.tensor_scalar(mask_n[:, :, :], mask_i[:, :, :], 0.0, NEG, ALU.is_equal, ALU.mult).then_inc(mask_ready, 1)

            def step(i):
                t = i + -1
                if t.exists():
                    dve.wait_ge(pv_ready, t.count())
                    if t.after(1):
                        dve.wait_ge(o_ready, t.count(less=1))
                    for b in range(2):
                        rows = slice(b * S, (b + 1) * S)
                        rc = dve.reciprocal(rden[rows, :, :], pv[rows, :, b, 16:18])
                    rc.then_inc(inverse_ready, 1)
                    dve.wait_ge(inverse_ready, t.count())
                    if t.after(1):
                        dve.wait_ge(ot_ready, t.count(less=1))
                    for b in range(2):
                        rows = slice(b * S, (b + 1) * S)
                        mu = dve.tensor_tensor(o[rows, :, :, :], pv[rows, :, b, 0:16].rearrange("p a (h d) -> p a h d", h=2),
                                               rden[rows, :, :].unsqueeze(3).to_broadcast([S, 8, 2, HD]), ALU.mult)
                    mu.then_inc(o_ready, 1)
                t = i + -2
                if t.exists():
                    dve.wait_ge(summed, t.count())
                    dve.bn_stats(stats[:, :], r[:, t.slot(2), :]).then_inc(stats_ready, 1)
                    dve.wait_ge(stats_ready, t.count())
                    settle(dve, passed_dve)
                    dve.bn_aggr(mv[:, t.slot(2), :], stats[:, :]).then_inc(mean_ready, 1)
                    dve.wait_ge(mean_ready, t.count())
                    if t.after(2):
                        dve.wait_ge(rstd_ready, t.count(less=2))
                    dve.tensor_scalar(ve[:, t.slot(2), :], mv[:, t.slot(2), 1:2], LN_EPS, None, ALU.add).then_inc(var_ready, 1)
                t = i + -3
                if t.exists():
                    dve.wait_ge(rstd_ready, t.count())
                    if t.after(2):
                        dve.wait_ge(stored[t.slot(2)], (t.uses(2) - 1) * 16)
                    dve.tensor_scalar(y[:, t.slot(2), :], r[:, t.slot(2), :], mv[:, t.slot(2), 0:1], rstd[:, t.slot(2), :],
                                      ALU.subtract, ALU.mult).then_inc(y_normed, 1)
                t = i + -1
                if t.exists():
                    dve.wait_ge(y_ready, t.count())
                    dve.wait_ge(residual_biased, t.count())
                    if t.after(2):
                        dve.wait_ge(y_normed, t.count(less=2))
                    dve.tensor_tensor(r[:, t.slot(2), :], b_y, xr[:, t.slot(2), :], ALU.add).then_inc(summed, 1)
                t = i + 2
                if t.exists():
                    dve.wait_ge(s_ready, t.count())
                    if t.after(2):
                        dve.wait_ge(shifted, t.count(less=2))
                    dve.tensor_reduce(top[:, t.slot(2), :], s_ps[t.slot(2)][:, :, :], AX, ALU.max).then_inc(top_ready, 1)
                    dve.wait_ge(top_ready, t.count())
                    if t.after(2):
                        dve.wait_ge(pt_ready, t.count(2, less=2))
                    dve.tensor_tensor(prob[:, t.slot(2), :, :], s_ps[t.slot(2)][:, :, :],
                                      top[:, t.slot(2), :].unsqueeze(2).to_broadcast([P, NH, S]), ALU.subtract)\
                        .then_inc(shifted, 1)
            skewed(dve, step, 4, 3, peeled=8)


def turn_blocks(nc, stage, k, blocks):
    with ExitStack() as ctx:
        mk = Maker(nc, ctx, stage + "_turn")
        banks = [mk.ps(f"bank{i}", [P, 4, P]) for i in range(4)]
        turned, copied = mk.sem("turned"), mk.sem("copied")
        block = mk.block()

        @block.tensor
        def _(pe):
            for n, (src, dst) in enumerate(blocks):
                if n >= 4:
                    pe.wait_ge(copied, n - 3)
                rows, cols = src.shape
                nc.tensor.transpose(banks[n % 4][0:cols, 0, 0:rows], src, k["ident"][0:rows, 0:rows]).then_inc(turned, 1)

        @block.scalar
        def _(act):
            for n, (src, dst) in enumerate(blocks):
                rows, cols = src.shape
                act.wait_ge(turned, n + 1)
                act.copy(dst, banks[n % 4][0:cols, 0, 0:rows]).then_inc(copied, 1)


def load_all(nc, stage, pairs):
    with ExitStack() as ctx:
        mk = Maker(nc, ctx, stage + "_load")
        loaded = mk.sem("loaded")
        block = mk.block()

        @block.sync
        def _(sp):
            for dst, src in pairs:
                sp.dma_start(dst, src).then_inc(loaded, 16)
            sp.wait_ge(loaded, 16 * len(pairs))


def link_to(eng, sem):
    done = [0]

    def link(ins):
        done[0] += 1
        ins.then_inc(sem, 1)
        eng.wait_ge(sem, done[0])
    return link


def experts(nc, stage, k, x_in, a, x_out, top2, xs, ys, xs_filled, pool_dmas):
    E = 8
    K = 2 if top2 else 1
    FC = 2 if top2 else 4
    kind = Sorted2 if top2 else Sorted1
    T = kind.ALL
    H = 512
    with ExitStack() as ctx:
        mk = Maker(nc, ctx, stage)
        sb = mk.sb
        w_up = sb("w_up", [P, E, H])
        w_down = sb("w_down", [P, E, FC, P])
        x_all = sb("x_all", [P, NT, D])
        dest = sb("dest", [P, K, NT], U32)
        source = sb("source", [P, K, NT], U32)
        yg = sb("yg", [P, NT, K, D])
        gate = sb("gate", [P, K, NT])
        expert_of = sb("expert_of", [1, T], I32)
        b_up = None if top2 else sb("b_up", [P, E, H])
        b_down = None if top2 else sb("b_down", [P, E, D])
        route(nc, stage, k, x_in, a, top2, xs, xs_filled, pool_dmas[0], T, w_up, w_down, b_up, b_down, x_all, dest, source,
              gate, expert_of)
        run_experts(nc, stage, k, top2, kind, xs, ys, w_up, w_down, b_up, b_down, expert_of, x_all, dest, source, yg, pool_dmas)
        combine(nc, stage, k, K, ys, source, gate, x_all, yg, x_out, pool_dmas[2])


def route(nc, stage, k, x_in, a, top2, xs, xs_filled, scattered, T, w_up, w_down, b_up, b_down, x_all, dest, source,
          gate, expert_of):
    E, K, FC, H = 8, 2 if top2 else 1, 2 if top2 else 4, 512
    with ExitStack() as ctx:
        mk = Maker(nc, ctx, stage + "_route")
        sb, ps, sem = mk.sb, mk.ps, mk.sem
        w_gate = sb("w_gate", [P, E])
        b_gate = None if top2 else sb("b_gate", [P, E])
        raw = {n: sb("raw_" + n, [P, E, FC, P]) for n in ("W1", "W2", "W3")} if top2 else {}
        raw_gate = sb("raw_gate", [E, P]) if top2 else None
        x = sb("x", [P, 4, 4, D])
        xt = sb("xt", [P, 2, 4, P])
        before = sb("before", [P, P], BF16)
        all_ones = sb("all_ones", [P, P], BF16)
        order = sb("order", [P, E])
        steps128 = sb("steps128", [P, HALF])
        tile_no = sb("tile_no", [1, T // 2])
        big = {n: sb(n, [P, NT, E]) for n in ("logit", "shifted", "ex", "rest", "equal", "ranked", "pos", "even", "odd", "total")}
        sel = sb("sel", [P, K, NT, E])
        sel_bf = sb("sel_bf", [P, NT, E], BF16)
        mx = sb("mx", [P, 3, NT])
        first = sb("first", [P, NT])
        small = {n: sb(n, [P, NT]) for n in ("diff", "e2", "z", "rz")}
        fits = sb("fits", [P, 2, E, HALF])
        ends = [sb(f"ends{i}", [P, 2, E]) for i in range(2)]
        n_tiles = sb("n_tiles", [P, 2, E])
        base = sb("base", [P, 2, E])
        dest_f = sb("dest_f", [P, K, NT])
        source_f = sb("source_f", [P, K, NT])
        passed = sb("passed", [1, T, E])
        expert_f = sb("expert_f", [1, 2, T])
        turn_ps = [ps(f"turn{i}", [P, 4, P]) for i in range(2)]
        logits_ps = ps("logits", [P, NT, E])
        before_ps, total_ps = ps("before", [P, NT, E]), ps("total", [P, NT, E])
        earlier = 0 if top2 else 16 * 2 * NT
        weights_in, gate_in, made = sem("weights_in"), sem("gate_in"), sem("made")
        loaded = [sem(f"x_loaded{i}") for i in range(4)]
        x_kept, xt_ready, xt_copied, logits_ready = sem("x_kept"), sem("xt_ready"), sem("xt_copied"), sem("logits_ready")
        gate_turned, gate_copied = sem("gate_turned"), sem("gate_copied")
        exp_asked, exp_ready, selected, counted = sem("exp_asked"), sem("exp_ready"), sem("selected"), sem("counted")
        routed, link_sem = sem("routed"), sem("chain")
        w_turned, w_copied = sem("w_turned"), sem("w_copied")
        x_v = x_in.rearrange("(g n p) d -> g p n d", p=P, n=4)
        blocks = []
        if top2:
            up_v = w_up[:, :, :].rearrange("p e (s c n) -> p e s c n", s=2, n=P)
            for e in range(E):
                for c in range(FC):
                    blocks += [(raw["W1"][:, e, c, :], up_v[:, e, 0, c, :]), (raw["W2"][:, e, c, :], up_v[:, e, 1, c, :]),
                               (raw["W3"][:, e, c, :], w_down[:, e, c, :])]
        block = mk.block()

        @block.sync
        def _(sp):
            if top2:
                sp.dma_start(raw_gate[:, :], a["Wg"]).then_inc(gate_in, 16)
            else:
                sp.dma_start(w_gate[:, :], a["Wr"]).then_inc(gate_in, 16)
                sp.dma_start(b_gate[:, :], a["br"].rearrange("(a e) -> a e", a=1).to_broadcast([P, E])).then_inc(gate_in, 16)

            def step(i):
                if i.exists():
                    if i.after(4):
                        sp.wait_ge(xt_ready, i.count(less=4))
                        sp.wait_ge(x_kept, i.count(less=4))
                    sp.dma_start(x[:, i.slot(4), :, :], x_v[i.n]).then_inc(loaded[i.slot(4)], 16)
            skewed(sp, step, 0, 0, Quad)
            if top2:
                sp.dma_start(raw["W1"][:, :, :, :], a["W1"].rearrange("e (c f) d -> f e c d", f=P)).then_inc(weights_in, 16)
                sp.dma_start(raw["W2"][:, :, :, :], a["W2"].rearrange("e (c f) d -> f e c d", f=P)).then_inc(weights_in, 16)
                sp.dma_start(raw["W3"][:, :, :, :], a["W3"].rearrange("e d (c f) -> d e c f", f=P)).then_inc(weights_in, 16)
            else:
                sp.dma_start(w_up[:, :, :], a["W1"].rearrange("e h f -> h e f")).then_inc(weights_in, 16)
                sp.dma_start(w_down[:, :, :, :], a["W2"].rearrange("e (c f) h -> f e c h", f=P)).then_inc(weights_in, 16)
                sp.dma_start(b_up[:, :, :].rearrange("p e h -> p (e h)"),
                             a["b1"].rearrange("(a e) h -> a (e h)", a=1).to_broadcast([P, E * H])).then_inc(weights_in, 16)
                sp.dma_start(b_down[:, :, :].rearrange("p e h -> p (e h)"),
                             a["b2"].rearrange("(a e) h -> a (e h)", a=1).to_broadcast([P, E * D])).then_inc(weights_in, 16)
            sp.wait_ge(weights_in, 48 if top2 else 64)

        @block.gpsimd
        def _(pool):
            pool.memset(before[:, :], 1.0).then_inc(made, 1)
            pool.memset(all_ones[:, :], 1.0).then_inc(made, 1)
            pool.iota(order[:, :], pattern=[[-1, E]], base=E, channel_multiplier=0, allow_small_or_imprecise_dtypes=True).then_inc(made, 1)
            pool.iota(steps128[:, :], pattern=[[P, HALF]], base=0, channel_multiplier=0, allow_small_or_imprecise_dtypes=True).then_inc(made, 1)
            pool.iota(tile_no[:, :], pattern=[[1, T // 2]], base=0, channel_multiplier=0, allow_small_or_imprecise_dtypes=True).then_inc(made, 1)
            pool.wait_ge(made, 5)
            pool.affine_select(out=before[:, :], in_=before[:, :], compare_op=ALU.is_gt, fill=0.0, base=0,
                               pattern=[[1, P]], channel_multiplier=-1).then_inc(made, 1)
            pool.wait_ge(x_kept, NT // 4)
            pool.wait_ge(routed, 1)
            pool.wait_ge(xs_filled, 16 * Sorted2.ALL)
            for t in range(HALF):
                for r in range(K):
                    pool.indirect_dma_start(xs[0], bass.IndirectOffsetOnAxis(ap=dest[:, r, t:t + 1], axis=0), x_all[:, t, :], None)\
                        .then_inc(scattered, 16)
            pool.wait_ge(scattered, 16 * K * HALF + earlier)

        @block.tensor
        def _(pe):
            pe.wait_ge(gate_in, 16 if top2 else 32)
            if top2:
                nc.tensor.transpose(before_ps[:, :, :].rearrange("p a b -> p (a b)")[:, 0:E], raw_gate[:, :], k["ident"][0:E, 0:E])\
                    .then_inc(gate_turned, 1)
                pe.wait_ge(gate_copied, 1)

            def step(i):
                t = i + 1
                if t.exists():
                    pe.wait_ge(loaded[t.slot(4)], t.uses(4) * 16)
                    if t.after(2):
                        pe.wait_ge(xt_copied, t.count(less=2))
                    for n in range(4):
                        tr = nc.tensor.transpose(turn_ps[t.slot(2)][:, n, :], x[:, t.slot(4), n, :], k["ident"][:, :])
                    tr.then_inc(xt_ready, 1)
                t = i
                if t.exists():
                    pe.wait_ge(xt_copied, t.count())
                    for n in range(4):
                        tile = t.n * 4 + n
                        mm = nc.tensor.matmul(logits_ps[:, bass.ds(tile, 1), :], xt[:, t.slot(2), n, :], w_gate[:, :], start=True, stop=True)
                    mm.then_inc(logits_ready, 1)
            skewed(pe, step, 1, 0, Quad)
            pe.wait_ge(made, 6)
            pe.wait_ge(selected, 1)
            nc.tensor.matmul(total_ps[:, :, :], all_ones[:, :], sel_bf[:, :, :], start=True, stop=True)
            nc.tensor.matmul(before_ps[:, :, :], before[:, :], sel_bf[:, :, :], start=True, stop=True).then_inc(counted, 1)
            if blocks:
                pe.wait_ge(weights_in, 48)
            for n, (src, dst) in enumerate(blocks):
                if n >= 2:
                    pe.wait_ge(w_copied, n - 1)
                nc.tensor.transpose(turn_ps[n % 2][:, 0, :], src, k["ident"][:, :]).then_inc(w_turned, 1)

        @block.scalar
        def _(act):
            if top2:
                act.wait_ge(gate_turned, 1)
                act.copy(w_gate[:, :], before_ps[:, :, :].rearrange("p a b -> p (a b)")[:, 0:E]).then_inc(gate_copied, 1)

            def step(i):
                if i.exists():
                    act.wait_ge(xt_ready, i.count())
                    if i.after(2):
                        act.wait_ge(logits_ready, i.count(less=2))
                    act.copy(xt[:, i.slot(2), :, :], turn_ps[i.slot(2)][:, :, :]).then_inc(xt_copied, 1)
            skewed(act, step, 0, 0, Quad)
            act.wait_ge(exp_asked, 1)
            if top2:
                act.activation(small["e2"][:, :], small["diff"][:, :], ACT.Exp).then_inc(exp_ready, 1)
            else:
                act.activation(big["ex"][:, :, :], big["shifted"][:, :, :], ACT.Exp).then_inc(exp_ready, 1)
            for n, (src, dst) in enumerate(blocks):
                act.wait_ge(w_turned, n + 1)
                act.copy(dst, turn_ps[n % 2][:, 0, :]).then_inc(w_copied, 1)

        @block.vector
        def _(dve):
            link = link_to(dve, link_sem)
            tt, ts, stt, red = dve.tensor_tensor, dve.tensor_scalar, dve.scalar_tensor_tensor, dve.tensor_reduce
            full = lambda n: big[n][:, :, :]
            wide = lambda v: v.unsqueeze(2).to_broadcast([P, NT, E])
            rows = lambda v: v.unsqueeze(1).to_broadcast([P, NT, E])

            def choose(r, src):
                link(red(mx[:, r, :], src, AX, ALU.max))
                link(tt(full("equal"), src, wide(mx[:, r, :]), ALU.is_equal))
                link(tt(full("ranked"), full("equal"), rows(order[:, :]), ALU.mult))
                link(red(first[:, :], full("ranked"), AX, ALU.max))
                link(tt(sel[:, r, :, :], full("ranked"), wide(first[:, :]), ALU.is_equal))

            def step(i):
                if i.exists():
                    dve.wait_ge(loaded[i.slot(4)], i.uses(4) * 16)
                    first_tile = i.n * 4
                    dve.tensor_copy(x_all[:, bass.ds(first_tile, 4), :], x[:, i.slot(4), :, :]).then_inc(x_kept, 1)
            skewed(dve, step, 0, 0, Quad)
            dve.wait_ge(made, 6)
            dve.wait_ge(logits_ready, NT // 4)
            if top2:
                link(dve.tensor_copy(full("logit"), logits_ps[:, :, :]))
                choose(0, full("logit"))
                link(ts(full("rest"), sel[:, 0, :, :], -1.0, 1.0, ALU.mult, ALU.add))
                link(tt(full("ex"), full("rest"), full("logit"), ALU.mult))
                link(stt(out=full("rest"), in0=sel[:, 0, :, :], scalar=-3.0e38, in1=full("ex"), op0=ALU.mult, op1=ALU.add))
                choose(1, full("rest"))
                tt(small["diff"][:, :], mx[:, 1, :], mx[:, 0, :], ALU.subtract).then_inc(exp_asked, 1)
                tt(sel_bf[:, :, :], sel[:, 0, :, :], sel[:, 1, :, :], ALU.add).then_inc(selected, 1)
            else:
                dve.wait_ge(gate_in, 32)
                link(tt(full("logit"), logits_ps[:, :, :], rows(b_gate[:, :]), ALU.add))
                link(red(mx[:, 2, :], full("logit"), AX, ALU.max))
                tt(full("shifted"), full("logit"), wide(mx[:, 2, :]), ALU.subtract).then_inc(exp_asked, 1)
                dve.wait_ge(exp_ready, 1)
                choose(0, full("ex"))
                dve.tensor_copy(sel_bf[:, :, :], sel[:, 0, :, :]).then_inc(selected, 1)
                link(red(small["z"][:, :], full("ex"), AX, ALU.add))
                link(dve.reciprocal(small["rz"][:, :], small["z"][:, :]))
                link(tt(gate[:, 0, :], mx[:, 0, :], small["rz"][:, :], ALU.mult))
            dve.wait_ge(counted, 1)
            link(dve.tensor_copy(full("total"), total_ps[:, :, :]))
            halves = {n: big[n][:, :, :].rearrange("p (h t) e -> p h t e", h=2) for n in ("total", "even", "odd", "pos")}
            src, stride, spare = "total", 1, ["even", "odd"]
            while stride < HALF:
                dst = spare[0]
                dve.tensor_copy(halves[dst][:, :, 0:stride, :], halves[src][:, :, 0:stride, :])
                for h in range(2):
                    last = tt(halves[dst][:, h, stride:, :], halves[src][:, h, stride:, :], halves[src][:, h, :HALF - stride, :], ALU.add)
                link(last)
                src, stride, spare = dst, 2 * stride, spare[::-1]
            for h in range(2):
                last = tt(fits[:, h, :, :], halves[src][:, h, HALF - 1, :].unsqueeze(2).to_broadcast([P, E, HALF]),
                          steps128[:, :].unsqueeze(1).to_broadcast([P, E, HALF]), ALU.is_gt)
            link(last)
            link(red(n_tiles[:, :, :], fits[:, :, :, :], AX, ALU.add))
            link(dve.tensor_copy(ends[0][:, :, :], n_tiles[:, :, :]))
            now, stride = 0, 1
            while stride < E:
                dve.tensor_copy(ends[1 - now][:, :, 0:stride], ends[now][:, :, 0:stride])
                link(tt(ends[1 - now][:, :, stride:], ends[now][:, :, stride:], ends[now][:, :, :E - stride], ALU.add))
                now, stride = 1 - now, 2 * stride
            link(tt(base[:, :, :], ends[now][:, :, :], n_tiles[:, :, :], ALU.subtract))
            link(ts(base[:, :, :], base[:, :, :], float(P), None, ALU.mult))
            link(tt(full("pos"), big[src][:, :, :], full("total"), ALU.subtract))
            link(tt(full("pos"), full("pos"), before_ps[:, :, :], ALU.add))
            for h in range(2):
                last = tt(halves["pos"][:, h, :, :], halves["pos"][:, h, :, :], base[:, h:h + 1, :].to_broadcast([P, HALF, E]), ALU.add)
            link(last)
            for r in range(K):
                link(tt(full("equal"), full("pos"), sel[:, r, :, :], ALU.mult))
                link(red(dest_f[:, r, :], full("equal"), AX, ALU.add))
            dve.tensor_copy(dest[:, :, :], dest_f[:, :, :]).then_inc(routed, 1)
            dve.tensor_copy(source_f[:, :, 0:HALF], dest_f[:, :, 0:HALF])
            link(ts(source_f[:, :, HALF:], dest_f[:, :, HALF:], float(T // 2 * P), None, ALU.add))
            link(dve.tensor_copy(source[:, :, :], source_f[:, :, :]))
            for h in range(2):
                last = tt(passed[:, h * (T // 2):(h + 1) * (T // 2), :], tile_no[:, :].unsqueeze(2).to_broadcast([1, T // 2, E]),
                          ends[now][0:1, h:h + 1, :].to_broadcast([1, T // 2, E]), ALU.is_ge)
            link(last)
            link(red(expert_f[:, 0, :], passed[:, :, :], AX, ALU.add))
            link(ts(expert_f[:, 1, :], expert_f[:, 0, :], float(E - 1), None, ALU.min))
            link(dve.tensor_copy(expert_of[:, :], expert_f[:, 1, :]))
            if top2:
                dve.wait_ge(exp_ready, 1)
                link(ts(small["z"][:, :], small["e2"][:, :], 1.0, None, ALU.add))
                link(dve.reciprocal(gate[:, 0, :], small["z"][:, :]))
                link(tt(gate[:, 1, :], small["e2"][:, :], gate[:, 0, :], ALU.mult))


def run_experts(nc, stage, k, top2, kind, xs, ys, w_up, w_down, b_up, b_down, expert_of, x_all, dest, source, yg, pool_dmas):
    FC, K = (2, 2) if top2 else (4, 1)
    scattered, gathered = pool_dmas[0:2]
    earlier = 0 if top2 else 16 * 2 * NT
    HID = FC * P

    def experts_from(engine):
        held = []

        def look(i):
            first, count = (0, 2) if i.c == -2 else (i.n, 8 if i.static and i.c + 10 > kind.ALL else 10)
            if i.c == -2 or i.c >= 0 and i.c % 8 == 0:
                held[:] = nc.values_load_multi_w_load_instructions(
                    expert_of[0:1, bass.ds(first, count)], engines=(engine,), min_val=0, max_val=7,
                    skip_runtime_bounds_check_because="route() counts at most seven")[1]
            at = i.c % 8 if i.c >= 0 else i.c
            return (held[at] if i.c >= 0 else None), (held[at + 2] if at + 2 < len(held) and i.c >= -2 else None)
        return look

    with ExitStack() as ctx:
        mk = Maker(nc, ctx, stage + "_run")
        sb, ps, sem = mk.sb, mk.ps, mk.sem
        x = sb("x", [P, 2, 4, D])
        y = sb("y", [P, 2, 4, D])
        xt = sb("xt", [P, 2, P])
        act1 = sb("act1", [P, 2, HID]) if top2 else None
        h = sb("h", [P, 2, HID])
        ht = sb("ht", [P, 2, FC, P])
        xt_ps, up_ps, ht_ps, y_ps = ([ps(f"{n}{i}", [P, 512]) for i in range(2)] for n in ("xt", "up", "ht", "y"))
        loaded = [sem(f"x_loaded{i}") for i in range(2)]
        stored = [sem(f"stored{i}") for i in range(2)]
        x_turned, x_copied, up_ready, silu_ready, h_ready, h_turned, h_copied, down_ready, y_copied = (
            sem(n) for n in ("x_turned", "x_copied", "up_ready", "silu_ready", "h_ready", "h_turned", "h_copied", "down_ready", "y_copied"))
        xs_v = [t[0:kind.ALL // 2 * P, :].rearrange("(g n p) d -> g p n d", p=P, n=4) for t in xs]
        ys_v = ys[0:kind.ALL * P, :].rearrange("(g n p) d -> g p n d", p=P, n=4)
        block = mk.block()

        @block.sync
        def _(sp):
            half = [0]

            def second():
                sp.wait_ge(scattered, 16 * K * NT + earlier)
                half[0] = 1

            def step(i):
                t = i + -1
                if t.exists() and t.c % 4 == 3:
                    n, slot, uses = four(t)
                    sp.wait_ge(y_copied, t.count())
                    sp.dma_start(ys_v[n], y[:, slot, :, :]).then_inc(stored[slot], 16)
                t = i + 8
                if t.exists() and t.c % 4 == 0:
                    n, slot, uses = four(t)
                    if t.after(8):
                        sp.wait_ge(x_turned, t.count(less=5))
                    sp.dma_start(x[:, slot, :, :], xs_v[half[0]][n - half[0] * (kind.ALL // 8)]).then_inc(loaded[slot], 16)
            skewed(sp, step, 8, 1, kind, pause=(kind.ALL // 2 - 8, second))
            for s in stored:
                sp.wait_ge(s, 16 * kind.ALL // 8)

        @block.gpsimd
        def _(pool):
            for t in range(HALF, NT):
                for r in range(K):
                    pool.indirect_dma_start(xs[1], bass.IndirectOffsetOnAxis(ap=dest[:, r, t:t + 1], axis=0), x_all[:, t, :], None)\
                        .then_inc(scattered, 16)
            pool.wait_ge(scattered, 16 * K * NT + earlier)
            for s in stored:
                pool.wait_ge(s, 16 * kind.ALL // 16)
            for t in range(HALF):
                for r in range(K):
                    pool.indirect_dma_start(yg[:, t, r, :], None, ys[0:kind.ALL // 2 * P, :],
                                            bass.IndirectOffsetOnAxis(ap=source[:, r, t:t + 1], axis=0)).then_inc(gathered, 16)
            pool.wait_ge(gathered, 16 * K * HALF + earlier // 2)

        @block.tensor
        def _(pe):
            look = experts_from(mybir.EngineType.PE)

            def step(i):
                e_now, e_ahead = look(i)
                t = i + 3
                if t.exists():
                    n, slot, uses = four(t)
                    if t.c % 4 == 0:
                        pe.wait_ge(loaded[slot], uses * 16)
                    if t.after(2):
                        pe.wait_ge(x_copied, t.count(less=2))
                    nc.tensor.transpose(xt_ps[t.slot(2)][:, 0:P], x[:, slot, t.c % 4, :], k["ident"][:, :]).then_inc(x_turned, 1)
                t = i + 2
                if t.exists():
                    pe.wait_ge(x_copied, t.count())
                    if t.after(2):
                        pe.wait_ge(h_ready, t.count(less=2))
                    nc.tensor.matmul(up_ps[t.slot(2)][:, :], xt[:, t.slot(2), :], w_up[:, bass.ds(e_ahead, 1), :], start=True, stop=True)\
                        .then_inc(up_ready, 1)
                t = i + 1
                if t.exists():
                    pe.wait_ge(h_ready, t.count())
                    if t.after(2):
                        pe.wait_ge(h_copied, t.count(less=2))
                    for c in range(FC):
                        tr = nc.tensor.transpose(ht_ps[t.slot(2)][:, c * P:(c + 1) * P], h[:, t.slot(2), c * P:(c + 1) * P], k["ident"][:, :])
                    tr.then_inc(h_turned, 1)
                t = i
                if t.exists():
                    pe.wait_ge(h_copied, t.count())
                    if t.after(2):
                        pe.wait_ge(y_copied, t.count(less=2))
                    for c in range(FC):
                        mm = nc.tensor.matmul(y_ps[t.slot(2)][:, 0:D], ht[:, t.slot(2), c, :], w_down[:, bass.ds(e_now, 1), c, :],
                                              start=(c == 0), stop=(c == FC - 1))
                    mm.then_inc(down_ready, 1)
            skewed(pe, step, 3, 0, kind)

        @block.scalar
        def _(act):
            def step(i):
                t = i + 3
                if t.exists():
                    act.wait_ge(x_turned, t.count())
                    if t.after(2):
                        act.wait_ge(up_ready, t.count(less=2))
                    act.copy(xt[:, t.slot(2), :], xt_ps[t.slot(2)][:, 0:P]).then_inc(x_copied, 1)
                t = i + 2
                if t.exists() and top2:
                    act.wait_ge(up_ready, t.count())
                    if t.after(2):
                        act.wait_ge(h_ready, t.count(less=2))
                    act.activation(act1[:, t.slot(2), :], up_ps[t.slot(2)][:, 0:HID], ACT.Silu).then_inc(silu_ready, 1)
                t = i + 1
                if t.exists():
                    act.wait_ge(h_turned, t.count())
                    if t.after(2):
                        act.wait_ge(down_ready, t.count(less=2))
                    act.activation(ht[:, t.slot(2), :, :].rearrange("p c n -> p (c n)"), ht_ps[t.slot(2)][:, 0:HID],
                                   ACT.Copy if top2 else ACT.Relu).then_inc(h_copied, 1)
            skewed(act, step, 3, 0, kind)

        @block.vector
        def _(dve):
            look = experts_from(mybir.EngineType.DVE)

            def step(i):
                e_now, e_ahead = (None, None) if top2 else look(i)
                t = i + 2
                if t.exists():
                    s2 = t.slot(2)
                    dve.wait_ge(silu_ready if top2 else up_ready, t.count())
                    if t.after(2):
                        dve.wait_ge(h_turned, t.count(less=2))
                    if top2:
                        dve.tensor_tensor(h[:, s2, :], up_ps[s2][:, HID:2 * HID], act1[:, s2, :], ALU.mult).then_inc(h_ready, 1)
                    else:
                        dve.tensor_tensor(h[:, s2, :], up_ps[s2][:, :], b_up[:, bass.ds(e_ahead, 1), :].rearrange("p a n -> p (a n)"), ALU.add)\
                            .then_inc(h_ready, 1)
                t = i
                if t.exists():
                    n, slot, uses = four(t)
                    dve.wait_ge(down_ready, t.count())
                    if t.c % 4 == 0 and t.after(8):
                        dve.wait_ge(stored[slot], (uses - 1) * 16)
                    if top2:
                        dve.tensor_copy(y[:, slot, t.c % 4, :], y_ps[t.slot(2)][:, 0:D]).then_inc(y_copied, 1)
                    else:
                        dve.tensor_tensor(y[:, slot, t.c % 4, :], y_ps[t.slot(2)][:, 0:D],
                                          b_down[:, bass.ds(e_now, 1), :].rearrange("p a n -> p (a n)"), ALU.add).then_inc(y_copied, 1)
            skewed(dve, step, 3, 0, kind)


def combine(nc, stage, k, K, ys, source, gate, x_all, yg, x_out, gathered):
    with ExitStack() as ctx:
        mk = Maker(nc, ctx, stage + "_combine")
        sb, sem = mk.sb, mk.sem
        r1 = sb("r1", [P, 4, D])
        r = sb("r", [P, 2, 4, D])
        stats = sb("stats", [P, 4, 6])
        mv = sb("mv", [P, 2, 4, 2])
        ve = sb("ve", [P, 2, 4])
        rstd = sb("rstd", [P, 2, 4])
        out = sb("out", [P, 2, 4, D])
        earlier = 0 if K == 2 else 16 * 2 * HALF // 2
        stored = [sem(f"stored{i}") for i in range(2)]
        partly, summed, stats_ready, mean_ready, var_ready, rstd_ready, normed, passed_dve = (
            sem(n) for n in ("partly", "summed", "stats_ready", "mean_ready", "var_ready", "rstd_ready", "normed", "passed_dve"))
        out_v = x_out.rearrange("(g n p) d -> g p n d", p=P, n=4)
        block = mk.block()

        @block.sync
        def _(sp):
            def step(i):
                if i.exists():
                    sp.wait_ge(normed, i.count())
                    sp.dma_start(out_v[i.n], out[:, i.slot(2), :, :]).then_inc(stored[i.slot(2)], 16)
            skewed(sp, step, 0, 0, Group)
            for s in stored:
                sp.wait_ge(s, 16 * NT // 8)

        @block.gpsimd
        def _(pool):
            for g in range(NT // 4):
                for tile in (HALF + 2 * g, HALF + 2 * g + 1):
                    landed = gathered[tile // 4 % 2]
                    if tile % 4 == 0 and tile >= HALF + 8:
                        pool.wait_ge(landed, (tile - HALF) // 8 * 64 * K + earlier)
                    for m in range(K):
                        pool.indirect_dma_start(yg[:, tile, m, :], None, ys, bass.IndirectOffsetOnAxis(ap=source[:, m, tile:tile + 1], axis=0))\
                            .then_inc(landed, 16)
                pool.wait_ge(var_ready, g + 1)
                if g >= 2:
                    pool.wait_ge(normed, g - 1)
                pool.tensor_tensor(rstd[:, g % 2, :], ve[:, g % 2, :], k["half"][:, :], ALU.pow).then_inc(rstd_ready, 1)

        @block.vector
        def _(dve):
            second_half = []

            def step(i):
                t = i
                if t.exists():
                    s2 = t.slot(2)
                    if t.c >= NT // 8 if t.static else second_half:
                        dve.wait_ge(gathered[s2], (t.uses(2) - NT // 16) * 64 * K + earlier)
                    if t.after(2):
                        dve.wait_ge(normed, t.count(less=2))
                    if t.after(1) and K == 2:
                        dve.wait_ge(summed, t.count(less=1))
                    for m in range(K):
                        dst = r[:, s2, :, :] if m == K - 1 else r1[:, :, :]
                        for n in range(4):
                            tile = t.n * 4 + n
                            base = r1[:, n, :] if m else x_all[:, bass.ds(tile, 1), :].rearrange("p a d -> p (a d)")
                            mine = yg[:, bass.ds(tile, 1), m, :].rearrange("p a d -> p (a d)")
                            st = dve.scalar_tensor_tensor(out=dst[:, n, :], in0=mine, scalar=gate[:, m, bass.ds(tile, 1)],
                                                          in1=base, op0=ALU.mult, op1=ALU.add)
                        if m < K - 1:
                            st.then_inc(partly, 1)
                            dve.wait_ge(partly, t.count())
                    st.then_inc(summed, 1)
                    dve.wait_ge(summed, t.count())
                    if t.after(1):
                        dve.wait_ge(mean_ready, t.count(less=1))
                    for n in range(4):
                        bs = dve.bn_stats(stats[:, n, :], r[:, s2, n, :])
                    bs.then_inc(stats_ready, 1)
                    dve.wait_ge(stats_ready, t.count())
                    settle(dve, passed_dve)
                    for n in range(4):
                        ag = dve.bn_aggr(mv[:, s2, n, :], stats[:, n, :])
                    ag.then_inc(mean_ready, 1)
                    dve.wait_ge(mean_ready, t.count())
                    if t.after(2):
                        dve.wait_ge(rstd_ready, t.count(less=2))
                    dve.tensor_scalar(ve[:, s2, :], mv[:, s2, :, 1], LN_EPS, None, ALU.add).then_inc(var_ready, 1)
                t = i + -1
                if t.exists():
                    s2 = t.slot(2)
                    dve.wait_ge(rstd_ready, t.count())
                    if t.after(2):
                        dve.wait_ge(stored[s2], (t.uses(2) - 1) * 16)
                    for n in range(4):
                        no = dve.tensor_scalar(out[:, s2, n, :], r[:, s2, n, :], mv[:, s2, n, 0:1],
                                               rstd[:, s2, n:n + 1], ALU.subtract, ALU.mult)
                    no.then_inc(normed, 1)
            skewed(dve, step, 0, 1, Group, pause=(NT // 8, lambda: second_half.append(1)))


KK, VV, PP = 0, S + 1, 2 * (S + 1)
ROW = 3 * (S + 1)
RMS_EPS, ETA_MIN = 1e-6, 1e-6
F = 64
N_MEM = float(F * D)


def memory_products(nc, stage, k, x_in, a, rows_out, k_all, v_all, qt_all, eta_col, w_out_t):
    with ExitStack() as ctx:
        mk = Maker(nc, ctx, stage)
        sb, ps, sem = mk.sb, mk.ps, mk.sem
        raw = sb("raw", [P, 4, D])
        w_all = sb("w_all", [P, 2 * F + D])
        w_norm = sb("w_norm", [P, 1])
        eta = sb("eta", [P, 1])
        eta_neg = sb("eta_neg", [P, 1])
        load_all(nc, stage, [(raw[0:F, 0, :], a["Wk"]), (raw[0:F, 1, :], a["Wq"]), (raw[:, 2, :], a["Wv"]), (raw[:, 3, :], a["Wout"]),
                             (w_norm[:, :], a["norm_weight"].rearrange("(d a) -> d a", a=1)),
                             (eta[0:F, :], a["eta"].rearrange("(f a) -> f a", a=1)),
                             (eta[F:P, :], a["eta"].rearrange("(f a) -> f a", a=1))])
        turn_blocks(nc, stage, k, [(raw[0:F, 0, :], w_all[:, 0:F]), (raw[0:F, 1, :], w_all[:, F:2 * F]), (raw[:, 2, :], w_all[:, 2 * F:]),
                                   (raw[:, 3, :], w_out_t)])
        x = sb("x", [P, 2, 4, D])
        sq = sb("sq", [P, D])
        ms = sb("ms", [P, 4, 1])
        mse = sb("mse", [P, 4, 1])
        rr = sb("rr", [P, 4, 1])
        xs = sb("xs", [P, 2, D])
        xt = sb("xt", [P, 2, P])
        low = sb("low", [P, 2, 2 * F])
        e = sb("e", [P, 2, 2 * F])
        kq = sb("kq", [P, 2, 2, F])
        q_bd = sb("q_bd", [P, 2, 2, F])
        own_batch = sb("own_batch", [P, 2])
        kt = sb("kt", [F, 2, P])
        ket = sb("ket", [F, 2, 2, S + 1])
        vt = sb("vt", [P, 2, 2, S + 1])
        row = sb("row", [P, 2, 4, ROW])
        t_ps, p_ps, vt_ps, k_ps, q_ps = (ps(n, [P, 512]) for n in ("t", "p", "vt", "k", "q"))
        g_ps = [ps(f"g{i}", [P, 512]) for i in range(2)]
        loaded = [sem(f"x_loaded{i}") for i in range(2)]
        stored = [sem(f"stored{i}") for i in range(2)]
        (eta_ready, squares, mse_ready, rr_ready, xs_ready, xt_ready, xt_copied, proj_ready, low_ready, e_ready, kq_ready,
         k_kept, q_spread, k_turned, q_turned, k_copied, q_copied, ke_ready, v_copied, vt_copied, g_ready, row_copied, row_ready) = (
            sem(n) for n in ("eta_ready", "squares", "mse_ready", "rr_ready", "xs_ready", "xt_ready", "xt_copied", "proj_ready",
                             "low_ready", "e_ready", "kq_ready", "k_kept", "q_spread", "k_turned",
                             "q_turned", "k_copied", "q_copied", "ke_ready", "v_copied",
                             "vt_copied", "g_ready", "row_copied", "row_ready"))
        x_v = x_in.rearrange("(g n p) d -> g p n d", p=P, n=4)
        rows_v = rows_out.rearrange("(g n p) r -> g p n r", p=P, n=4)
        passed_pe = sem("passed_pe")
        kind = Eights
        block = mk.block()

        @block.sync
        def _(sp):
            def step(i):
                t = i + -1
                if t.exists() and t.c % 4 == 3:
                    n, slot, uses = four(t)
                    sp.wait_ge(row_ready, t.count())
                    sp.wait_ge(row_copied, t.count())
                    sp.dma_start(rows_v[n], row[:, slot, :, :]).then_inc(stored[slot], 16)
                t = i + 11
                if t.exists() and t.c % 4 == 0:
                    n, slot, uses = four(t)
                    if t.after(8):
                        sp.wait_ge(xs_ready, t.count(less=5))
                    sp.dma_start(x[:, slot, :, :], x_v[n]).then_inc(loaded[slot], 16)
            skewed(sp, step, 11, 1, kind)
            for s in stored:
                sp.wait_ge(s, 16 * NT // 8)

        @block.gpsimd
        def _(pool):
            def step(i):
                t = i
                if t.exists():
                    s2 = t.slot(2)
                    pool.wait_ge(kq_ready, t.count())
                    if t.after(2):
                        pool.wait_ge(q_turned, t.count(less=2))
                    pool.tensor_tensor(q_bd[:, s2, :, :], kq[:, s2, 1:2, :].to_broadcast([P, 2, F]),
                                       own_batch[:, :].unsqueeze(2).to_broadcast([P, 2, F]), ALU.mult).then_inc(q_spread, 1)
                    pool.tensor_copy(k_all[:, bass.ds(t.n, 1), :], kq[:, s2, 0:1, :]).then_inc(k_kept, 1)
                t = i + 4
                if t.exists():
                    pool.wait_ge(mse_ready, t.count())
                    if t.after(4):
                        pool.wait_ge(xs_ready, t.count(less=4))
                    pool.tensor_tensor(rr[:, t.slot(4), :], mse[:, t.slot(4), :], k["half"][:, 0:1], ALU.pow).then_inc(rr_ready, 1)
            pool.wait_ge(eta_ready, 7)
            skewed(pool, step, 4, 0, kind)

        @block.tensor
        def _(pe):
            def step(i):
                t = i
                if t.exists():
                    pe.wait_ge(kq_ready, t.count())
                    if t.after(1):
                        pe.wait_ge(ke_ready, t.count(less=1))
                    settle(pe, passed_pe)
                    nc.tensor.transpose(k_ps[0:F, 0:P], kq[:, t.slot(2), 0, :], k["ident"][:, :]).then_inc(k_turned, 1)
                t = i + 2
                if t.exists():
                    pe.wait_ge(xs_ready, t.count())
                    if t.after(1):
                        pe.wait_ge(xt_copied, t.count(less=1))
                    nc.tensor.transpose(t_ps[:, 0:P], xs[:, t.slot(2), :], k["ident"][:, :]).then_inc(xt_ready, 1)
                t = i + 1
                if t.exists():
                    s2 = t.slot(2)
                    pe.wait_ge(xt_copied, t.count())
                    if t.after(1):
                        pe.wait_ge(kq_ready, t.count(less=1))
                        pe.wait_ge(vt_copied, t.count(less=1))
                        pe.wait_ge(v_copied, t.count(less=1))
                    nc.tensor.matmul(p_ps[:, 0:2 * F], xt[:, s2, :], w_all[:, 0:2 * F], start=True, stop=True)
                    nc.tensor.matmul(vt_ps[:, P:P + D], xt[:, s2, :], w_all[:, 2 * F:], start=True, stop=True)
                    nc.tensor.matmul(vt_ps[:, 0:P], w_all[:, 2 * F:], xt[:, s2, :], start=True, stop=True).then_inc(proj_ready, 1)
                t = i
                if t.exists():
                    pe.wait_ge(q_spread, t.count())
                    if t.after(1):
                        pe.wait_ge(q_copied, t.count(less=1))
                    nc.tensor.transpose(q_ps[:, 0:P], q_bd[:, t.slot(2), :, :], k["ident"][:, :]).then_inc(q_turned, 1)
                t = i
                if t.exists():
                    s2 = t.slot(2)
                    pe.wait_ge(k_copied, t.count())
                    pe.wait_ge(ke_ready, t.count())
                    pe.wait_ge(vt_copied, t.count())
                    if t.after(2):
                        pe.wait_ge(row_ready, t.count(less=2))
                        pe.wait_ge(row_copied, t.count(less=2))
                    settle(pe, passed_pe)
                    for n in range(3):
                        for b in range(2):
                            rows = slice(b * S, (b + 1) * S)
                            lhs, rhs = ((kt[:, s2, rows], ket[:, s2, b, :]), (vt[:, s2, b, 0:S], vt[:, s2, b, :]),
                                        (ket[:, s2, b, 0:S], ket[:, s2, b, :]))[n]
                            mm = nc.tensor.matmul(g_ps[s2][rows, n * (S + 1):(n + 1) * (S + 1)], lhs, rhs, start=True, stop=True)
                    mm.then_inc(g_ready, 1)
            pe.wait_ge(eta_ready, 5)
            skewed(pe, step, 3, 0, kind)

        @block.scalar
        def _(act):
            def step(i):
                t = i
                if t.exists():
                    act.wait_ge(k_turned, t.count())
                    if t.after(2):
                        act.wait_ge(g_ready, t.count(less=2))
                    act.copy(kt[:, t.slot(2), :], k_ps[0:F, 0:P]).then_inc(k_copied, 1)
                t = i + 2
                if t.exists():
                    act.wait_ge(xt_ready, t.count())
                    if t.after(2):
                        act.wait_ge(proj_ready, t.count(less=2))
                    act.mul(xt[:, t.slot(2), :], t_ps[:, 0:P], w_norm[:, 0:1]).then_inc(xt_copied, 1)
                t = i + 1
                if t.exists():
                    s2 = t.slot(2)
                    act.wait_ge(proj_ready, t.count())
                    if t.after(2):
                        act.wait_ge(g_ready, t.count(less=2))
                    act.copy(vt[:, s2, :, 0:S], vt_ps[:, 0:P].rearrange("p (b s) -> p b s", b=2)).then_inc(vt_copied, 1)
                    act.wait_ge(low_ready, t.count())
                    if t.after(2):
                        act.wait_ge(kq_ready, t.count(less=2))
                    act.activation(e[:, s2, :], low[:, s2, :], ACT.Exp).then_inc(e_ready, 1)
                    act.copy(v_all[:, bass.ds(t.n, 1), :], vt_ps[:, P:P + D]).then_inc(v_copied, 1)
                t = i
                if t.exists():
                    act.wait_ge(q_turned, t.count())
                    act.copy(qt_all[:, bass.ds(t.n, 1), :], q_ps[:, 0:P]).then_inc(q_copied, 1)
            act.wait_ge(eta_ready, 5)
            skewed(act, step, 3, 0, kind)

        @block.vector
        def _(dve):
            dve.memset(vt[:, :, :, :], 1.0).then_inc(eta_ready, 1)
            dve.memset(ket[:, :, :, :], 1.0).then_inc(eta_ready, 1)
            dve.memset(own_batch[:, :], 0.0).then_inc(eta_ready, 1)
            dve.tensor_scalar(eta_neg[:, :], eta[:, :], -1.0, None, ALU.mult).then_inc(eta_ready, 1)
            dve.wait_ge(eta_ready, 4)
            dve.tensor_scalar(eta_col, eta[:, :], eta_neg[:, :], ETA_MIN, ALU.max, ALU.max).then_inc(eta_ready, 1)
            dve.wait_ge(eta_ready, 5)
            for b in range(2):
                dve.memset(own_batch[b * S:(b + 1) * S, b:b + 1], 1.0).then_inc(eta_ready, 1)

            def step(i):
                t = i + -1
                if t.exists():
                    n, slot, uses = four(t)
                    s2 = t.slot(2)
                    dve.wait_ge(g_ready, t.count())
                    if t.c % 4 == 0 and t.after(8):
                        dve.wait_ge(stored[slot], (uses - 1) * 16)
                    dst = row[:, slot, t.c % 4, :]
                    dve.tensor_copy(dst[:, 0:PP], g_ps[s2][:, 0:PP]).then_inc(row_copied, 1)
                    dve.wait_ge(row_copied, t.count())
                    dve.tensor_tensor(dst[:, PP:ROW], g_ps[s2][:, PP:ROW], dst[:, VV:PP], ALU.mult).then_inc(row_ready, 1)
                t = i
                if t.exists():
                    dve.wait_ge(k_copied, t.count())
                    if t.after(2):
                        dve.wait_ge(g_ready, t.count(less=2))
                    dve.tensor_scalar(ket[:, t.slot(2), :, 0:S], k_ps[0:F, 0:P].rearrange("p (b s) -> p b s", b=2),
                                      eta_col[0:F, :], None, ALU.mult).then_inc(ke_ready, 1)
                t = i + 4
                if t.exists():
                    n, slot, uses = four(t)
                    s4 = t.slot(4)
                    if t.c % 4 == 0:
                        dve.wait_ge(loaded[slot], uses * 16)
                    if t.after(1):
                        dve.wait_ge(squares, t.count(less=1))
                    dve.tensor_tensor_reduce(out=sq[:, :], in0=x[:, slot, t.c % 4, :], in1=x[:, slot, t.c % 4, :], scale=1.0 / D, scalar=0.0,
                                             op0=ALU.mult, op1=ALU.add, accum_out=ms[:, s4, :]).then_inc(squares, 1)
                t = i + 3
                if t.exists():
                    n, slot, uses = four(t)
                    s4 = t.slot(4)
                    dve.wait_ge(rr_ready, t.count())
                    if t.after(2):
                        dve.wait_ge(xt_ready, t.count(less=2))
                    dve.tensor_scalar(xs[:, t.slot(2), :], x[:, slot, t.c % 4, :], rr[:, s4, :], None, ALU.mult).then_inc(xs_ready, 1)
                t = i + 4
                if t.exists():
                    s4 = t.slot(4)
                    dve.wait_ge(squares, t.count())
                    if t.after(4):
                        dve.wait_ge(rr_ready, t.count(less=4))
                    dve.tensor_scalar(mse[:, s4, :], ms[:, s4, :], RMS_EPS, None, ALU.add).then_inc(mse_ready, 1)
                t = i + 1
                if t.exists():
                    dve.wait_ge(proj_ready, t.count())
                    if t.after(2):
                        dve.wait_ge(e_ready, t.count(less=2))
                    dve.tensor_scalar(low[:, t.slot(2), :], p_ps[:, 0:2 * F], 0.0, None, ALU.min).then_inc(low_ready, 1)
                t = i + 1
                if t.exists():
                    dve.wait_ge(e_ready, t.count())
                    if t.after(2):
                        dve.wait_ge(k_turned, t.count(less=2))
                        dve.wait_ge(k_kept, t.count(less=2))
                    dve.scalar_tensor_tensor(out=kq[:, t.slot(2), :, :], in0=p_ps[:, 0:2 * F].rearrange("p (a f) -> p a f", a=2), scalar=0.0,
                                             in1=e[:, t.slot(2), :].rearrange("p (a f) -> p a f", a=2), op0=ALU.max, op1=ALU.add).then_inc(kq_ready, 1)
            skewed(dve, step, 4, 1, kind)


def memory_recurrence(nc, stage, k, rows_in, coef, offset):
    with ExitStack() as ctx:
        mk = Maker(nc, ctx, stage)
        sb, sem = mk.sb, mk.sem
        g = sb("g", [P, S, ROW])
        prod = sb("prod", [P, S * S // 4])
        junk = sb("junk", [P, 3, S])
        quad = sb("quad", [P, S])
        common = sb("common", [P, S])
        cv, row, wt, half_gain, gain = (sb(n, [P, S]) for n in ("cv", "row", "wt", "half_gain", "gain"))
        sv_neg2, p_n, p2_n, dd = (sb(n, [P, S]) for n in ("sv_neg2", "p_n", "p2_n", "dd"))
        v = {n: sb(n, [P, 1]) for n in ("off", "off_new", "var", "var_new", "var_eps", "var_eps_new", "r2c", "half", "eps", "pm", "cross2", "u", "r2", "h2", "rho", "rho2_even", "rho2_odd",
                                        "gg", "vm_neg2", "wsv2", "h", "mm", "kv_neg2")}
        v = {n: t[:, :] for n, t in v.items()}
        N_CHUNK = 4
        loaded = [sem(f"rows_loaded{i}") for i in range(N_CHUNK)]
        step_sem, root_asked, root_ready = sem("steps"), sem("root_asked"), sem("root_ready")
        cleared, h2_ready, new_terms, scaled_terms = sem("cleared"), sem("h2_ready"), sem("new_terms"), sem("scaled_terms")
        gained, quad_done = sem("gained"), sem("quad_done")
        rows_v = rows_in.rearrange("(b t) r -> b t r", t=S)
        block = mk.block()

        @block.sync
        def _(sp):
            n = S // N_CHUNK
            for i in range(N_CHUNK):
                sp.dma_start(g[:, i * n:(i + 1) * n, :], rows_v[:, i * n:(i + 1) * n, :]).then_inc(loaded[i], 16)

        @block.gpsimd
        def _(pool):
            for t in range(S):
                pool.wait_ge(root_asked, 2 * t + 1)
                pool.tensor_tensor(coef[:, t:t + 1], v["r2c"], v["half"], ALU.pow).then_inc(root_ready, 1)
                pool.wait_ge(root_asked, 2 * t + 2)
                pool.tensor_tensor(v["rho"], v["var_eps_new"], k["half"][:, 0:1], ALU.pow).then_inc(root_ready, 1)

        @block.scalar
        def _(act):
            act.wait_ge(loaded[0], 16)
            act.wait_ge(loaded[1], 16)
            act.wait_ge(loaded[2], 16)
            act.wait_ge(loaded[3], 16)
            act.wait_ge(cleared, 1)
            for t in range(S):
                rest = S - 1 - t
                act.wait_ge(root_ready, 2 * t + 1)
                act.wait_ge(h2_ready, t + 1)
                if t:
                    act.wait_ge(scaled_terms, 3 * t)
                act.activation(v["var_new"], v["h2"], ACT.Identity, scale=coef[:, t:t + 1], bias=v["var"]).then_inc(new_terms, 1)
                if rest:
                    if t:
                        act.wait_ge(gained, t)
                    act.mul(wt[:, 0:rest], g[:, t + 1:S, KK + t], coef[:, t:t + 1]).then_inc(new_terms, 1)
                    act.wait_ge(root_ready, 2 * t + 2)
                    if t:
                        act.wait_ge(quad_done, t)
                    rho2 = v["rho2_odd" if t % 2 else "rho2_even"]
                    act.mul(rho2, v["rho"], v["rho"]).then_inc(scaled_terms, 1)
                    act.wait_ge(scaled_terms, 3 * t + 1)
                    act.wait_ge(new_terms, 2 * t + 2)
                    act.mul(v["var"], v["var_new"], rho2).then_inc(scaled_terms, 1)
                    act.wait_ge(scaled_terms, 3 * t + 2)
                    act.wait_ge(root_asked, 2 * t + 2)
                    act.activation(v["var_eps"], v["var"], ACT.Identity, bias=v["eps"]).then_inc(scaled_terms, 1)

        @block.vector
        def _(dve):
            done = [0]

            def put(ins):
                done[0] += 1
                ins.then_inc(step_sem, 1)
                return done[0]

            def need(*marks):
                dve.wait_ge(step_sem, max(marks))

            ts, stt, tt, ttr = dve.tensor_scalar, dve.scalar_tensor_tensor, dve.tensor_tensor, dve.tensor_tensor_reduce
            for s in loaded:
                dve.wait_ge(s, 16)
            ksum, pp, sv = (g[:, :, n + S] for n in (KK, PP, VV))
            put(ts(sv_neg2[:, :], sv, -2.0, None, ALU.mult))
            m = put(ts(p_n[:, :], pp, -1.0 / N_MEM, None, ALU.mult))
            put(ts(p2_n[:, :], pp, 2.0 / N_MEM, None, ALU.mult))
            need(m)
            need(put(tt(dd[:, :], p_n[:, :], pp, ALU.mult)))
            diagonal = g[:, :, :].rearrange("p t r -> p (t r)")[:, PP:PP + (S - 1) * (ROW + 1) + 1:ROW + 1]
            need(put(tt(dd[:, :], dd[:, :], diagonal, ALU.add)))
            put(ts(dd[:, :], dd[:, :], 1.0 / N_MEM, None, ALU.mult))
            put(dve.memset(quad[:, :], 0.0))
            put(dve.memset(v["off"], 0.0))
            put(dve.memset(v["half"], 0.5))
            put(dve.memset(v["var_eps"], LN_EPS))
            put(dve.memset(v["eps"], LN_EPS))
            need(put(dve.memset(v["var"], 0.0)))
            dve.memset(junk[:, 0, :], 0.0).then_inc(cleared, 1)
            dve.tensor_scalar(v["r2c"], g[:, 0, VV:VV + 1], 1e-30, None, ALU.max).then_inc(root_asked, 1)
            need(put(dve.memset(v["cross2"], 0.0)))
            for t in range(S):
                col = slice(t, t + 1)
                rest = S - 1 - t
                vv_tt = g[:, t, VV + t:VV + t + 1]
                if t and rest:
                    need(cv_ready)
                    pr = prod[:, 0:rest * t].rearrange("p (a b) -> p a b", b=t)
                    pr_ready = put(tt(pr, g[:, t + 1:S, KK:KK + t], cv[:, 0:t].unsqueeze(1).to_broadcast([P, rest, t]), ALU.mult))
                dve.wait_ge(root_ready, 2 * t + 1)
                c_t = coef[:, col]
                if t:
                    dve.wait_ge(scaled_terms, 3 * t)
                    need(cross_ready)
                stt(out=v["h2"], in0=c_t, scalar=dd[:, col], in1=v["cross2"], op0=ALU.mult, op1=ALU.add).then_inc(h2_ready, 1)
                off_new = put(stt(out=v["off_new"], in0=c_t, scalar=p_n[:, col], in1=v["off"], op0=ALU.mult, op1=ALU.add))
                if rest:
                    nx = t + 1
                    ncol = slice(nx, nx + 1)
                    row_ready = put(tt(row[:, 0:nx], coef[:, 0:nx], g[:, nx, KK:KK + nx], ALU.mult))
                dve.wait_ge(h2_ready, t + 1)
                stt(out=v["var_eps_new"], in0=v["h2"], scalar=c_t, in1=v["var_eps"], op0=ALU.mult, op1=ALU.add).then_inc(root_asked, 1)
                if not rest:
                    break
                need(off_new)
                gg = put(ts(v["gg"], v["off_new"], ksum[:, ncol], None, ALU.mult))
                if t:
                    need(pr_ready)
                    common_ready = put(dve.tensor_reduce(common[:, 0:rest], pr, AX, ALU.add))
                need(row_ready)
                vm = put(ttr(out=junk[:, 1, 0:nx], in0=row[:, 0:nx], in1=g[:, nx, VV:VV + nx], scale=-2.0, scalar=0.0,
                             op0=ALU.mult, op1=ALU.add, accum_out=v["vm_neg2"]))
                dve.wait_ge(new_terms, 2 * t + 2)
                if t:
                    need(common_ready)
                    half = put(stt(out=half_gain[:, 0:rest], in0=wt[:, 0:rest], scalar=vv_tt, in1=common[:, 0:rest],
                                   op0=ALU.mult, op1=ALU.add))
                else:
                    half = put(ts(half_gain[:, 0:rest], wt[:, 0:rest], vv_tt, None, ALU.mult))
                wsv = put(ttr(out=junk[:, 2, 0:nx], in0=row[:, 0:nx], in1=sv[:, 0:nx], scale=2.0, scalar=0.0,
                              op0=ALU.mult, op1=ALU.add, accum_out=v["wsv2"]))
                need(half)
                tt(gain[:, 0:rest], half_gain[:, 0:rest], wt[:, 0:rest], ALU.mult).then_inc(gained, 1)
                need(gg, vm)
                kv = put(stt(out=v["kv_neg2"], in0=v["gg"], scalar=sv_neg2[:, ncol], in1=v["vm_neg2"], op0=ALU.mult, op1=ALU.add))
                dve.wait_ge(root_ready, 2 * t + 2)
                off = put(ts(v["off"], v["off_new"], v["rho"], None, ALU.mult))
                dve.wait_ge(gained, t + 1)
                if t:
                    stt(out=quad[:, nx:S], in0=quad[:, nx:S], scalar=v["rho2_even" if t % 2 else "rho2_odd"], in1=gain[:, 0:rest],
                        op0=ALU.mult, op1=ALU.add).then_inc(quad_done, 1)
                else:
                    dve.tensor_copy(quad[:, nx:S], gain[:, 0:rest]).then_inc(quad_done, 1)
                need(wsv)
                lengths = put(stt(out=v["h"], in0=v["gg"], scalar=float(D), in1=v["wsv2"], op0=ALU.mult, op1=ALU.add))
                scaled = put(ts(coef[:, 0:nx], coef[:, 0:nx], v["rho"], None, ALU.mult))
                need(lengths)
                dve.wait_ge(quad_done, t + 1)
                mm = put(stt(out=v["mm"], in0=v["h"], scalar=v["gg"], in1=quad[:, ncol], op0=ALU.mult, op1=ALU.add))
                need(off)
                pm = put(ts(v["pm"], p2_n[:, ncol], v["off"], None, ALU.mult))
                need(mm, kv)
                u = put(stt(out=v["u"], in0=v["mm"], scalar=v["rho"], in1=v["kv_neg2"], op0=ALU.mult, op1=ALU.add))
                cv_ready = put(stt(out=cv[:, 0:nx], in0=coef[:, 0:nx], scalar=2.0, in1=g[:, nx, VV:VV + nx], op0=ALU.mult, op1=ALU.mult))
                need(u)
                r2 = put(ts(v["r2"], v["u"], v["rho"], g[:, nx, VV + nx:VV + nx + 1], ALU.mult, ALU.add))
                need(pm)
                cross_ready = put(ttr(out=junk[:, 0, 0:nx], in0=coef[:, 0:nx], in1=g[:, nx, PP:PP + nx], scale=2.0 / N_MEM,
                                      scalar=v["pm"], op0=ALU.mult, op1=ALU.add, accum_out=v["cross2"]))
                need(r2)
                ts(v["r2c"], v["r2"], 1e-30, None, ALU.max).then_inc(root_asked, 1)
            dve.wait_ge(root_ready, 2 * S)
            dve.wait_ge(new_terms, 2 * S - 1)
            need(put(ts(coef[:, :], coef[:, :], v["rho"], None, ALU.mult)))
            put(ts(offset, v["off_new"], v["rho"], None, ALU.mult))


def memory_and_mixer(nc, stage, k, x_in, ctx_in, k_all, v_all, qt_all, eta_col, w_out_t, coef, offset, x_out):
    with ExitStack() as ctx:
        mk = Maker(nc, ctx, stage)
        sb, ps, sem = mk.sb, mk.ps, mk.sem
        coef_t = sb("coef_t", [P, 2, NT])
        mine = sb("mine", [P, 2, NT])
        off_in = sb("off_in", [P, 2, NT])
        ones64 = sb("ones64", [P, F])
        off = sb("off", [P, NT])
        kc_bd = sb("kc_bd", [P, 2, 2, F])
        x = sb("x", [P, 2, 4, D])
        c = sb("c", [P, 2, 4, D])
        mem = sb("mem", [P, 2, D])
        read = sb("read", [P, 2, P])
        xm = sb("xm", [P, 4, D])
        xct = sb("xct", [P, 2, 2, P])
        g_bd = sb("g_bd", [P, 2, 2, S])
        r = [sb(f"r{n}", [P, 2, D]) for n in range(2)]
        stats = [sb(f"stats{n}", [P, 6]) for n in range(2)]
        mv = [sb(f"mv{n}", [P, 2, 2]) for n in range(2)]
        ve = [sb(f"ve{n}", [P, 2, 1]) for n in range(2)]
        rstd = [sb(f"rstd{n}", [P, 2, 1]) for n in range(2)]
        y = sb("y", [P, 2, 4, D])
        m_ps, read_ps, out_ps, turn_ps, h_ps, mix_ps = (ps(n, [P, 512]) for n in ("m", "read", "out", "turn", "h", "mix"))
        (zeroed, mine_set, off_set, setup_ps, setup_copied, kc_ready, m_ready, m_copied, read_ready, read_copied, out_ready, turned, turn_copied,
         h_ready, g_ready, mix_ready) = (
            sem(n) for n in ("zeroed", "mine_set", "off_set", "setup_ps", "setup_copied", "kc_ready", "m_ready", "m_copied", "read_ready", "read_copied",
                             "out_ready", "turned", "turn_copied", "h_ready", "g_ready", "mix_ready"))
        summed, stats_ready, mean_ready, var_ready, rstd_ready, normed = (
            [sem(f"{n}{j}") for j in range(2)] for n in ("summed", "stats_ready", "mean_ready", "var_ready", "rstd_ready", "normed"))
        passed_dve, passed_pe, passed_pool = sem("passed_dve"), sem("passed_pe"), sem("passed_pool")
        x_loaded = [sem(f"x_loaded{i}") for i in range(2)]
        c_loaded = [sem(f"c_loaded{i}") for i in range(2)]
        stored = [sem(f"stored{i}") for i in range(2)]
        x_v, c_v, out_v = (t.rearrange("(g n p) d -> g p n d", p=P, n=4) for t in (x_in, ctx_in, x_out))
        block = mk.block()

        @block.sync
        def _(sp):
            def step(i):
                t = i + -1
                if t.exists() and t.c % 4 == 3:
                    n, slot, uses = four(t)
                    sp.wait_ge(normed[1], t.count())
                    sp.dma_start(out_v[n], y[:, slot, :, :]).then_inc(stored[slot], 16)
                t = i + 8
                if t.exists() and t.c % 4 == 0:
                    n, slot, uses = four(t)
                    if t.after(8):
                        sp.wait_ge(summed[0], t.count(less=5))
                    sp.dma_start(x[:, slot, :, :], x_v[n]).then_inc(x_loaded[slot], 16)
                t = i + 4
                if t.exists() and t.c % 4 == 0:
                    n, slot, uses = four(t)
                    if t.after(8):
                        sp.wait_ge(mix_ready, t.count(less=5))
                    sp.dma_start(c[:, slot, :, :], c_v[n]).then_inc(c_loaded[slot], 16)
            skewed(sp, step, 8, 1, Eights)
            for n in range(2):
                sp.wait_ge(stored[n], 16 * NT // 8)

        @block.gpsimd
        def _(pool):
            pool.memset(mine[:, :, :], 0.0).then_inc(mine_set, 1)
            pool.wait_ge(mine_set, 1)
            pool.affine_select(out=mine[:, :, :], in_=mine[:, :, :], compare_op=ALU.not_equal, fill=1.0, base=0,
                               pattern=[[-1, 2], [-2, NT]], channel_multiplier=1).then_inc(mine_set, 1)

            pool.wait_ge(setup_copied, 2)

            def step(i):
                t = i + 6
                if t.exists():
                    s2 = t.slot(2)
                    if t.after(2):
                        pool.wait_ge(m_ready, t.count(less=2))
                    settle(pool, passed_pool)
                    pool.tensor_tensor(kc_bd[:, s2, :, :], k_all[:, bass.ds(t.n, 1), :].to_broadcast([P, 2, F]),
                                       coef_t[:, :, bass.ds(t.n, 1)].to_broadcast([P, 2, F]), ALU.mult).then_inc(kc_ready, 1)
                for n, t in ((0, i + 3), (1, i)):
                    if t.exists():
                        s2 = t.slot(2)
                        pool.wait_ge(var_ready[n], t.count())
                        if t.after(2):
                            pool.wait_ge(normed[n], t.count(less=2))
                        pool.tensor_tensor(rstd[n][:, s2, :], ve[n][:, s2, :], k["half"][:, 0:1], ALU.pow).then_inc(rstd_ready[n], 1)
            skewed(pool, step, 6, 1, Eights)

        @block.tensor
        def _(pe):
            pe.wait_ge(zeroed, 3)
            pe.wait_ge(off_set, 1)
            pe.wait_ge(mine_set, 2)
            for b in range(2):
                nc.tensor.matmul(m_ps[b * S:(b + 1) * S, 0:NT], coef[:, :], mine[:, b, :], start=True, stop=True)
            for b in range(2):
                mm = nc.tensor.matmul(h_ps[b * S:(b + 1) * S, 0:NT], ones64[:, :], off_in[:, b, :], start=True, stop=True)
            mm.then_inc(setup_ps, 1)
            pe.wait_ge(setup_copied, 2)

            def step(i):
                t = i + 3
                if t.exists():
                    pe.wait_ge(read_copied, t.count())
                    if t.after(1):
                        pe.wait_ge(summed[0], t.count(less=1))
                    nc.tensor.matmul(out_ps[:, 0:D], read[:, t.slot(2), :], w_out_t, start=True, stop=True).then_inc(out_ready, 1)
                t = i + 1
                if t.exists():
                    pe.wait_ge(turn_copied, t.count())
                    if t.after(1):
                        pe.wait_ge(g_ready, t.count(less=1))
                    nc.tensor.matmul(h_ps[:, 0:P], xct[:, t.slot(2), 1, :], xct[:, t.slot(2), 0, :], start=True, stop=True).then_inc(h_ready, 1)
                t = i + 5
                if t.exists():
                    s2 = t.slot(2)
                    pe.wait_ge(kc_ready, t.count())
                    if t.after(1):
                        pe.wait_ge(m_copied, t.count(less=1))
                    settle(pe, passed_pe)
                    nc.tensor.matmul(m_ps[:, 0:D], kc_bd[:, s2, :, :], v_all[:, bass.ds(t.n, 1), :], start=True, stop=True).then_inc(m_ready, 1)
                t = i
                if t.exists():
                    n, slot, uses = four(t)
                    pe.wait_ge(g_ready, t.count())
                    if t.after(1):
                        pe.wait_ge(summed[1], t.count(less=1))
                    nc.tensor.matmul(mix_ps[:, 0:D], g_bd[:, t.slot(2), :, :], c[:, slot, t.c % 4, :], start=True, stop=True).then_inc(mix_ready, 1)
                t = i + 4
                if t.exists():
                    pe.wait_ge(m_copied, t.count())
                    if t.after(1):
                        pe.wait_ge(read_copied, t.count(less=1))
                    settle(pe, passed_pe)
                    nc.tensor.matmul(read_ps[:, 0:P], mem[:, t.slot(2), :], qt_all[:, bass.ds(t.n, 1), :], start=True, stop=True)\
                        .then_inc(read_ready, 1)
                t = i + 2
                if t.exists():
                    n, slot, uses = four(t)
                    if t.c % 4 == 0:
                        pe.wait_ge(c_loaded[slot], uses * 16)
                    pe.wait_ge(normed[0], t.count())
                    if t.after(1):
                        pe.wait_ge(turn_copied, t.count(less=1))
                    nc.tensor.transpose(turn_ps[:, P:2 * P], c[:, slot, t.c % 4, :], k["ident"][:, :])
                    nc.tensor.transpose(turn_ps[:, 0:P], xm[:, t.slot(4), :], k["ident"][:, :]).then_inc(turned, 1)
            skewed(pe, step, 6, 0, Eights)

        @block.scalar
        def _(act):
            act.wait_ge(setup_ps, 1)
            act.wait_ge(zeroed, 3)
            for b in range(2):
                rows = slice(b * S, (b + 1) * S)
                cp = act.copy(coef_t[rows, b, :], m_ps[rows, 0:NT])
            cp.then_inc(setup_copied, 1)
            act.copy(off[:, :], h_ps[:, 0:NT]).then_inc(setup_copied, 1)
            act.wait_ge(setup_copied, 2)

            def step(i):
                t = i + 1
                if t.exists():
                    act.wait_ge(h_ready, t.count())
                    if t.after(2):
                        act.wait_ge(mix_ready, t.count(less=2))
                    for b in range(2):
                        rows = slice(b * S, (b + 1) * S)
                        ge = act.activation(g_bd[rows, t.slot(2), b, :], h_ps[rows, rows], ACT.Gelu_apprx_tanh)
                    ge.then_inc(g_ready, 1)
                t = i + 5
                if t.exists():
                    act.wait_ge(m_ready, t.count())
                    if t.after(2):
                        act.wait_ge(read_ready, t.count(less=2))
                    act.activation(mem[:, t.slot(2), :], m_ps[:, 0:D], ACT.Identity, scale=eta_col,
                                   bias=off[:, bass.ds(t.n, 1)]).then_inc(m_copied, 1)
                t = i + 4
                if t.exists():
                    act.wait_ge(read_ready, t.count())
                    if t.after(2):
                        act.wait_ge(out_ready, t.count(less=2))
                    act.copy(read[:, t.slot(2), :], read_ps[:, 0:P]).then_inc(read_copied, 1)
                t = i + 2
                if t.exists():
                    act.wait_ge(turned, t.count())
                    if t.after(2):
                        act.wait_ge(h_ready, t.count(less=2))
                    act.copy(xct[:, t.slot(2), :, :], turn_ps[:, 0:2 * P].rearrange("p (a n) -> p a n", a=2)).then_inc(turn_copied, 1)
            skewed(act, step, 6, 0, Eights)

        @block.vector
        def _(dve):
            dve.memset(coef_t[:, :, :], 0.0).then_inc(zeroed, 1)
            dve.memset(g_bd[:, :, :, :], 0.0).then_inc(zeroed, 1)
            dve.memset(ones64[:, :], 1.0).then_inc(zeroed, 1)
            dve.wait_ge(mine_set, 2)
            dve.tensor_scalar(off_in[:, :, :], mine[:, :, :], offset, None, ALU.mult).then_inc(off_set, 1)
            dve.wait_ge(setup_copied, 2)

            def add(n, t, res, src):
                s2 = t.slot(2)
                if t.after(2):
                    dve.wait_ge(normed[n], t.count(less=2))
                dve.scalar_tensor_tensor(out=r[n][:, s2, :], in0=res, scalar=2.0 if n == 0 else 1.0, in1=src, op0=ALU.mult, op1=ALU.add)\
                    .then_inc(summed[n], 1)

            def statistics(n, t, part):
                s2 = t.slot(2)
                if part == 0:
                    dve.wait_ge(summed[n], t.count())
                    if t.after(1):
                        dve.wait_ge(mean_ready[n], t.count(less=1))
                    dve.bn_stats(stats[n][:, :], r[n][:, s2, :]).then_inc(stats_ready[n], 1)
                if part == 1:
                    dve.wait_ge(stats_ready[n], t.count())
                    settle(dve, passed_dve)
                    dve.bn_aggr(mv[n][:, s2, :], stats[n][:, :]).then_inc(mean_ready[n], 1)
                if part == 2:
                    dve.wait_ge(mean_ready[n], t.count())
                    if t.after(2):
                        dve.wait_ge(rstd_ready[n], t.count(less=2))
                    dve.tensor_scalar(ve[n][:, s2, :], mv[n][:, s2, 1:2], LN_EPS, None, ALU.add).then_inc(var_ready[n], 1)

            def norm(n, t, dst):
                s2 = t.slot(2)
                dve.wait_ge(rstd_ready[n], t.count())
                dve.tensor_scalar(dst, r[n][:, s2, :], mv[n][:, s2, 0:1], rstd[n][:, s2, :], ALU.subtract, ALU.mult)\
                    .then_inc(normed[n], 1)

            def step(i):
                first, second = i + 3, i
                if first.exists():
                    dve.wait_ge(out_ready, first.count())
                    n, slot, uses = four(first)
                    dve.wait_ge(x_loaded[slot], uses * 16)
                    add(0, first, x[:, slot, first.c % 4, :], out_ps[:, 0:D])
                t = i + 2
                if t.exists():
                    if t.after(4):
                        dve.wait_ge(summed[1], t.count(less=4))
                    norm(0, t, xm[:, t.slot(4), :])
                t = i + -1
                if t.exists():
                    n, slot, uses = four(t)
                    if t.c % 4 == 0 and t.after(8):
                        dve.wait_ge(stored[slot], (uses - 1) * 16)
                    norm(1, t, y[:, slot, t.c % 4, :])
                if second.exists():
                    dve.wait_ge(mix_ready, second.count())
                    add(1, second, xm[:, second.slot(4), :], mix_ps[:, 0:D])
                for part in range(3):
                    for n, t in enumerate((first, second)):
                        if t.exists():
                            statistics(n, t, part)
            skewed(dve, step, 6, 1, Eights)


def build(nc, a, out):
    flat = lambda t: t.rearrange("b s d -> (b s) d")
    x1 = nc.dram_tensor("x1", (B * S, D), F32, kind="Internal").ap()
    x2 = nc.dram_tensor("x2", (B * S, D), F32, kind="Internal").ap()
    with ExitStack() as ctx:
        k = constants(nc, Maker(nc, ctx, "k"))
        xs = [nc.dram_tensor(f"tokens_by_expert{h}", (Sorted2.ALL // 2 * P, D), F32, kind="Internal").ap() for h in range(2)]
        ys = nc.dram_tensor("expert_outputs", (Sorted2.ALL * P, D), F32, kind="Internal").ap()
        mk = Maker(nc, ctx, "experts")
        pool_dmas = [mk.sem("scattered"), mk.sem("gathered_early"), [mk.sem("gathered0"), mk.sem("gathered1")]]
        fill = zeros_for(nc, Maker(nc, ctx, "fill"), xs)
        wqkv, bqkv = a["L0_attn_W_qkv"], a["L0_attn_b_qkv"]
        w = {"wo": a["L0_attn_W_o"], "bo": a["L0_attn_b_o"]}
        for n, name in enumerate("qkv"):
            w["w" + name], w["b" + name] = wqkv[n * D:(n + 1) * D, :], bqkv[n * D:(n + 1) * D]
        attention(nc, "self", k, flat(a["x"]), None, None, w, x1, fill)
        w = {m + name: a[f"L0_xattn_{m.upper() if m == 'w' else m}{name}"] for m in "wb" for name in "qkvo"}
        mask = a["mask_Bx1x1xS2_if1"].rearrange("b u v s -> (b u v) s")
        attention(nc, "cross", k, x1, flat(a["ctx_1024"]), mask, w, x2)
        ffn = {n: a["L0_ffn_" + n] for n in ("Wg", "W1", "W2", "W3")}
        experts(nc, "ffn0", k, x2, ffn, x1, True, xs, ys, fill["filled"], pool_dmas)
        mem = {n: a["L1_attn_" + n] for n in ("norm_weight", "Wk", "Wv", "Wq", "eta", "Wout")}
        rows = nc.dram_tensor("memory_rows", (B * S, ROW), F32, kind="Internal").ap()
        with ExitStack() as mem_ctx:
            mm = Maker(nc, mem_ctx, "mem_state")
            w_out_t, coef, offset, eta = mm.sb("w_out_t", [P, D]), mm.sb("coef", [P, S]), mm.sb("offset", [P, 1]), mm.sb("eta", [P, 1])
            k_all, v_all, qt_all = mm.sb("k_all", [P, NT, F]), mm.sb("v_all", [P, NT, D]), mm.sb("qt_all", [P, NT, P])
            memory_products(nc, "products", k, x1, mem, rows, k_all, v_all, qt_all, eta[:, :], w_out_t[:, :])
            memory_recurrence(nc, "recur", k, rows, coef, offset[:, :])
            memory_and_mixer(nc, "mixer", k, x1, flat(a["ctx_1024"]), k_all, v_all, qt_all, eta[:, :], w_out_t[:, :], coef, offset[:, :], x2)
        ffn = {n: a["L1_ffn_" + n] for n in ("Wr", "br", "W1", "b1", "W2", "b2")}
        experts(nc, "ffn1", k, x2, ffn, flat(out), False, xs, ys, fill["filled"], pool_dmas)


INPUTS = ["x", "ctx_1024", "mask_Bx1x1xS2_if1",
          "L0_attn_W_qkv", "L0_attn_b_qkv", "L0_attn_W_o", "L0_attn_b_o",
          "L0_xattn_Wq", "L0_xattn_bq", "L0_xattn_Wk", "L0_xattn_bk", "L0_xattn_Wv", "L0_xattn_bv",
          "L0_xattn_Wo", "L0_xattn_bo",
          "L0_ffn_Wg", "L0_ffn_W1", "L0_ffn_W2", "L0_ffn_W3",
          "L1_attn_norm_weight", "L1_attn_Wk", "L1_attn_Wv", "L1_attn_Wq", "L1_attn_eta", "L1_attn_Wout",
          "L1_ffn_Wr", "L1_ffn_br", "L1_ffn_W1", "L1_ffn_b1", "L1_ffn_W2", "L1_ffn_b2"]


def kernel(**inputs):
    import numpy as _np
    import concourse.bacc as _bacc
    from concourse.bass_utils import run_bass_kernel_spmd as _run

    nc = _bacc.Bacc("TRN2", target_bir_lowering=False, num_devices=1)
    arrays, aps = {}, {}
    for name in INPUTS:
        v = _np.ascontiguousarray(inputs[name])
        arrays[f"in_{name}"] = v
        aps[name] = nc.dram_tensor(f"in_{name}", v.shape, mybir.dt.from_np(v.dtype), kind="ExternalInput").ap()
    out = nc.dram_tensor("decoded", (B, S, D), F32, kind="ExternalOutput").ap()
    build(nc, aps, out)
    r = _run(nc, [arrays], core_ids=[0])
    return r.results[0]["decoded"]
```
